# Optimizing a Trainium2 kernel written in Bass

```python
import numpy as np
import jax
import jax.numpy as jnp

def _softmax(x, axis=-1):
    return jax.nn.softmax(x, axis=axis)

def _gelu(x):
    return jax.nn.gelu(x, approximate=True)

def _silu(x):
    return jax.nn.silu(x)

def _sigmoid(x):
    return jax.nn.sigmoid(x)

def _layernorm(x, axis=-1, eps=1e-05):
    m = jnp.mean(x, axis=axis, keepdims=True)
    v = jnp.var(x, axis=axis, keepdims=True)
    return (x - m) / jnp.sqrt(v + eps)

def _scatter_add(tgt, idx, src, axis=0):
    return tgt.at[idx].add(src)

def _segment_sum(src, seg, n):
    return jax.ops.segment_sum(src, seg, n)
kernel_name = 'mk_seq_preln_d1_jaxref_r8_657a26'

def setup_inputs(seed: int=0):
    np.random.seed(seed)
    _w = jnp.asarray

    def _L0_attn_setup():
        import jax, jax.numpy as jnp
        import numpy as np
        import math
        D = 128
        H = 16
        DH = D // H
        K = 64
        W = 64
        IDX = 64
        B, S = (1, 256)
        key = jax.random.key(seed)
        ks = jax.random.split(key, 16)
        sD = 1.0 / math.sqrt(D)
        x = jax.random.normal(ks[0], (B, S, D), jnp.float32)
        mk = lambda i, shp: jax.random.normal(ks[i], shp, jnp.float32) * sD
        return {'x': x, 'wq': mk(1, (D, D)), 'bq': mk(2, (D,)), 'wk': mk(3, (D, D)), 'bk': mk(4, (D,)), 'wv': mk(5, (D, D)), 'bv': mk(6, (D,)), 'wo': mk(7, (D, D)), 'bo': mk(8, (D,)), 'wqi': mk(9, (IDX, D)), 'bqi': mk(10, (IDX,)), 'wki': mk(11, (IDX, D)), 'bki': mk(12, (IDX,))}
    _L0_attn_in = _L0_attn_setup()

    def _L0_ffn_setup():
        import jax, jax.numpy as jnp
        import numpy as np
        B, N, D, H, E = (4, 128, 128, 16, 8)
        DK = D // H
        HID = 4 * D
        EPS = 1e-05

        def _layernorm(x, w, b):
            m = jnp.mean(x, axis=-1, keepdims=True)
            v = jnp.mean(jnp.square(x - m), axis=-1, keepdims=True)
            return (x - m) * jax.lax.rsqrt(v + EPS) * w + b

        def _msa(x, w_qkv, w_proj):
            b, n, d = x.shape
            qkv = (x @ w_qkv).reshape(b, n, 3, H, DK)
            q = qkv[:, :, 0].transpose(0, 2, 1, 3)
            k = qkv[:, :, 1].transpose(0, 2, 1, 3)
            v = qkv[:, :, 2].transpose(0, 2, 1, 3)
            attn = jnp.einsum('bhnd,bhmd->bhnm', q, k) * (1.0 / np.sqrt(DK))
            attn = jax.nn.softmax(attn, axis=-1)
            y = jnp.einsum('bhnm,bhmd->bhnd', attn, v)
            y = y.transpose(0, 2, 1, 3).reshape(b, n, d)
            return y @ w_proj

        def _moe_mlp(x, gate_w, gate_b, w1, w2):
            b, n, d = x.shape
            xf = x.reshape(b * n, d)
            logits = xf @ gate_w + gate_b
            one_hot = jax.nn.one_hot(jnp.argmax(logits, axis=-1), E, dtype=xf.dtype)
            h = jax.nn.gelu(jnp.einsum('td,edh->teh', xf, w1), approximate=True)
            y = jnp.einsum('teh,ehd->ted', h, w2)
            out = jnp.einsum('te,ted->td', one_hot, y)
            return out.reshape(b, n, d)
        key = jax.random.key(seed)
        ks = jax.random.split(key, 8)
        s = 0.02
        return {'x': jax.random.normal(ks[0], (B, N, D), jnp.float32), 'ln1_w': jnp.ones((D,), jnp.float32), 'ln1_b': jnp.zeros((D,), jnp.float32), 'w_qkv': jax.random.normal(ks[1], (D, 3 * D), jnp.float32) * s, 'w_proj': jax.random.normal(ks[2], (D, D), jnp.float32) * s, 'ln2_w': jnp.ones((D,), jnp.float32), 'ln2_b': jnp.zeros((D,), jnp.float32), 'gate_w': jax.random.normal(ks[3], (D, E), jnp.float32) * s, 'gate_b': jnp.zeros((E,), jnp.float32), 'w1': jax.random.normal(ks[4], (E, D, HID), jnp.float32) * s, 'w2': jax.random.normal(ks[5], (E, HID, D), jnp.float32) * s}
    _L0_ffn_in = _L0_ffn_setup()
    _d = {'L0_attn_x': _L0_attn_in['x'], 'L0_attn_wq': _L0_attn_in['wq'], 'L0_attn_bq': _L0_attn_in['bq'], 'L0_attn_wk': _L0_attn_in['wk'], 'L0_attn_bk': _L0_attn_in['bk'], 'L0_attn_wv': _L0_attn_in['wv'], 'L0_attn_bv': _L0_attn_in['bv'], 'L0_attn_wo': _L0_attn_in['wo'], 'L0_attn_bo': _L0_attn_in['bo'], 'L0_attn_wqi': _L0_attn_in['wqi'], 'L0_attn_bqi': _L0_attn_in['bqi'], 'L0_attn_wki': _L0_attn_in['wki'], 'L0_attn_bki': _L0_attn_in['bki'], 'L0_ffn_ln1_w': _L0_ffn_in['ln1_w'], 'L0_ffn_ln1_b': _L0_ffn_in['ln1_b'], 'L0_ffn_w_qkv': _L0_ffn_in['w_qkv'], 'L0_ffn_w_proj': _L0_ffn_in['w_proj'], 'L0_ffn_ln2_w': _L0_ffn_in['ln2_w'], 'L0_ffn_ln2_b': _L0_ffn_in['ln2_b'], 'L0_ffn_gate_w': _L0_ffn_in['gate_w'], 'L0_ffn_gate_b': _L0_ffn_in['gate_b'], 'L0_ffn_w1': _L0_ffn_in['w1'], 'L0_ffn_w2': _L0_ffn_in['w2']}
    _x0 = _d['L0_attn_x']
    _d['L0_attn_x'] = jax.random.normal(jax.random.fold_in(jax.random.key(seed), 1), (1, 2048, 128), dtype=_x0.dtype)
    del _x0
    return _d

def reference(L0_attn_x, L0_attn_wq, L0_attn_bq, L0_attn_wk, L0_attn_bk, L0_attn_wv, L0_attn_bv, L0_attn_wo, L0_attn_bo, L0_attn_wqi, L0_attn_bqi, L0_attn_wki, L0_attn_bki, L0_ffn_ln1_w, L0_ffn_ln1_b, L0_ffn_w_qkv, L0_ffn_w_proj, L0_ffn_ln2_w, L0_ffn_ln2_b, L0_ffn_gate_w, L0_ffn_gate_b, L0_ffn_w1, L0_ffn_w2):

    def _L0_attn_ref(x, wq, bq, wk, bk, wv, bv, wo, bo, wqi, bqi, wki, bki):
        import jax, jax.numpy as jnp
        import numpy as np
        import math
        D = 128
        H = 16
        DH = D // H
        K = 64
        W = 64
        IDX = 64
        B, S = (1, 256)
        Bx, Sx, _ = x.shape
        scale = 1.0 / math.sqrt(DH)

        def proj(w, b):
            return (x @ w.T + b).reshape(Bx, Sx, H, DH).transpose(0, 2, 1, 3)
        q, k, v = (proj(wq, bq), proj(wk, bk), proj(wv, bv))
        A = Sx - W
        k_work, v_work = (k[:, :, A:], v[:, :, A:])
        k_assoc, v_assoc = (k[:, :, :A], v[:, :, :A])
        scores_work = jnp.einsum('bhsd,bhwd->bhsw', q, k_work) * scale
        q_idx = x @ wqi.T + bqi
        k_idx = x[:, :A] @ wki.T + bki
        idx_scores = jax.nn.relu(jnp.einsum('bse,bae->bsa', q_idx, k_idx))
        kk = min(K, A)
        _, top_idx = jax.lax.top_k(idx_scores, kk)
        gather = jax.vmap(lambda kv, ix: kv[:, ix])
        k_g = gather(k_assoc, top_idx)
        v_g = gather(v_assoc, top_idx)
        scores_assoc = jnp.einsum('bhsd,bhskd->bhsk', q, k_g) * scale
        wmask = jnp.arange(W)[None, :] - jnp.arange(Sx)[:, None] >= 1 + A
        scores_work = jnp.where(wmask[None, None], -jnp.inf, scores_work)
        weights = jax.nn.softmax(jnp.concatenate([scores_assoc, scores_work], axis=-1), axis=-1)
        out = jnp.einsum('bhsk,bhskd->bhsd', weights[..., :kk], v_g) + jnp.einsum('bhsw,bhwd->bhsd', weights[..., kk:], v_work)
        out = out.transpose(0, 2, 1, 3).reshape(Bx, Sx, D)
        return out @ wo.T + bo

    def _L0_ffn_ref(x, ln1_w, ln1_b, w_qkv, w_proj, ln2_w, ln2_b, gate_w, gate_b, w1, w2):
        import jax, jax.numpy as jnp
        import numpy as np
        B, N, D, H, E = (4, 128, 128, 16, 8)
        DK = D // H
        HID = 4 * D
        EPS = 1e-05

        def _layernorm(x, w, b):
            m = jnp.mean(x, axis=-1, keepdims=True)
            v = jnp.mean(jnp.square(x - m), axis=-1, keepdims=True)
            return (x - m) * jax.lax.rsqrt(v + EPS) * w + b

        def _msa(x, w_qkv, w_proj):
            b, n, d = x.shape
            qkv = (x @ w_qkv).reshape(b, n, 3, H, DK)
            q = qkv[:, :, 0].transpose(0, 2, 1, 3)
            k = qkv[:, :, 1].transpose(0, 2, 1, 3)
            v = qkv[:, :, 2].transpose(0, 2, 1, 3)
            attn = jnp.einsum('bhnd,bhmd->bhnm', q, k) * (1.0 / np.sqrt(DK))
            attn = jax.nn.softmax(attn, axis=-1)
            y = jnp.einsum('bhnm,bhmd->bhnd', attn, v)
            y = y.transpose(0, 2, 1, 3).reshape(b, n, d)
            return y @ w_proj

        def _moe_mlp(x, gate_w, gate_b, w1, w2):
            b, n, d = x.shape
            xf = x.reshape(b * n, d)
            logits = xf @ gate_w + gate_b
            one_hot = jax.nn.one_hot(jnp.argmax(logits, axis=-1), E, dtype=xf.dtype)
            h = jax.nn.gelu(jnp.einsum('td,edh->teh', xf, w1), approximate=True)
            y = jnp.einsum('teh,ehd->ted', h, w2)
            out = jnp.einsum('te,ted->td', one_hot, y)
            return out.reshape(b, n, d)
        x = x + _msa(_layernorm(x, ln1_w, ln1_b), w_qkv, w_proj)
        x = x + _moe_mlp(_layernorm(x, ln2_w, ln2_b), gate_w, gate_b, w1, w2)
        return x
    x = L0_attn_x
    x = x + _L0_attn_ref(_layernorm(x, axis=-1), L0_attn_wq, L0_attn_bq, L0_attn_wk, L0_attn_bk, L0_attn_wv, L0_attn_bv, L0_attn_wo, L0_attn_bo, L0_attn_wqi, L0_attn_bqi, L0_attn_wki, L0_attn_bki)
    x = x + _L0_ffn_ref(_layernorm(x, axis=-1), L0_ffn_ln1_w, L0_ffn_ln1_b, L0_ffn_w_qkv, L0_ffn_w_proj, L0_ffn_ln2_w, L0_ffn_ln2_b, L0_ffn_gate_w, L0_ffn_gate_b, L0_ffn_w1, L0_ffn_w2)
    return x

_drawn_inputs = setup_inputs


def setup_inputs(seed=0):
    import zlib

    import numpy as np

    out = dict(_drawn_inputs(seed))
    spreads = {'L0_ffn_ln1_w': (1.0, 0.6),
     'L0_ffn_ln1_b': (0.0, 0.8),
     'L0_ffn_ln2_w': (1.0, 0.6),
     'L0_ffn_ln2_b': (0.0, 2.0),
     'L0_ffn_gate_b': (0.0, 1.416)}
    factors = {'L0_attn_bq': 4.041,
     'L0_attn_bk': 64.0,
     'L0_attn_bki': 35.622,
     'L0_ffn_w_qkv': 8.0,
     'L0_ffn_w_proj': 8.0,
     'L0_ffn_gate_w': 3.507,
     'L0_ffn_w1': 2.913,
     'L0_ffn_w2': 2.9}
    for name, (base, spread) in spreads.items():
        noise = np.random.default_rng([zlib.crc32(name.encode()), seed]).standard_normal(out[name].shape)
        drawn = base * np.exp(spread * noise) if base else spread * noise
        out[name] = jnp.asarray(drawn.astype(out[name].dtype))
    for name, factor in factors.items():
        out[name] = (out[name] * factor).astype(out[name].dtype)
    return out
```

```python
from contextlib import ExitStack

import concourse.bass as bass
from concourse import mybir

F32 = mybir.dt.float32
BF16 = mybir.dt.bfloat16
I32 = mybir.dt.int32
ALU = mybir.AluOpType
ACT = mybir.ActivationFunctionType
AX_X = mybir.AxisListType.X

P = 128
S = 2048
D = 128
H = 16
DH = D // H
WORK = 64
ASSOC = S - WORK
TOPK = 64
IDX = 64
E = 8
HID = 4 * D
EPS = 1e-5
SCALE = float(DH) ** -0.5

QG = 512
GROUPS = S // QG
TPG = QG // P
TILES = S // P
PASSES = 2
PAIRS = H // 2
PPP = PAIRS // PASSES
STEPS = TILES * PPP
GSTEPS = PASSES * STEPS
SLOTS = 6
KQ = SLOTS * DH
KROWS = KQ + 3
VW = DH + 1
Q_PART = (0, 0, 0, 1, 1, 2)
K_PART = (0, 1, 2, 0, 1, 0)

BIG = 3.3895313892515355e38
TAKEN = -3.0e38
TIE = 2.0 ** -100

SHIFT = (0.0, 48.0)
LIMIT = (72.0, 116.0)

XROUND = 8
TOPK_OPS = 4 + 2 * XROUND + 1


def topk_step(k):
    return 24 + (k * 6) // 5


def build(nc, in_, out):
    ctx = ExitStack()
    with ctx:
        def sb(name, shape, dt):
            return ctx.enter_context(nc.sbuf_tensor(name, shape, dt))

        def ps(name, shape, dt):
            return ctx.enter_context(nc.psum_tensor(name, shape, dt))

        def sem(name):
            return ctx.enter_context(nc.semaphore(name))

        x = sb("x", [P, TILES, D], F32)
        xT = sb("xT", [P, S], F32)
        Qs = sb("Qs", [P, 3, S], BF16)
        Ks = sb("Ks", [P, 3, S], BF16)
        KA = sb("KA", [P, PAIRS, S], BF16)
        QA = sb("QA", [P, PAIRS, QG], BF16)
        VA = sb("VA", [P, TILES, H, VW], F32)
        Pb = sb("Pb", [P, 4, 2 * QG], F32)
        MT = sb("MT", [P, 2, TILES, QG], BF16)
        Mq = sb("Mq", [P, 2, S], BF16)
        sw = sb("sw", [P, ASSOC], F32)
        tie = sb("tie", [P, S], F32)
        kiT = sb("kiT", [IDX, S], F32)
        qiT = sb("qiT", [IDX, S], F32)
        OT = sb("OT", [P, PASSES, 2, QG], F32)
        msc = OT[0:H, 0, :, :]
        att = sb("att", [P, TPG, D], F32)
        attT = sb("attT", [P, QG], F32)
        Ms = sb("Ms", [H, 3, QG], BF16)
        mx = sb("mx", [P, TILES, H], F32)
        ngm = sb("ngm", [P, TILES, H], F32)
        nq = sb("nq", [P, TILES, H], F32)
        ok = sb("ok", [P, TILES, H], F32)
        mv = sb("mv", [P, TILES, 2], F32)
        st = sb("st", [P, TILES, 6], F32)
        ve = sb("ve", [P, TILES], F32)
        rs = sb("rs", [P, TILES], F32)
        rt = sb("rt", [P, TILES], F32)
        mhalf = sb("mhalf", [P, TILES], F32)
        top8 = sb("top8", [P, 8], F32)
        rec = sb("rec", [P, 2, H], F32)
        kn = sb("kn", [H, GROUPS], F32)
        kd = sb("kd", [H, 2 + H], F32)
        fl = sb("fl", [P, 4], F32)
        fli = sb("fli", [1, 2], I32)
        ident = sb("ident", [P, P], F32)
        identb = sb("identb", [P, P], BF16)
        ones = sb("ones", [H, P], F32)
        hmask = sb("hmask", [P, H], F32)
        w_q = sb("w_q", [P, 2, D], F32)
        w_k = sb("w_k", [P, 2, D], F32)
        w_v = sb("w_v", [P, 2, D], F32)
        w_o = sb("w_o", [P, 2, D], F32)
        w_i = sb("w_i", [P, 2, IDX], F32)
        colb = sb("colb", [P, 8], F32)
        bv = sb("bv", [P, D], F32)
        bo = sb("bo", [P, D], F32)
        gw = sb("gw", [P, E], F32)
        gb = sb("gb", [P, E], F32)
        rank = sb("rank", [P, E], F32)
        y = tie[:, :].rearrange("p (t d) -> p t d", d=D)
        mtflat = MT[:, :, :, :].rearrange("p a b c -> p (a b c)")
        Kbd = mtflat[:, 0:2 * H * WORK].rearrange("p (a h n) -> p a h n", a=2, h=H)
        sqq = Pb[:, 0, 0:QG]
        sqk = Pb[:, 0, QG:2 * QG]
        qf = Pb[:, 1, 0:QG]
        qr = Pb[:, 1, QG:2 * QG]
        kf = Pb[:, 2, 0:QG]
        kr = Pb[:, 2, QG:2 * QG]
        w1 = mtflat[:, 0:2 * E * HID].bitcast(F32).rearrange("p (e h) -> p e h", e=E)
        w2 = mtflat[:, 2 * E * HID:4 * E * HID].bitcast(F32).rearrange("p (e c d) -> p e c d", e=E, c=4)
        hT = Pb[:, :, :].rearrange("p a b -> p (a b)").rearrange("p (a c n) -> p a c n", a=2, c=4)
        lg = sb("lg", [P, TPG, E], F32)
        l1 = sb("l1", [P, TPG, E], F32)
        lm = sb("lm", [P, TPG], F32)
        oh = sb("oh", [P, TPG, E], F32)
        acc = attT[:, :].rearrange("p (t d) -> p t d", d=D)

        Sp = ps("Sp", [P, 4, QG], F32)
        Po = ps("Po", [P, 2, QG], F32)
        X = ps("X", [P, 2, QG], F32)

        qd = [nc.dram_tensor(f"q_rows{a}", [D, SLOTS, S], BF16).ap() for a in range(2)]
        kd_ = [nc.dram_tensor(f"k_rows{a}", [D, SLOTS, S], BF16).ap() for a in range(2)]
        md = [nc.dram_tensor(f"shift_rows{a}", [3, H, S], BF16).ap() for a in range(2)]

        s_x = [sem(f"x_loaded{g}") for g in range(GROUPS)]
        s_w = sem("weights_loaded")
        s_moe_w = sem("expert_weights_loaded")
        s_const = sem("constants_ready")
        s_id0 = sem("identity_zeroed")
        s_id = sem("identity_ready")
        s_init = sem("vector_init_done")
        s_var = sem("variance_ready")
        s_pow = sem("rsqrt_guess_ready")
        s_xg = sem("normalised_tiles_ready")
        s_xt_ps = sem("tiles_transposed")
        s_xT = sem("xT_ready")
        s_q_ps = sem("q_projected")
        s_k_ps = sem("k_projected")
        s_v_ps = sem("v_projected")
        s_i_ps = sem("index_projected")
        s_qf = sem("q_float_ready")
        s_kf = sem("k_float_ready")
        s_qs = sem("q_parts_ready")
        s_ks = sem("k_parts_ready")
        s_va = sem("values_ready")
        s_iT = sem("index_rows_ready")
        s_sqq = sem("q_squares_ready")
        s_sqk = sem("k_squares_ready")
        s_nq_ps = sem("q_norms_summed")
        s_kn_ps = sem("k_norms_summed")
        s_kn = sem("k_norm_max_taken")
        s_kbd = sem("window_keys_ready")
        s_win_ps = sem("window_scores_ready")
        s_win = sem("window_max_taken")
        s_ngm = sem("shift_ready")
        s_m_ps = sem("shift_transposed")
        s_ms = sem("shift_parts_ready")
        s_kdg = sem("k_norm_diagonal_ready")
        s_kb_ps = sem("k_norm_spread")
        s_ok = sem("bound_checked")
        s_ok_ps = sem("bound_transposed")
        s_flag = sem("flag_ready")
        s_qd = sem("q_rows_stored")
        s_kd = sem("k_rows_stored")
        s_md = sem("shift_rows_stored")
        s_ka = sem("k_operand_loaded")
        s_qa = [sem(f"q_operand_loaded{i}") for i in range(PASSES)]
        s_qk = sem("scores_ready")
        s_exp = sem("weights_exp_done")
        s_pv = sem("weights_used")
        s_po = sem("outputs_copied")
        s_ot_ps = sem("outputs_transposed")
        s_att = sem("outputs_normalised")
        s_attT_ps = sem("att_transposed")
        s_attT = sem("attT_ready")
        s_wo_ps = sem("att_projected")
        s_res = sem("residual_added")
        s_idx_ps = sem("index_scores_ready")
        s_idx = sem("index_scores_copied")
        s_mq = sem("mask_ready")
        s_mt = [sem(f"mask_transposed{i}") for i in range(2)]
        s_ln2 = sem("moe_tiles_ready")
        s_g_ps = sem("gate_scores_ready")
        s_h_ps = sem("hidden_ready")
        s_h = sem("gelu_done")
        s_y_ps = sem("expert_output_ready")
        s_y = sem("expert_output_added")
        s_fin = sem("result_ready")
        s_out = sem("result_stored")
        s_chain = sem("vector_chain")

        block = ctx.enter_context(nc.Block())

        @block.sync
        def _(sp):
            for g in range(GROUPS):
                sp.dma_start(x[:, g * TPG:(g + 1) * TPG, :],
                             in_["x"].rearrange("b (t p) d -> p (b t) d", p=P)[:, g * TPG:(g + 1) * TPG, :]
                             ).then_inc(s_x[g], 16)
            loads = [(w_q[:, 0, :], in_["wqT"]), (w_k[:, 0, :], in_["wkT"]), (w_v[:, 0, :], in_["wvT"]),
                     (w_o[:, 0, :], in_["woT"]), (w_i[:, 0, :], in_["wqiT"]), (w_i[:, 1, :], in_["wkiT"]),
                     (w_q[:, 1, :], in_["w_qkv"][:, 0:D]), (w_k[:, 1, :], in_["w_qkv"][:, D:2 * D]),
                     (w_v[:, 1, :], in_["w_qkv"][:, 2 * D:3 * D]), (w_o[:, 1, :], in_["w_proj"]),
                     (gw[:, :], in_["gate_w"]),
                     (bv[:, :], in_["bv"].partition_broadcast(P)), (bo[:, :], in_["bo"].partition_broadcast(P)),
                     (gb[:, :], in_["gate_b"].partition_broadcast(P))]
            for i, name in enumerate(["bq", "bk", "bqi", "bki", "ln1_w", "ln1_b", "ln2_w", "ln2_b"]):
                n = in_[name].shape[0]
                loads.append((colb[0:n, i:i + 1], in_[name].rearrange("(p a) -> p a", a=1)))
            for dst, src in loads:
                sp.dma_start(dst, src).then_inc(s_w, 16)
            assert len(loads) == WEIGHT_LOADS

            def store_parts(a):
                for part, slots, dram, done in ((Ks, K_PART, kd_[a], s_kd), (Qs, Q_PART, qd[a], s_qd)):
                    sp.wait_ge(s_ks if part is Ks else s_qs, GROUPS * (a + 1))
                    for slot in range(SLOTS):
                        sp.dma_start(dram[:, slot, :], part[:, slots[slot], :]).then_inc(done, 16)

            def load_k(a):
                sp.wait_ge(s_kd, 16 * SLOTS * (a + 1))
                if a:
                    sp.wait_ge(s_qk, GROUPS * GSTEPS)
                else:
                    sp.wait_ge(s_init, 1)
                rows = kd_[a].rearrange("(j hx d) s n -> hx (d s) j n", hx=2, d=DH)
                for hx in range(2):
                    sp.dma_start(KA[64 * hx:64 * hx + KQ, :, :], rows[hx]).then_inc(s_ka, 16)

            def store_shifts(a):
                for g in range(GROUPS):
                    sp.wait_ge(s_ms, GROUPS * a + g + 1)
                    sp.dma_start(md[a].rearrange("s h n -> h s n")[:, :, g * QG:(g + 1) * QG], Ms[:, :, :]
                                 ).then_inc(s_md, 16)

            def load_q(G, hh):
                a, g = divmod(G, GROUPS)
                if g == 0 and hh == 0:
                    sp.wait_ge(s_qd, 16 * SLOTS * (a + 1))
                    sp.wait_ge(s_md, 16 * GROUPS * (a + 1))
                if 2 * G + hh >= 2:
                    sp.wait_ge(s_qk, STEPS * (2 * G + hh - 1))
                cols = slice(g * QG, (g + 1) * QG)
                rows = qd[a].rearrange("(j hx d) s n -> hx (d s) j n", hx=2, d=DH)
                shifts = md[a].rearrange("s (j hx) n -> hx s j n", hx=2)
                js = slice(hh * PPP, (hh + 1) * PPP)
                for hx in range(2):
                    sp.dma_start(QA[64 * hx:64 * hx + KQ, js, :], rows[hx][:, js, cols]).then_inc(s_qa[hh], 16)
                    sp.dma_start(QA[64 * hx + KQ:64 * hx + KROWS, js, :], shifts[hx][:, js, cols]
                                 ).then_inc(s_qa[hh], 16)

            def transpose_mask(t):
                sp.wait_ge(s_mq, t + 1)
                g, tt = divmod(t, TPG)
                if g >= 2 and tt == 0:
                    sp.wait_ge(s_qk, GSTEPS * (g - 1))
                sp.dma_start_transpose(MT[:, g % 2, :, tt * P:(tt + 1) * P], Mq[:, t % 2, :]
                                       ).then_inc(s_mt[t % 2], 16)

            store_parts(0)
            load_k(0)
            store_shifts(0)
            sp.wait_ge(s_win, TILES)
            for t in range(TPG):
                transpose_mask(t)
            load_q(0, 0)
            load_q(0, 1)
            for g in range(1, GROUPS):
                for t in range(TPG):
                    transpose_mask(g * TPG + t)
                load_q(g, 0)
                load_q(g, 1)
            store_parts(1)
            load_k(1)
            store_shifts(1)
            load_q(GROUPS, 0)
            load_q(GROUPS, 1)
            sp.wait_ge(s_win, 2 * TILES)
            for e in range(E):
                sp.dma_start(w1[:, e, :], in_["w1"][e]).then_inc(s_moe_w, 16)
                sp.dma_start(w2[:, e, :, :], in_["w2"][e].rearrange("(c p) d -> p c d", p=P)).then_inc(s_moe_w, 16)
            for G in range(GROUPS + 1, 2 * GROUPS):
                load_q(G, 0)
                load_q(G, 1)
            for g in range(GROUPS):
                sp.wait_ge(s_fin, g + 1)
                sp.dma_start(out.rearrange("b (t p) d -> p (b t) d", p=P)[:, g * TPG:(g + 1) * TPG, :],
                             x[:, g * TPG:(g + 1) * TPG, :]).then_inc(s_out, 16)
            sp.wait_ge(s_out, 16 * GROUPS)

        @block.gpsimd
        def _(pool):
            nc.gpsimd.memset(ident[:, :], 0.0).then_inc(s_id0, 1)
            nc.gpsimd.memset(identb[:, :], 0.0).then_inc(s_id0, 1)
            nc.gpsimd.memset(hmask[:, :], 1.0).then_inc(s_id0, 1)
            pool.wait_ge(s_id0, 3)
            for m in (ident, identb):
                nc.gpsimd.affine_select(out=m[:, :], in_=m[:, :], compare_op=ALU.not_equal, fill=1.0, base=0,
                                        pattern=[[-1, P]], channel_multiplier=1).then_inc(s_id, 1)
            nc.gpsimd.affine_select(out=hmask[:, :], in_=hmask[:, :], compare_op=ALU.is_ge, fill=0.0, base=0,
                                    pattern=[[-DH, H]], channel_multiplier=1).then_inc(s_id0, 1)
            pool.wait_ge(s_id0, 4)
            nc.gpsimd.affine_select(out=hmask[:, :], in_=hmask[:, :], compare_op=ALU.is_ge, fill=0.0, base=DH - 1,
                                    pattern=[[DH, H]], channel_multiplier=-1).then_inc(s_id, 1)
            nc.gpsimd.memset(mhalf[:, :], -0.5).then_inc(s_const, 1)
            nc.gpsimd.iota(tie[:, :].bitcast(I32), pattern=[[1, S]], base=1, channel_multiplier=0).then_inc(s_const, 1)
            nc.gpsimd.iota(rank[:, :].bitcast(I32), pattern=[[-1, E]], base=E, channel_multiplier=0
                           ).then_inc(s_const, 1)
            pool.wait_ge(s_const, 3)
            for n in range(4):
                pool.wait_ge(s_var, n + 1)
                nc.gpsimd.tensor_tensor(rs[:, :], ve[:, :], mhalf[:, :], ALU.pow).then_inc(s_pow, 1)

        @block.scalar
        def _(act):
            def prologue(a):
                for g in range(GROUPS):
                    G = GROUPS * a + g
                    cols = slice(g * QG, (g + 1) * QG)
                    act.wait_ge(s_xt_ps, G + 1)
                    if a == 0:
                        nc.scalar.activation(xT[:, cols], X[:, 0, :], ACT.Copy).then_inc(s_xT, 1)
                    else:
                        nc.scalar.activation(xT[:, cols], X[:, 0, :], ACT.Identity, scale=colb[:, 4:5],
                                             bias=colb[:, 5:6]).then_inc(s_xT, 1)
                    act.wait_ge(s_qf, G + 1)
                    nc.scalar.activation(sqq, qf, ACT.Square).then_inc(s_sqq, 1)
                    act.wait_ge(s_kf, G + 1)
                    if G:
                        act.wait_ge(s_kn_ps, G)
                    nc.scalar.activation(sqk, Sp[:, 1, :], ACT.Square).then_inc(s_sqk, 1)
                    if a == 0:
                        act.wait_ge(s_i_ps, g + 1)
                        nc.scalar.activation(qiT[:, cols], Sp[0:IDX, 3, :], ACT.Identity, bias=colb[0:IDX, 2:3]
                                             ).then_inc(s_iT, 1)
                        nc.scalar.activation(kiT[:, cols], Po[0:IDX, 1, :], ACT.Identity, bias=colb[0:IDX, 3:4]
                                             ).then_inc(s_iT, 1)

            def attention(a):
                for G in range(GROUPS * a, GROUPS * (a + 1)):
                    for s in range(GSTEPS):
                        n = GSTEPS * G + s
                        act.wait_ge(s_qk, n + 1)
                        if n >= 4:
                            act.wait_ge(s_pv, (n - 4) // 2 + 1)
                        nc.scalar.activation(Pb[:, n % 4, :], Sp[:, 2 * (n % 2):2 * (n % 2) + 2, :], ACT.Exp
                                             ).then_inc(s_exp, 1)

            act.wait_ge(s_w, 16 * WEIGHT_LOADS)
            prologue(0)
            attention(0)
            prologue(1)
            attention(1)
            for g in range(GROUPS):
                G = 2 * GROUPS + g
                cols = slice(g * QG, (g + 1) * QG)
                act.wait_ge(s_xt_ps, G + 1)
                nc.scalar.activation(xT[:, cols], X[:, 0, :], ACT.Identity, scale=colb[:, 6:7], bias=colb[:, 7:8]
                                     ).then_inc(s_xT, 1)
                for e in range(E):
                    i = g * E + e
                    if i >= 2:
                        act.wait_ge(s_y_ps, i - 1)
                    for c in range(4):
                        act.wait_ge(s_h_ps, 4 * i + c + 1)
                        nc.scalar.activation(hT[:, i % 2, c, :], Sp[:, c, :], ACT.Gelu_apprx_tanh).then_inc(s_h, 1)

        @block.tensor
        def _(pe):
            mm = nc.tensor.matmul

            def transpose_tiles(G):
                pe.wait_ge(s_xg, G + 1)
                if G:
                    pe.wait_ge(s_xT, G)
                for tt in range(TPG):
                    last = nc.tensor.transpose(X[:, 0, tt * P:(tt + 1) * P], att[:, tt, :], ident[:, :])
                last.then_inc(s_xt_ps, 1)
                pe.wait_ge(s_xT, G + 1)

            def prologue(a):
                if a:
                    pe.wait_ge(s_res, GROUPS)
                for g in range(GROUPS):
                    G = GROUPS * a + g
                    cols = slice(g * QG, (g + 1) * QG)
                    transpose_tiles(G)
                    if G:
                        pe.wait_ge(s_qf, G)
                    mm(Sp[:, 0, :], w_q[:, a, :], xT[:, cols], start=True, stop=True).then_inc(s_q_ps, 1)
                    if G:
                        pe.wait_ge(s_kf, G)
                        pe.wait_ge(s_sqk, G)
                    mm(Sp[:, 1, :], w_k[:, a, :], xT[:, cols], start=True, stop=True).then_inc(s_k_ps, 1)
                    if G:
                        pe.wait_ge(s_va, G)
                    for tt in range(TPG):
                        last = mm(Sp[:, 2, tt * P:(tt + 1) * P], xT[:, g * QG + tt * P:g * QG + (tt + 1) * P],
                                  w_v[:, a, :], start=True, stop=True)
                    last.then_inc(s_v_ps, 1)
                    if a == 0:
                        if g:
                            pe.wait_ge(s_iT, 2 * g)
                        mm(Sp[0:IDX, 3, :], w_i[:, 0, :], xT[:, cols], start=True, stop=True)
                        mm(Po[0:IDX, 1, :], w_i[:, 1, :], xT[:, cols], start=True, stop=True).then_inc(s_i_ps, 1)
                    pe.wait_ge(s_sqq, G + 1)
                    for tt in range(TPG):
                        t = g * TPG + tt
                        last = mm(Po[:, 0, t * H:(t + 1) * H], sqq[:, tt * P:(tt + 1) * P], hmask[:, :],
                                  start=True, stop=True, skip_group_check=True)
                    last.then_inc(s_nq_ps, 1)
                    pe.wait_ge(s_sqk, G + 1)
                    if G:
                        pe.wait_ge(s_kn, G)
                    mm(X[0:H, 1, :], hmask[:, :], sqk, start=True, stop=True).then_inc(s_kn_ps, 1)
                pe.wait_ge(s_kdg, a + 1)
                if a == 0:
                    pe.wait_ge(s_iT, 2 * GROUPS)
                mm(Po[:, 1, 0:H], ones[:, :], kd[:, 2:2 + H], start=True, stop=True).then_inc(s_kb_ps, 1)
                pe.wait_ge(s_kbd, a + 1)
                pe.wait_ge(s_va, GROUPS * (a + 1))
                pe.wait_ge(s_sqk, GROUPS * (a + 1))
                for t in range(TILES):
                    n = TILES * a + t
                    if t >= 2:
                        pe.wait_ge(s_win, n - 1)
                    for i, (qp, kp) in enumerate(((0, 0), (0, 1), (1, 0))):
                        for hf in range(2):
                            last = mm(Sp[:, 2 * (t % 2) + hf, :], Qs[:, qp, t * P:(t + 1) * P],
                                      Kbd[:, kp, hf * 8:(hf + 1) * 8, :], start=(i == 0), stop=(i == 2),
                                      skip_group_check=True)
                    last.then_inc(s_win_ps, 1)
                pe.wait_ge(s_ngm, a + 1)
                pe.wait_ge(s_kn, GROUPS * (a + 1))
                for g in range(GROUPS):
                    G = GROUPS * a + g
                    if g >= 1:
                        pe.wait_ge(s_ms, G)
                    for tt in range(TPG):
                        last = nc.tensor.transpose(X[0:H, 1, tt * P:(tt + 1) * P], ngm[:, g * TPG + tt, :],
                                                   ident[:, :])
                    last.then_inc(s_m_ps, 1)
                pe.wait_ge(s_ok, a + 1)
                pe.wait_ge(s_ms, GROUPS * (a + 1))
                nc.tensor.transpose(X[0:1, 1, 0:P], fl[:, 0:1], ident[:, :]).then_inc(s_ok_ps, 1)
                pe.wait_ge(s_flag, a + 1)

            def index_chunk(t, c):
                i = 4 * t + c
                w = min(QG, ASSOC - c * QG)
                if i >= 2:
                    pe.wait_ge(s_idx, i - 1)
                mm(X[:, c % 2, 0:w], qiT[:, t * P:(t + 1) * P], kiT[:, c * QG:c * QG + w], start=True, stop=True
                   ).then_inc(s_idx_ps, 1)

            def scores(G, s):
                a = G // GROUPS
                n = GSTEPS * G + s
                hh, r = divmod(s, STEPS)
                kb, jj = divmod(r, PPP)
                j = hh * PPP + jj
                if r == 0:
                    pe.wait_ge(s_qa[hh], 64 * (G + 1))
                if n >= 2:
                    pe.wait_ge(s_exp, n - 1)
                for hx in range(2):
                    last = mm(Sp[:, 2 * (n % 2) + hx, :], KA[64 * hx:64 * hx + KROWS, j, kb * P:(kb + 1) * P],
                              QA[64 * hx:64 * hx + KROWS, j, :], start=True, stop=(a == 1), skip_group_check=True)
                if a == 0:
                    for hx in range(2):
                        last = mm(Sp[:, 2 * (n % 2) + hx, :], identb[:, :], MT[:, G % 2, kb, :],
                                  start=False, stop=True, skip_group_check=True)
                last.then_inc(s_qk, 1)

            def weighted_values(G, s):
                n = GSTEPS * G + s
                hh, r = divmod(s, STEPS)
                kb, jj = divmod(r, PPP)
                q = jj // 2
                pe.wait_ge(s_exp, n + 1)
                if kb == 0 and 2 * G + hh >= 1:
                    pe.wait_ge(s_po, 2 * G + hh)
                for i in range(4):
                    h = hh * 8 + q * 4 + i
                    last = mm(Po[32 * i:32 * i + VW, q, :], VA[:, kb, h, :],
                              Pb[:, (n - 1 + i // 2) % 4, (i % 2) * QG:(i % 2 + 1) * QG],
                              start=(kb == 0), stop=(kb == TILES - 1), skip_group_check=True)
                last.then_inc(s_pv, 1)

            def tail_outputs(G):
                pe.wait_ge(s_po, 2 * (G + 1))
                for tt in range(TPG):
                    if tt >= 2:
                        pe.wait_ge(s_att, TPG * G + tt - 1)
                    for i in range(4):
                        last = nc.tensor.transpose(X[:, tt % 2, i * P:(i + 1) * P],
                                                   OT[:, i // 2, i % 2, tt * P:(tt + 1) * P], ident[:, :])
                    last.then_inc(s_ot_ps, 1)

            def tail_transpose(G):
                pe.wait_ge(s_att, TPG * (G + 1))
                for tt in range(TPG):
                    last = nc.tensor.transpose(X[:, 0, tt * P:(tt + 1) * P], att[:, tt, :], ident[:, :])
                last.then_inc(s_attT_ps, 1)

            def tail_project(G):
                pe.wait_ge(s_attT, G + 1)
                for tt in range(TPG):
                    last = mm(X[:, 1, tt * P:(tt + 1) * P], attT[:, tt * P:(tt + 1) * P], w_o[:, G // GROUPS, :],
                              start=True, stop=True)
                last.then_inc(s_wo_ps, 1)

            def attention(a):
                pe.wait_ge(s_ka, 32 * (a + 1))
                for G in range(GROUPS * a, GROUPS * (a + 1)):
                    g = G % GROUPS
                    if a == 0:
                        for i in range(2):
                            pe.wait_ge(s_mt[i], 16 * 2 * (g + 1))
                    for s in range(GSTEPS):
                        scores(G, s)
                        if s % 2 and s > 1:
                            weighted_values(G, s - 2)
                        if g:
                            if s == 5:
                                if a == 0:
                                    pe.wait_ge(s_idx, 4 * TPG * min(g + 1, GROUPS))
                                tail_outputs(G - 1)
                            if s == 13:
                                tail_transpose(G - 1)
                            if s == 17:
                                tail_project(G - 1)
                        if a == 0 and g + 1 < GROUPS:
                            for k in range(TPG * TOPK_OPS):
                                if topk_step(k) == s and k % TOPK_OPS < 4:
                                    if k == 0 and g:
                                        pe.wait_ge(s_res, G)
                                    index_chunk((g + 1) * TPG + k // TOPK_OPS, k % TOPK_OPS)
                    weighted_values(G, GSTEPS - 1)
                G = GROUPS * (a + 1) - 1
                tail_outputs(G)
                tail_transpose(G)
                tail_project(G)

            pe.wait_ge(s_id, 3)
            pe.wait_ge(s_w, 16 * WEIGHT_LOADS)
            pe.wait_ge(s_init, 1)
            prologue(0)
            for t in range(TPG):
                for c in range(4):
                    index_chunk(t, c)
            pe.wait_ge(s_idx, 4 * TPG)
            attention(0)
            prologue(1)
            attention(1)
            pe.wait_ge(s_res, 2 * GROUPS)
            pe.wait_ge(s_moe_w, 32 * E)
            for g in range(GROUPS):
                cols = slice(g * QG, (g + 1) * QG)
                transpose_tiles(2 * GROUPS + g)
                if g:
                    pe.wait_ge(s_fin, g)
                for tt in range(TPG):
                    last = mm(X[:, 1, tt * E:(tt + 1) * E], xT[:, g * QG + tt * P:g * QG + (tt + 1) * P], gw[:, :],
                              start=True, stop=True)
                last.then_inc(s_g_ps, 1)

                def hidden(e):
                    for c in range(4):
                        i = 4 * (g * E + e) + c
                        if i >= 4:
                            pe.wait_ge(s_h, i - 3)
                        mm(Sp[:, c, :], w1[:, e, c * P:(c + 1) * P], xT[:, cols], start=True, stop=True
                           ).then_inc(s_h_ps, 1)

                def output(e):
                    i = g * E + e
                    pe.wait_ge(s_h, 4 * (i + 1))
                    if i >= 2:
                        pe.wait_ge(s_y, i - 1)
                    for tt in range(TPG):
                        for c in range(4):
                            last = mm(Po[:, i % 2, tt * P:(tt + 1) * P], hT[:, i % 2, c, tt * P:(tt + 1) * P],
                                      w2[:, e, c, :], start=(c == 0), stop=(c == 3), skip_group_check=True)
                    last.then_inc(s_y_ps, 1)

                hidden(0)
                for e in range(E):
                    if e + 1 < E:
                        hidden(e + 1)
                    output(e)

        @block.vector
        def _(dve):
            v = nc.vector
            chained = [0]

            def link(ins):
                chained[0] += 1
                ins.then_inc(s_chain, 1)
                dve.wait_ge(s_chain, chained[0])

            def statistics(src, n):
                for t in range(TILES):
                    if n == 0 and t % TPG == 0:
                        dve.wait_ge(s_x[t // TPG], 16)
                    last = v.bn_stats(st[:, t, :], src[:, t, :])
                link(last)
                for t in range(TILES):
                    last = v.bn_aggr(mv[:, t, :], st[:, t, :])
                link(last)
                v.tensor_scalar(ve[:, :], mv[:, :, 1], EPS, None, ALU.add).then_inc(s_var, 1)
                dve.wait_ge(s_var, n + 1)
                dve.wait_ge(s_pow, n + 1)
                link(v.tensor_tensor(rt[:, :], rs[:, :], rs[:, :], ALU.mult))
                link(v.tensor_tensor(rt[:, :], rt[:, :], ve[:, :], ALU.mult))
                link(v.tensor_scalar(rt[:, :], rt[:, :], -0.5, 1.5, ALU.mult, ALU.add))
                link(v.tensor_tensor(rs[:, :], rs[:, :], rt[:, :], ALU.mult))

            def normalise(dst, src, t):
                return v.tensor_scalar(dst, src[:, t, :], mv[:, t, 0:1], rs[:, t:t + 1], ALU.subtract, ALU.mult)

            def tiles_for_transpose(src, G):
                if G:
                    dve.wait_ge(s_xt_ps, G)
                for tt in range(TPG):
                    last = normalise(att[:, tt, :], src, (G % GROUPS) * TPG + tt)
                last.then_inc(s_xg, 1)

            def split(full, rest, parts, cols):
                link(v.tensor_copy(parts[:, 0, cols], full))
                link(v.tensor_tensor(rest, full, parts[:, 0, cols], ALU.subtract))
                link(v.tensor_copy(parts[:, 1, cols], rest))
                return v.tensor_tensor(parts[:, 2, cols], rest, parts[:, 1, cols], ALU.subtract)

            def prologue(a, src):
                if a:
                    dve.wait_ge(s_attT_ps, GROUPS)
                    dve.wait_ge(s_qd, 16 * SLOTS)
                    dve.wait_ge(s_kd, 16 * SLOTS)
                tiles_for_transpose(src, GROUPS * a)
                for g in range(GROUPS):
                    G = GROUPS * a + g
                    cols = slice(g * QG, (g + 1) * QG)
                    if g + 1 < GROUPS:
                        tiles_for_transpose(src, G + 1)
                    dve.wait_ge(s_q_ps, G + 1)
                    if G:
                        dve.wait_ge(s_sqq, G)
                    if a == 0:
                        v.tensor_scalar(qf, Sp[:, 0, :], colb[:, 0:1], SCALE, ALU.add, ALU.mult).then_inc(s_qf, 1)
                    else:
                        v.tensor_scalar(qf, Sp[:, 0, :], SCALE, None, ALU.mult).then_inc(s_qf, 1)
                    dve.wait_ge(s_k_ps, G + 1)
                    if a == 0:
                        v.tensor_scalar(kf, Sp[:, 1, :], colb[:, 1:2], None, ALU.add).then_inc(s_kf, 1)
                    else:
                        v.tensor_copy(kf, Sp[:, 1, :]).then_inc(s_kf, 1)
                    dve.wait_ge(s_qf, G + 1)
                    split(qf, qr, Qs, cols).then_inc(s_qs, 1)
                    dve.wait_ge(s_kf, G + 1)
                    split(kf, kr, Ks, cols).then_inc(s_ks, 1)
                    dve.wait_ge(s_v_ps, G + 1)
                    vdst = VA[:, g * TPG:(g + 1) * TPG, :, 0:DH]
                    vsrc = Sp[:, 2, :].rearrange("p (t h d) -> p t h d", t=TPG, h=H)
                    if a == 0:
                        for tt in range(TPG):
                            last = v.tensor_tensor(vdst[:, tt], vsrc[:, tt],
                                                   bv[:, :].rearrange("p (h d) -> p h d", h=H), ALU.add)
                    else:
                        last = v.tensor_copy(vdst, vsrc)
                    last.then_inc(s_va, 1)
                    dve.wait_ge(s_kn_ps, G + 1)
                    v.tensor_reduce(kn[:, g:g + 1], X[0:H, 1, :], AX_X, ALU.max).then_inc(s_kn, 1)
                dve.wait_ge(s_ks, GROUPS * (a + 1))
                for part in range(2):
                    last = v.tensor_tensor(Kbd[:, part], Ks[:, part, ASSOC:S].unsqueeze(1).to_broadcast([P, H, WORK]),
                                           hmask[:, :].unsqueeze(2).to_broadcast([P, H, WORK]), ALU.mult)
                last.then_inc(s_kbd, 1)
                dve.wait_ge(s_kn, GROUPS * (a + 1))
                link(v.tensor_reduce(kd[:, 0:1], kn[:, :], AX_X, ALU.max))
                v.tensor_scalar(kd[:, 2:2 + H], ident[0:H, 0:H], kd[:, 0:1], None, ALU.mult).then_inc(s_kdg, 1)
                for t in range(TILES):
                    n = TILES * a + t
                    dve.wait_ge(s_win_ps, n + 1)
                    v.tensor_reduce(mx[:, t, :],
                                    Sp[:, 2 * (t % 2):2 * (t % 2) + 2, :].rearrange("p b (h n) -> p (b h) n", n=WORK),
                                    AX_X, ALU.max).then_inc(s_win, 1)
                dve.wait_ge(s_win, TILES * (a + 1))
                v.tensor_scalar(ngm[:, :, :], mx[:, :, :], -1.0, -SHIFT[a], ALU.mult, ALU.add).then_inc(s_ngm, 1)
                dve.wait_ge(s_nq_ps, GROUPS * (a + 1))
                link(v.tensor_copy(nq[:, :, :], Po[:, 0, 0:TILES * H].rearrange("p (t h) -> p t h", h=H)))
                dve.wait_ge(s_kb_ps, a + 1)
                link(v.tensor_tensor(nq[:, :, :], nq[:, :, :],
                                     Po[:, 1, 0:H].unsqueeze(1).to_broadcast([P, TILES, H]), ALU.mult))
                if a == 0:
                    link(v.tensor_scalar(ok[:, :, :], nq[:, :, :], 4.0, LIMIT[0] ** 2, ALU.mult, ALU.is_le))
                else:
                    link(v.tensor_scalar(mx[:, :, :], mx[:, :, :], LIMIT[1], None, ALU.add))
                    link(v.tensor_scalar(ok[:, :, :], mx[:, :, :], 0.0, None, ALU.max))
                    link(v.tensor_tensor(mx[:, :, :], ok[:, :, :], mx[:, :, :], ALU.mult))
                    link(v.tensor_tensor(ok[:, :, :], nq[:, :, :], mx[:, :, :], ALU.is_le))
                v.tensor_reduce(fl[:, 0:1], ok[:, :, :].rearrange("p t h -> p (t h)"), AX_X, ALU.min
                                ).then_inc(s_ok, 1)
                for g in range(GROUPS):
                    G = GROUPS * a + g
                    dve.wait_ge(s_m_ps, G + 1)
                    if G:
                        dve.wait_ge(s_md, 16 * G)
                    link(v.tensor_copy(msc[:, 0, :], X[0:H, 1, :]))
                    split(msc[:, 0, :], msc[:, 1, :], Ms, slice(0, QG)).then_inc(s_ms, 1)
                dve.wait_ge(s_ok_ps, a + 1)
                link(v.tensor_reduce(fl[0:1, 1:2], X[0:1, 1, 0:P], AX_X, ALU.min))
                v.tensor_copy(fli[0:1, a:a + 1], fl[0:1, 1:2]).then_inc(s_flag, 1)

            def select(t, k):
                w = sw[:, :]
                if k < 4:
                    i = 4 * t + k
                    n = min(QG, ASSOC - k * QG)
                    dve.wait_ge(s_idx_ps, i + 1)
                    if k == 0 and t:
                        dve.wait_ge(s_mq, t)
                    v.scalar_tensor_tensor(out=w[:, k * QG:k * QG + n], in0=X[:, k % 2, 0:n], scalar=0.0,
                                           in1=tie[:, k * QG:k * QG + n], op0=ALU.max, op1=ALU.add
                                           ).then_inc(s_idx, 1)
                    if k == 3:
                        dve.wait_ge(s_idx, i + 1)
                elif k < TOPK_OPS - 1:
                    if k % 2 == 0:
                        link(v.max(top8[:, :], w))
                    else:
                        link(v.match_replace(w, top8[:, :], w, TAKEN))
                else:
                    if t >= 2:
                        dve.wait_ge(s_mt[t % 2], 16 * (t // 2))
                    v.tensor_scalar(Mq[:, t % 2, 0:ASSOC], w, TAKEN, -BIG, ALU.is_gt, ALU.mult).then_inc(s_mq, 1)

            def copy_outputs(G, hh):
                dve.wait_ge(s_pv, (GSTEPS * G + STEPS * (hh + 1)) // 2)
                if G and hh == 0:
                    dve.wait_ge(s_ot_ps, TPG * G)
                v.tensor_copy(OT[:, hh, :, :], Po[:, :, :]).then_inc(s_po, 1)

            def tail_normalise(G):
                for tt in range(TPG):
                    n = TPG * G + tt
                    dve.wait_ge(s_ot_ps, n + 1)
                    o = X[:, tt % 2, :].rearrange("p (h c) -> p h c", h=H)
                    link(v.reciprocal(rec[:, tt % 2, :], o[:, :, DH]))
                    v.tensor_tensor(att[:, tt, :].rearrange("p (h d) -> p h d", h=H), o[:, :, 0:DH],
                                    rec[:, tt % 2, :].unsqueeze(2).to_broadcast([P, H, DH]), ALU.mult
                                    ).then_inc(s_att, 1)

            def tail_copy(G):
                dve.wait_ge(s_attT_ps, G + 1)
                v.tensor_copy(attT[:, :], X[:, 0, :]).then_inc(s_attT, 1)

            def tail_residual(G):
                a, g = divmod(G, GROUPS)
                dve.wait_ge(s_wo_ps, G + 1)
                res = (x if a == 0 else y)[:, g * TPG:(g + 1) * TPG, :]
                o = X[:, 1, :].rearrange("p (t d) -> p t d", d=D)
                if a == 0:
                    link(v.tensor_tensor(acc[:, :, :], o, bo[:, :].unsqueeze(1).to_broadcast([P, TPG, D]), ALU.add))
                    v.tensor_tensor(res, res, acc[:, :, :], ALU.add).then_inc(s_res, 1)
                else:
                    v.tensor_tensor(res, res, o, ALU.add).then_inc(s_res, 1)

            def attention(a):
                for G in range(GROUPS * a, GROUPS * (a + 1)):
                    g = G % GROUPS
                    for s in range(GSTEPS):
                        if g:
                            if s == 7:
                                tail_normalise(G - 1)
                            if s == 15:
                                tail_copy(G - 1)
                            if s == 20:
                                tail_residual(G - 1)
                        if a == 0 and g + 1 < GROUPS:
                            for k in range(TPG * TOPK_OPS):
                                if topk_step(k) == s:
                                    select((g + 1) * TPG + k // TOPK_OPS, k % TOPK_OPS)
                        if s == STEPS + 1:
                            copy_outputs(G, 0)
                    copy_outputs(G, 1)
                tail_normalise(G)
                tail_copy(G)
                tail_residual(G)

            link(v.memset(KA[:, :, :], 1.0))
            v.memset(VA[:, :, :, :], 1.0)
            v.memset(Mq[:, :, ASSOC:S], 0.0)
            v.memset(ones[:, :], 1.0)
            v.memset(Po[:, :, :], 0.0).then_inc(s_init, 1)
            dve.wait_ge(s_init, 1)
            statistics(x, 0)
            dve.wait_ge(s_const, 3)
            v.tensor_scalar(tie[:, :], tie[:, :].bitcast(I32), -TIE, None, ALU.mult)
            link(v.tensor_scalar(rank[:, :], rank[:, :].bitcast(I32), 1.0, None, ALU.mult))
            dve.wait_ge(s_w, 16 * WEIGHT_LOADS)
            dve.wait_ge(s_id, 3)
            prologue(0, x)
            for t in range(TPG):
                for k in range(TOPK_OPS):
                    select(t, k)
            attention(0)
            dve.wait_ge(s_res, GROUPS)
            statistics(x, 1)
            for t in range(TILES):
                last = normalise(y[:, t, :], x, t)
            link(last)
            statistics(y, 2)
            prologue(1, y)
            attention(1)
            dve.wait_ge(s_res, 2 * GROUPS)
            statistics(y, 3)
            dve.wait_ge(s_attT_ps, 2 * GROUPS)
            tiles_for_transpose(y, 2 * GROUPS)
            for g in range(GROUPS):
                G = 2 * GROUPS + g
                if g + 1 < GROUPS:
                    tiles_for_transpose(y, G + 1)
                dve.wait_ge(s_g_ps, g + 1)
                link(v.tensor_tensor(lg[:, :, :], X[:, 1, 0:TPG * E].rearrange("p (t e) -> p t e", e=E),
                                     gb[:, :].unsqueeze(1).to_broadcast([P, TPG, E]), ALU.add))
                link(v.tensor_reduce(lm[:, :], lg[:, :, :], AX_X, ALU.max))
                link(v.tensor_tensor(l1[:, :, :], lg[:, :, :], lm[:, :].unsqueeze(2).to_broadcast([P, TPG, E]),
                                     ALU.is_equal))
                link(v.tensor_tensor(l1[:, :, :], l1[:, :, :], rank[:, :].unsqueeze(1).to_broadcast([P, TPG, E]),
                                     ALU.mult))
                link(v.tensor_reduce(lm[:, :], l1[:, :, :], AX_X, ALU.max))
                link(v.tensor_tensor(oh[:, :, :], l1[:, :, :], lm[:, :].unsqueeze(2).to_broadcast([P, TPG, E]),
                                     ALU.is_equal))
                res = x[:, g * TPG:(g + 1) * TPG, :]
                link(v.tensor_tensor(res, res, y[:, g * TPG:(g + 1) * TPG, :], ALU.add))
                for e in range(E):
                    i = g * E + e
                    dve.wait_ge(s_y_ps, i + 1)
                    for tt in range(TPG):
                        last = v.scalar_tensor_tensor(out=res[:, tt, :], in0=Po[:, i % 2, tt * P:(tt + 1) * P],
                                                      scalar=oh[:, tt, e:e + 1], in1=res[:, tt, :],
                                                      op0=ALU.mult, op1=ALU.add)
                    last.then_inc(s_y, 1)
                    dve.wait_ge(s_y, i + 1)
                v.tensor_copy(lm[:, 0:1], lm[:, 0:1]).then_inc(s_fin, 1)


WEIGHT_LOADS = 22


def kernel(**inputs):
    import numpy as np
    import concourse.bacc as bacc
    from concourse.bass_utils import run_bass_kernel_spmd

    def flat(name):
        return np.ascontiguousarray(inputs[name])

    def turned(name):
        return np.ascontiguousarray(np.asarray(inputs[name]).T)

    given = {
        "x": flat("L0_attn_x"), "wqT": turned("L0_attn_wq"), "bq": flat("L0_attn_bq"), "wkT": turned("L0_attn_wk"),
        "bk": flat("L0_attn_bk"), "wvT": turned("L0_attn_wv"), "bv": flat("L0_attn_bv"), "woT": turned("L0_attn_wo"),
        "bo": flat("L0_attn_bo"), "wqiT": turned("L0_attn_wqi"), "bqi": flat("L0_attn_bqi"),
        "wkiT": turned("L0_attn_wki"), "bki": flat("L0_attn_bki"), "ln1_w": flat("L0_ffn_ln1_w"),
        "ln1_b": flat("L0_ffn_ln1_b"), "w_qkv": flat("L0_ffn_w_qkv"), "w_proj": flat("L0_ffn_w_proj"),
        "ln2_w": flat("L0_ffn_ln2_w"), "ln2_b": flat("L0_ffn_ln2_b"), "gate_w": flat("L0_ffn_gate_w"),
        "gate_b": flat("L0_ffn_gate_b"), "w1": flat("L0_ffn_w1"), "w2": flat("L0_ffn_w2"),
    }
    nc = bacc.Bacc("TRN2", target_bir_lowering=False, num_devices=1)
    in_ = {n: nc.dram_tensor(f"in_{n}", a.shape, mybir.dt.from_np(a.dtype), kind="ExternalInput").ap()
           for n, a in given.items()}
    out = nc.dram_tensor("out", (1, S, D), F32, kind="ExternalOutput").ap()
    build(nc, in_, out)
    r = run_bass_kernel_spmd(nc, [{f"in_{n}": a for n, a in given.items()}], core_ids=[0])
    return r.results[0]["out"]
```

```python
from contextlib import ExitStack

import concourse.bass as bass
from concourse import mybir

F32 = mybir.dt.float32
BF16 = mybir.dt.bfloat16
I32 = mybir.dt.int32
ALU = mybir.AluOpType
ACT = mybir.ActivationFunctionType
AX_X = mybir.AxisListType.X

P = 128
S = 2048
D = 128
H = 16
DH = D // H
WORK = 64
ASSOC = S - WORK
TOPK = 64
IDX = 64
E = 8
HID = 4 * D
EPS = 1e-5
SCALE = float(DH) ** -0.5

QG = 512
GROUPS = S // QG
TPG = QG // P
TILES = S // P
PASSES = 2
PAIRS = H // 2
PPP = PAIRS // PASSES
STEPS = TILES * PPP
GSTEPS = PASSES * STEPS
SLOTS = 6
KQ = SLOTS * DH
KROWS = KQ + 3
VW = DH + 1
Q_PART = (0, 0, 0, 1, 1, 2)
K_PART = (0, 1, 2, 0, 1, 0)

MASK = 2.0 ** 117
TAKEN = -3.0e38
KEPT = 3.0e38
STRIPES = 64
TIE = 2.0 ** -100

SHIFT = (0.0, 48.0)
LIMIT = (72.0, 116.0)

ROUNDS = TOPK // 8
COPIES = -(-ASSOC // QG)
PIECES = COPIES + STRIPES // 8 + ROUNDS + 1
FIRST_PIECE = 22


def piece_at(s):
    k = s - FIRST_PIECE
    return divmod(k, PIECES) if 0 <= k < TPG * PIECES else None


def count_at(s):
    k = s - 6 - FIRST_PIECE
    return k // PIECES if 0 <= k < TPG * PIECES and k % PIECES == PIECES - 1 else None


CHECK_STEP = 114
CAREFUL_STEP = 121


KEYS_AHEAD = 4


def masker(g, s):
    if s % 2 == 0:
        return "pool"
    busy = g < GROUPS - 1 and FIRST_PIECE <= s < FIRST_PIECE + TPG * PIECES
    return "pe" if busy else "dve"


MASKED_BEFORE = {who: [sum(masker(n // GSTEPS, n % GSTEPS) == who for n in range(m))
                       for m in range(GROUPS * GSTEPS + 1)] for who in ("pool", "dve")}


def masked(who, g, s):
    return MASKED_BEFORE[who][GSTEPS * g + s]


def bank_pair(n):
    G, s = divmod(n, GSTEPS)
    free = G >= GROUPS - 1 and s >= 24
    return (n - 24) % 3 if free else n % 2


BANKS = [bank_pair(n) for n in range(2 * GROUPS * GSTEPS)]
LAST_IN_BANKS = [max((m for m in range(max(0, n - 8), n) if BANKS[m] == BANKS[n]), default=None)
                 for n in range(2 * GROUPS * GSTEPS)]


def build(nc, in_, out):
    ctx = ExitStack()
    with ctx:
        def sb(name, shape, dt):
            return ctx.enter_context(nc.sbuf_tensor(name, shape, dt))

        def ps(name, shape, dt):
            return ctx.enter_context(nc.psum_tensor(name, shape, dt))

        def sem(name):
            return ctx.enter_context(nc.semaphore(name))

        x = sb("x", [P, TILES, D], F32)
        xT = sb("xT", [P, S], F32)
        Qs = sb("Qs", [P, 2, S], BF16)
        Ks = sb("Ks", [P, 2, S], BF16)
        KA = sb("KA", [P, PAIRS, S], BF16)
        QA = sb("QA", [P, H, QG], BF16)
        VA = sb("VA", [P, TILES, H, VW], F32)
        Pb = sb("Pb", [P, 4, 2 * QG], F32)
        MT = sb("MT", [P, 2, TILES, QG], BF16)
        Mq = sb("Mq", [P, 2, S], BF16)
        sw = sb("sw", [P, ASSOC], F32)
        tie = sb("tie", [P, S], F32)
        kiT = sb("kiT", [IDX, S], F32)
        qiT = sb("qiT", [IDX, S], F32)
        OT = sb("OT", [P, PASSES, 2, QG], F32)
        msc = sw[0:H, 0:2 * QG].rearrange("p (a n) -> p a n", a=2)
        Ms = sw[0:H, 2 * QG:2 * QG + 3 * QG // 2].bitcast(BF16).rearrange("p (a n) -> p a n", a=3)
        att = sb("att", [P, TPG, D], F32)
        attT = sb("attT", [P, QG], F32)
        mx = sb("mx", [P, TILES, H], F32)
        ngm = sb("ngm", [P, TILES, H], F32)
        nq = sb("nq", [P, TILES, H], F32)
        ok = sb("ok", [P, TILES, H], F32)
        mv = sb("mv", [P, TILES, 2], F32)
        st = sb("st", [P, TILES, 6], F32)
        ve = sb("ve", [P, TILES], F32)
        rs = sb("rs", [P, TILES], F32)
        rt = sb("rt", [P, TILES], F32)
        mhalf = sb("mhalf", [P, TILES], F32)
        top8 = sb("top8", [P, 8], F32)
        cand = sb("cand", [P, STRIPES * 8], F32)
        cnt = sb("cnt", [P, TILES], F32)
        cm = sb("cm", [P, 4], F32)
        keep = sb("keep", [P, KEYS_AHEAD, QG], BF16)
        rec = sb("rec", [P, 2, H], F32)
        kn = sb("kn", [H, GROUPS], F32)
        kd = sb("kd", [H, 2 + H], F32)
        fl = sb("fl", [P, 4], F32)
        fli = sb("fli", [1, GROUPS + 1], I32)
        ident = sb("ident", [P, P], F32)
        identb = sb("identb", [P, P], BF16)
        ones = sb("ones", [H, P], F32)
        hmask = sb("hmask", [P, H], F32)
        w_q = sb("w_q", [P, 2, D], F32)
        w_k = sb("w_k", [P, 2, D], F32)
        w_v = sb("w_v", [P, 2, D], F32)
        w_o = sb("w_o", [P, 2, D], F32)
        w_i = sb("w_i", [P, 2, IDX], F32)
        colb = sb("colb", [P, 8], F32)
        bv = sb("bv", [P, D], F32)
        bo = sb("bo", [P, D], F32)
        gw = sb("gw", [P, E], F32)
        gb = sb("gb", [P, E], F32)
        rank = sb("rank", [P, E], F32)
        Lo = Mq
        y = tie[:, :].rearrange("p (t d) -> p t d", d=D)
        mtflat = MT[:, :, :, :].rearrange("p a b c -> p (a b c)")
        Kbd = mtflat[:, 0:2 * H * WORK].rearrange("p (a h n) -> p a h n", a=2, h=H)
        sqq = Pb[:, 0, 0:QG]
        sqk = Pb[:, 0, QG:2 * QG]
        qf = Pb[:, 1, 0:QG]
        qr = Pb[:, 1, QG:2 * QG]
        kf = Pb[:, 2, 0:QG]
        kr = Pb[:, 2, QG:2 * QG]
        w1 = mtflat[:, 0:2 * E * HID].bitcast(F32).rearrange("p (e h) -> p e h", e=E)
        w2 = mtflat[:, 2 * E * HID:4 * E * HID].bitcast(F32).rearrange("p (e c d) -> p e c d", e=E, c=4)
        hT = Pb[:, :, :].rearrange("p a b -> p (a b)").rearrange("p (a c n) -> p a c n", a=2, c=4)
        lg = sb("lg", [P, TPG, E], F32)
        l1 = sb("l1", [P, TPG, E], F32)
        lm = sb("lm", [P, TPG], F32)
        oh = sb("oh", [P, TPG, E], F32)
        acc = attT[:, :].rearrange("p (t d) -> p t d", d=D)
        qm = attT[:, :].bitcast(BF16)[:, 0:2 * P].rearrange("p (a n) -> p a n", a=2)
        cs = att[:, :, :].rearrange("p t d -> p (t d)")

        Sp = ps("Sp", [P, 4, QG], F32)
        Po = ps("Po", [P, 2, QG], F32)
        X = ps("X", [P, 2, QG], F32)

        def pair(n):
            return X[:, :, :] if BANKS[n] == 2 else Sp[:, 2 * BANKS[n]:2 * BANKS[n] + 2, :]

        qd = [nc.dram_tensor(f"q_rows{a}", [D, SLOTS, S], BF16).ap() for a in range(2)]
        kd_ = [nc.dram_tensor(f"k_rows{a}", [D, SLOTS, S], BF16).ap() for a in range(2)]
        md = [nc.dram_tensor(f"shift_rows{a}", [3, H, S], BF16).ap() for a in range(2)]

        s_x = [sem(f"x_loaded{g}") for g in range(GROUPS)]
        s_w = sem("weights_loaded")
        s_moe_w = sem("expert_weights_loaded")
        s_const = sem("constants_ready")
        s_id0 = sem("identity_zeroed")
        s_id = sem("identity_ready")
        s_init = sem("vector_init_done")
        s_ones = sem("operands_filled")
        s_var = sem("variance_ready")
        s_pow = sem("rsqrt_guess_ready")
        s_xg = sem("normalised_tiles_ready")
        s_xt_ps = sem("tiles_transposed")
        s_xT = sem("xT_ready")
        s_q_ps = sem("q_projected")
        s_k_ps = sem("k_projected")
        s_v_ps = sem("v_projected")
        s_i_ps = sem("index_projected")
        s_qf = sem("q_float_ready")
        s_kf = sem("k_float_ready")
        s_qs = sem("q_parts_ready")
        s_ks = sem("k_parts_ready")
        s_va = sem("values_ready")
        s_iT = sem("index_rows_ready")
        s_sqq = sem("q_squares_ready")
        s_sqk = sem("k_squares_ready")
        s_nq_ps = sem("q_norms_summed")
        s_kn_ps = sem("k_norms_summed")
        s_kn = sem("k_norm_max_taken")
        s_kbd = sem("window_keys_ready")
        s_win_ps = sem("window_scores_ready")
        s_win = sem("window_max_taken")
        s_ngm = sem("shift_ready")
        s_m_ps = sem("shift_transposed")
        s_ms = sem("shift_parts_ready")
        s_kdg = sem("k_norm_diagonal_ready")
        s_kb_ps = sem("k_norm_spread")
        s_ok = sem("bound_checked")
        s_ok_ps = sem("bound_transposed")
        s_flag = sem("flag_ready")
        s_qd = sem("q_rows_stored")
        s_kd = sem("k_rows_stored")
        s_md = sem("shift_rows_stored")
        s_ka = sem("k_operand_loaded")
        s_qa = [sem(f"q_operand_loaded{i}") for i in range(PASSES)]
        s_qk = sem("scores_ready")
        s_exp = sem("weights_exp_done")
        s_pv = sem("weights_used")
        s_po = sem("outputs_copied")
        s_ot_ps = sem("outputs_transposed")
        s_att = sem("outputs_normalised")
        s_attT_ps = sem("att_transposed")
        s_attT = sem("attT_ready")
        s_wo_ps = sem("att_projected")
        s_res = sem("residual_added")
        s_idx_ps = sem("index_scores_ready")
        s_idx = sem("index_scores_copied")
        s_mq = sem("mask_ready")
        s_mt = [sem(f"mask_transposed{i}") for i in range(2)]
        s_ln2 = sem("moe_tiles_ready")
        s_g_ps = sem("gate_scores_ready")
        s_h_ps = sem("hidden_ready")
        s_h = sem("gelu_done")
        s_y_ps = sem("expert_output_ready")
        s_y = sem("expert_output_added")
        s_fin = sem("result_ready")
        s_out = sem("result_stored")
        s_chain = sem("vector_chain")
        s_vm = sem("weights_masked_by_vector")
        s_pm = sem("weights_masked_by_pool")
        s_keep = sem("key_block_masks_ready")
        s_cnt = sem("selection_counted")
        s_cok = sem("counts_checked")
        s_cok_ps = sem("counts_transposed")
        s_cflag = sem("count_flag_ready")

        class Careful:

            def __init__(self, n):
                self.idx_ps = sem(f"c{n}_index_scores_ready")
                self.idx = sem(f"c{n}_index_scores_copied")
                self.mq = sem(f"c{n}_mask_ready")
                self.mt = sem(f"c{n}_mask_transposed")
                self.q = sem(f"c{n}_head_q_ready")
                self.sc = sem(f"c{n}_scores_ready")
                self.add = sem(f"c{n}_scores_masked")
                self.red = sem(f"c{n}_chunk_max_taken")
                self.mx = sem(f"c{n}_head_max_taken")
                self.ngm = sem(f"c{n}_shift_ready")
                self.m_ps = sem(f"c{n}_shift_transposed")
                self.ms = sem(f"c{n}_shift_parts_ready")
                self.md = sem(f"c{n}_shift_rows_stored")
                self.chain = sem(f"c{n}_vector_chain")

        care = [Careful(n) for n in range(GROUPS + 1)]

        block = ctx.enter_context(nc.Block())

        @block.sync
        def _(sp):
            for g in range(GROUPS):
                sp.dma_start(x[:, g * TPG:(g + 1) * TPG, :],
                             in_["x"].rearrange("b (t p) d -> p (b t) d", p=P)[:, g * TPG:(g + 1) * TPG, :]
                             ).then_inc(s_x[g], 16)
            loads = [(w_q[:, 0, :], in_["wqT"]), (w_k[:, 0, :], in_["wkT"]), (w_v[:, 0, :], in_["wvT"]),
                     (w_o[:, 0, :], in_["woT"]), (w_i[:, 0, :], in_["wqiT"]), (w_i[:, 1, :], in_["wkiT"]),
                     (w_q[:, 1, :], in_["w_qkv"][:, 0:D]), (w_k[:, 1, :], in_["w_qkv"][:, D:2 * D]),
                     (w_v[:, 1, :], in_["w_qkv"][:, 2 * D:3 * D]), (w_o[:, 1, :], in_["w_proj"]),
                     (gw[:, :], in_["gate_w"]),
                     (bv[:, :], in_["bv"].partition_broadcast(P)), (bo[:, :], in_["bo"].partition_broadcast(P)),
                     (gb[:, :], in_["gate_b"].partition_broadcast(P))]
            for i, name in enumerate(["bq", "bk", "bqi", "bki", "ln1_w", "ln1_b", "ln2_w", "ln2_b"]):
                n = in_[name].shape[0]
                loads.append((colb[0:n, i:i + 1], in_[name].rearrange("(p a) -> p a", a=1)))
            for dst, src in loads:
                sp.dma_start(dst, src).then_inc(s_w, 16)
            assert len(loads) == WEIGHT_LOADS

            def store_parts(a):
                for part, slots, dram, done in ((Ks, K_PART, kd_[a], s_kd), (Qs, Q_PART, qd[a], s_qd)):
                    sp.wait_ge(s_ks if part is Ks else s_qs, GROUPS * (a + 1))
                    for slot in range(SLOTS):
                        src = part[:, slots[slot], :] if slots[slot] < 2 else Lo[:, int(part is Ks), :]
                        sp.dma_start(dram[:, slot, :], src).then_inc(done, 16)

            def load_k(a):
                sp.wait_ge(s_kd, 16 * SLOTS * (a + 1))
                if a:
                    sp.wait_ge(s_qk, GROUPS * GSTEPS)
                else:
                    sp.wait_ge(s_ones, 4)
                rows = kd_[a].rearrange("(j hx d) s n -> hx (d s) j n", hx=2, d=DH)
                for hx in range(2):
                    sp.dma_start(KA[64 * hx:64 * hx + KQ, :, :], rows[hx]).then_inc(s_ka, 16)

            def store_shifts(a):
                for g in range(GROUPS):
                    sp.wait_ge(s_ms, GROUPS * a + g + 1)
                    sp.dma_start(md[a].rearrange("s h n -> h s n")[:, :, g * QG:(g + 1) * QG], Ms
                                 ).then_inc(s_md, 16)

            def load_q(G, hh):
                a, g = divmod(G, GROUPS)
                if g == 0 and hh == 0:
                    sp.wait_ge(s_qd, 16 * SLOTS * (a + 1))
                    sp.wait_ge(s_md, 16 * GROUPS * (a + 1))
                if 2 * G + hh >= 2:
                    sp.wait_ge(s_qk, STEPS * (2 * G + hh - 1))
                cols = slice(g * QG, (g + 1) * QG)
                rows = qd[a].rearrange("(j hx d) s n -> hx (d s) j n", hx=2, d=DH)
                shifts = md[a].rearrange("s (j hx) n -> hx s j n", hx=2)
                js = slice(hh * PPP, (hh + 1) * PPP)
                half = QA[:, :, :].rearrange("p (j hx) n -> p hx j n", hx=2)
                for hx in range(2):
                    sp.dma_start(half[64 * hx:64 * hx + KQ, hx, js, :], rows[hx][:, js, cols]).then_inc(s_qa[hh], 16)
                    sp.dma_start(half[64 * hx + KQ:64 * hx + KROWS, hx, js, :], shifts[hx][:, js, cols]
                                 ).then_inc(s_qa[hh], 16)

            def transpose_mask(t):
                sp.wait_ge(s_cnt, t + 1)
                g, tt = divmod(t, TPG)
                if g >= 2 and tt == 0:
                    sp.wait_ge(s_qk, GSTEPS * (g - 1))
                    sp.wait_ge(s_vm, masked("dve", g - 2, GSTEPS))
                    sp.wait_ge(s_keep, (g - 1) * GSTEPS // PPP)
                sp.dma_start_transpose(MT[:, g % 2, :, tt * P:(tt + 1) * P], Mq[:, t % 2, :]
                                       ).then_inc(s_mt[t % 2], 16)

            def careful(a, groups, c):
                if a == 0:
                    g = groups[0]
                    for i in range(2):
                        sp.wait_ge(s_mt[i], 16 * 2 * (g + 1))
                    for tt in range(TPG):
                        sp.wait_ge(c.mq, tt + 1)
                        sp.dma_start_transpose(MT[:, g % 2, :, tt * P:(tt + 1) * P], Mq[:, tt % 2, :]
                                               ).then_inc(c.mt, 16)
                        sp.wait_ge(c.mt, 16 * (tt + 1))
                for i, g in enumerate(groups):
                    sp.wait_ge(c.ms, i + 1)
                    sp.dma_start(md[a].rearrange("s h n -> h s n")[:, :, g * QG:(g + 1) * QG], Ms
                                 ).then_inc(c.md, 16)
                    sp.wait_ge(c.md, 16 * (i + 1))

            store_parts(0)
            load_k(0)
            store_shifts(0)
            sp.wait_ge(s_win, TILES)
            for g in range(GROUPS):
                for t in range(TPG):
                    transpose_mask(g * TPG + t)
                sp.wait_ge(s_cflag, g + 1)
                fine = sp.value_load(fli[0:1, g:g + 1], min_val=0, max_val=1)
                with sp.If(fine == 0):
                    if g == 0:
                        sp.wait_ge(s_md, 16 * GROUPS)
                    careful(0, [g], care[g])
                load_q(g, 0)
                load_q(g, 1)
            store_parts(1)
            load_k(1)
            store_shifts(1)
            sp.wait_ge(s_flag, 2)
            fine = sp.value_load(fli[0:1, GROUPS:GROUPS + 1], min_val=0, max_val=1)
            with sp.If(fine == 0):
                sp.wait_ge(s_md, 16 * 2 * GROUPS)
                careful(1, list(range(GROUPS)), care[GROUPS])
            load_q(GROUPS, 0)
            load_q(GROUPS, 1)
            sp.wait_ge(s_win, 2 * TILES)
            for e in range(E):
                sp.dma_start(w1[:, e, :], in_["w1"][e]).then_inc(s_moe_w, 16)
                sp.dma_start(w2[:, e, :, :], in_["w2"][e].rearrange("(c p) d -> p c d", p=P)).then_inc(s_moe_w, 16)
            for G in range(GROUPS + 1, 2 * GROUPS):
                load_q(G, 0)
                load_q(G, 1)
            for g in range(GROUPS):
                sp.wait_ge(s_fin, g + 1)
                sp.dma_start(out.rearrange("b (t p) d -> p (b t) d", p=P)[:, g * TPG:(g + 1) * TPG, :],
                             x[:, g * TPG:(g + 1) * TPG, :]).then_inc(s_out, 16)
            sp.wait_ge(s_out, 16 * GROUPS)

        @block.gpsimd
        def _(pool):
            nc.gpsimd.memset(ident[:, :], 0.0).then_inc(s_id0, 1)
            nc.gpsimd.memset(identb[:, :], 0.0).then_inc(s_id0, 1)
            nc.gpsimd.memset(hmask[:, :], 1.0).then_inc(s_id0, 1)
            pool.wait_ge(s_id0, 3)
            for m in (ident, identb):
                nc.gpsimd.affine_select(out=m[:, :], in_=m[:, :], compare_op=ALU.not_equal, fill=1.0, base=0,
                                        pattern=[[-1, P]], channel_multiplier=1).then_inc(s_id, 1)
            nc.gpsimd.affine_select(out=hmask[:, :], in_=hmask[:, :], compare_op=ALU.is_ge, fill=0.0, base=0,
                                    pattern=[[-DH, H]], channel_multiplier=1).then_inc(s_id0, 1)
            pool.wait_ge(s_id0, 4)
            nc.gpsimd.affine_select(out=hmask[:, :], in_=hmask[:, :], compare_op=ALU.is_ge, fill=0.0, base=DH - 1,
                                    pattern=[[DH, H]], channel_multiplier=-1).then_inc(s_id, 1)
            nc.gpsimd.memset(mhalf[:, :], -0.5).then_inc(s_const, 1)
            nc.gpsimd.iota(tie[:, :].bitcast(I32), pattern=[[1, S]], base=1, channel_multiplier=0).then_inc(s_const, 1)
            nc.gpsimd.iota(rank[:, :].bitcast(I32), pattern=[[-1, E]], base=E, channel_multiplier=0
                           ).then_inc(s_const, 1)
            pool.wait_ge(s_const, 3)
            for n in range(4):
                pool.wait_ge(s_var, n + 1)
                nc.gpsimd.tensor_tensor(rs[:, :], ve[:, :], mhalf[:, :], ALU.pow).then_inc(s_pow, 1)
                if n == 0:
                    nc.gpsimd.memset(VA[:, :, :, :], 1.0).then_inc(s_ones, 1)
                    pool.wait_ge(s_ones, 1)
                    nc.gpsimd.memset(KA[32:64, :, :], 1.0).then_inc(s_ones, 1)
                    pool.wait_ge(s_ones, 2)
                    nc.gpsimd.memset(KA[96:128, :, :], 1.0).then_inc(s_ones, 1)
                    pool.wait_ge(s_ones, 3)
                    nc.gpsimd.memset(QA[:, :, :], 0.0).then_inc(s_ones, 1)
                    pool.wait_ge(s_ones, 4)
                    for g in range(GROUPS):
                        for s in range(GSTEPS):
                            if masker(g, s) == "pool":
                                n = GSTEPS * g + s
                                pool.wait_ge(s_exp, n + 1)
                                if s % PPP == 0:
                                    pool.wait_ge(s_keep, n // PPP + 1)
                                w = Pb[:, n % 4, :].rearrange("p (b n) -> p b n", b=2)
                                k = keep[:, n // PPP % KEYS_AHEAD, :].unsqueeze(1).to_broadcast([P, 2, QG])
                                nc.gpsimd.tensor_tensor(w, w, k, ALU.mult).then_inc(s_pm, 1)

        @block.scalar
        def _(act):
            def prologue(a):
                for g in range(GROUPS):
                    G = GROUPS * a + g
                    cols = slice(g * QG, (g + 1) * QG)
                    act.wait_ge(s_xt_ps, G + 1)
                    if a == 0:
                        nc.scalar.activation(xT[:, cols], X[:, 0, :], ACT.Copy).then_inc(s_xT, 1)
                    else:
                        nc.scalar.activation(xT[:, cols], X[:, 0, :], ACT.Identity, scale=colb[:, 4:5],
                                             bias=colb[:, 5:6]).then_inc(s_xT, 1)
                    act.wait_ge(s_qf, G + 1)
                    nc.scalar.activation(sqq, qf, ACT.Square).then_inc(s_sqq, 1)
                    act.wait_ge(s_kf, G + 1)
                    if G:
                        act.wait_ge(s_kn_ps, G)
                    nc.scalar.activation(sqk, Sp[:, 1, :], ACT.Square).then_inc(s_sqk, 1)
                    if a == 0:
                        act.wait_ge(s_i_ps, g + 1)
                        nc.scalar.activation(qiT[:, cols], Sp[0:IDX, 3, :], ACT.Identity, bias=colb[0:IDX, 2:3]
                                             ).then_inc(s_iT, 1)
                        nc.scalar.activation(kiT[:, cols], Po[0:IDX, 1, :], ACT.Identity, bias=colb[0:IDX, 3:4]
                                             ).then_inc(s_iT, 1)

            def count(t):
                act.wait_ge(s_mq, t + 1)
                m = Mq[:, t % 2, 0:ASSOC]
                nc.scalar.activation(m, m, ACT.Identity, accum_out=cnt[:, t:t + 1]).then_inc(s_cnt, 1)

            def attention(a):
                for G in range(GROUPS * a, GROUPS * (a + 1)):
                    for s in range(GSTEPS):
                        if a == 0 and G + 1 < GROUPS and count_at(s) is not None:
                            count((G + 1) * TPG + count_at(s))
                        n = GSTEPS * G + s
                        act.wait_ge(s_qk, n + 1)
                        if n >= 4:
                            act.wait_ge(s_pv, (n - 4) // 2 + 1)
                        nc.scalar.activation(Pb[:, n % 4, :], pair(n), ACT.Exp).then_inc(s_exp, 1)

            act.wait_ge(s_w, 16 * WEIGHT_LOADS)
            prologue(0)
            for t in range(TPG):
                count(t)
            attention(0)
            prologue(1)
            attention(1)
            for g in range(GROUPS):
                G = 2 * GROUPS + g
                cols = slice(g * QG, (g + 1) * QG)
                act.wait_ge(s_xt_ps, G + 1)
                nc.scalar.activation(xT[:, cols], X[:, 0, :], ACT.Identity, scale=colb[:, 6:7], bias=colb[:, 7:8]
                                     ).then_inc(s_xT, 1)
                for e in range(E):
                    i = g * E + e
                    if i >= 2:
                        act.wait_ge(s_y_ps, i - 1)
                    for c in range(4):
                        act.wait_ge(s_h_ps, 4 * i + c + 1)
                        nc.scalar.activation(hT[:, i % 2, c, :], Sp[:, c, :], ACT.Gelu_apprx_tanh).then_inc(s_h, 1)

        @block.tensor
        def _(pe):
            mm = nc.tensor.matmul

            def transpose_tiles(G):
                pe.wait_ge(s_xg, G + 1)
                if G:
                    pe.wait_ge(s_xT, G)
                for tt in range(TPG):
                    last = nc.tensor.transpose(X[:, 0, tt * P:(tt + 1) * P], att[:, tt, :], ident[:, :])
                last.then_inc(s_xt_ps, 1)
                pe.wait_ge(s_xT, G + 1)

            def prologue(a):
                if a:
                    pe.wait_ge(s_res, GROUPS)
                for g in range(GROUPS):
                    G = GROUPS * a + g
                    cols = slice(g * QG, (g + 1) * QG)
                    transpose_tiles(G)
                    if G:
                        pe.wait_ge(s_qf, G)
                    mm(Sp[:, 0, :], w_q[:, a, :], xT[:, cols], start=True, stop=True).then_inc(s_q_ps, 1)
                    if G:
                        pe.wait_ge(s_kf, G)
                        pe.wait_ge(s_sqk, G)
                    mm(Sp[:, 1, :], w_k[:, a, :], xT[:, cols], start=True, stop=True).then_inc(s_k_ps, 1)
                    if G:
                        pe.wait_ge(s_va, G)
                    for tt in range(TPG):
                        last = mm(Sp[:, 2, tt * P:(tt + 1) * P], xT[:, g * QG + tt * P:g * QG + (tt + 1) * P],
                                  w_v[:, a, :], start=True, stop=True)
                    last.then_inc(s_v_ps, 1)
                    if a == 0:
                        if g:
                            pe.wait_ge(s_iT, 2 * g)
                        mm(Sp[0:IDX, 3, :], w_i[:, 0, :], xT[:, cols], start=True, stop=True)
                        mm(Po[0:IDX, 1, :], w_i[:, 1, :], xT[:, cols], start=True, stop=True).then_inc(s_i_ps, 1)
                    pe.wait_ge(s_sqq, G + 1)
                    for tt in range(TPG):
                        t = g * TPG + tt
                        last = mm(Po[:, 0, t * H:(t + 1) * H], sqq[:, tt * P:(tt + 1) * P], hmask[:, :],
                                  start=True, stop=True, skip_group_check=True)
                    last.then_inc(s_nq_ps, 1)
                    pe.wait_ge(s_sqk, G + 1)
                    if G:
                        pe.wait_ge(s_kn, G)
                    mm(X[0:H, 1, :], hmask[:, :], sqk, start=True, stop=True).then_inc(s_kn_ps, 1)
                pe.wait_ge(s_kdg, a + 1)
                if a == 0:
                    pe.wait_ge(s_iT, 2 * GROUPS)
                mm(Po[:, 1, 0:H], ones[:, :], kd[:, 2:2 + H], start=True, stop=True).then_inc(s_kb_ps, 1)
                pe.wait_ge(s_kbd, a + 1)
                pe.wait_ge(s_va, GROUPS * (a + 1))
                pe.wait_ge(s_sqk, GROUPS * (a + 1))
                for t in range(TILES):
                    n = TILES * a + t
                    if t >= 2:
                        pe.wait_ge(s_win, n - 1)
                    for i, (qp, kp) in enumerate(((0, 0), (0, 1), (1, 0))):
                        for hf in range(2):
                            last = mm(Sp[:, 2 * (t % 2) + hf, :], Qs[:, qp, t * P:(t + 1) * P],
                                      Kbd[:, kp, hf * 8:(hf + 1) * 8, :], start=(i == 0), stop=(i == 2),
                                      skip_group_check=True)
                    last.then_inc(s_win_ps, 1)
                pe.wait_ge(s_ngm, a + 1)
                pe.wait_ge(s_kn, GROUPS * (a + 1))
                for g in range(GROUPS):
                    G = GROUPS * a + g
                    if g >= 1:
                        pe.wait_ge(s_ms, G)
                    for tt in range(TPG):
                        last = nc.tensor.transpose(X[0:H, 1, tt * P:(tt + 1) * P], ngm[:, g * TPG + tt, :],
                                                   ident[:, :])
                    last.then_inc(s_m_ps, 1)
                pe.wait_ge(s_ok, a + 1)
                pe.wait_ge(s_ms, GROUPS * (a + 1))
                nc.tensor.transpose(X[0:1, 1, 0:P], fl[:, 0:1], ident[:, :]).then_inc(s_ok_ps, 1)
                pe.wait_ge(s_flag, a + 1)

            def index_chunk(t, c):
                i = 4 * t + c
                w = min(QG, ASSOC - c * QG)
                if i >= 2:
                    pe.wait_ge(s_idx, i - 1)
                mm(X[:, c % 2, 0:w], qiT[:, t * P:(t + 1) * P], kiT[:, c * QG:c * QG + w], start=True, stop=True
                   ).then_inc(s_idx_ps, 1)

            def check_counts(g):
                pe.wait_ge(s_cok, g + 1)
                nc.tensor.transpose(X[0:1, 1, 0:P], fl[:, 2:3], ident[:, :]).then_inc(s_cok_ps, 1)

            def exact_max(i, t, c):
                with pe.Fori(0, H) as h:
                    pe.wait_ge(c.q, h + (i * H + 1))
                    for ch in range(4):
                        if ch >= 2:
                            pe.wait_ge(c.red, h * 4 + (4 * i * H + ch - 1))
                        for n, (qp, kp) in enumerate(((0, 0), (0, 1), (1, 0))):
                            last = mm(X[:, ch % 2, :], qm[:, qp, :], Ks[:, kp, ch * QG:(ch + 1) * QG],
                                      start=(n == 0), stop=(n == 2), skip_group_check=True)
                        last.then_inc(c.sc, 1)

            def careful(a, groups, c):
                for i, g in enumerate(groups):
                    for tt in range(TPG):
                        t = g * TPG + tt
                        if a == 0:
                            for ch in range(COPIES):
                                w = min(QG, ASSOC - ch * QG)
                                if ch >= 2:
                                    pe.wait_ge(c.idx, COPIES * tt + ch - 1)
                                elif tt:
                                    pe.wait_ge(c.mx, H * tt)
                                mm(X[:, ch % 2, 0:w], qiT[:, t * P:(t + 1) * P], kiT[:, ch * QG:ch * QG + w],
                                   start=True, stop=True).then_inc(c.idx_ps, 1)
                            pe.wait_ge(c.idx, COPIES * (tt + 1))
                        exact_max(TPG * i + tt, t, c)
                    pe.wait_ge(c.ngm, i + 1)
                    if i:
                        pe.wait_ge(c.ms, i)
                    for tt in range(TPG):
                        last = nc.tensor.transpose(X[0:H, 1, tt * P:(tt + 1) * P], ngm[:, g * TPG + tt, :],
                                                   ident[:, :])
                    last.then_inc(c.m_ps, 1)
                pe.wait_ge(c.ms, len(groups))
                if a == 0:
                    pe.wait_ge(c.mt, 16 * TPG)

            def care_for(g):
                pe.wait_ge(s_cflag, g + 1)
                fine = pe.value_load(fli[0:1, g:g + 1], min_val=0, max_val=1)
                with pe.If(fine == 0):
                    careful(0, [g], care[g])

            def scores(G, s, guarded):
                a = G // GROUPS
                n = GSTEPS * G + s
                hh, r = divmod(s, STEPS)
                kb, jj = divmod(r, PPP)
                j = hh * PPP + jj
                masks = a == 0 and (guarded or masker(G, s) == "pe")
                if r == 0:
                    pe.wait_ge(s_qa[hh], 64 * (G + 1))
                if LAST_IN_BANKS[n] is not None:
                    pe.wait_ge(s_exp, LAST_IN_BANKS[n] + 1)
                for hx in range(2):
                    last = mm(pair(n)[:, hx, :], KA[:, j, kb * P:(kb + 1) * P], QA[:, 2 * j + hx, :],
                              start=True, stop=not masks, skip_group_check=True)
                if masks:
                    for hx in range(2):
                        last = mm(pair(n)[:, hx, :], identb[:, :], MT[:, G % 2, kb, :],
                                  start=False, stop=True, skip_group_check=True)
                last.then_inc(s_qk, 1)

            def weighted_values(G, s):
                n = GSTEPS * G + s
                hh, r = divmod(s, STEPS)
                kb, jj = divmod(r, PPP)
                q = jj // 2
                pe.wait_ge(s_exp, n + 1)
                if G < GROUPS:
                    pe.wait_ge(s_pm, masked("pool", G, s + 1))
                    if masker(G, s) == "dve":
                        pe.wait_ge(s_vm, masked("dve", G, s + 1))
                if kb == 0 and 2 * G + hh >= 1:
                    pe.wait_ge(s_po, 2 * G + hh)
                for i in range(4):
                    h = hh * 8 + q * 4 + i
                    last = mm(Po[32 * i:32 * i + VW, q, :], VA[:, kb, h, :],
                              Pb[:, (n - 1 + i // 2) % 4, (i % 2) * QG:(i % 2 + 1) * QG],
                              start=(kb == 0), stop=(kb == TILES - 1), skip_group_check=True)
                last.then_inc(s_pv, 1)

            def tail_outputs(G):
                pe.wait_ge(s_po, 2 * (G + 1))
                for tt in range(TPG):
                    if tt >= 2:
                        pe.wait_ge(s_att, TPG * G + tt - 1)
                    for i in range(4):
                        last = nc.tensor.transpose(X[:, tt % 2, i * P:(i + 1) * P],
                                                   OT[:, i // 2, i % 2, tt * P:(tt + 1) * P], ident[:, :])
                    last.then_inc(s_ot_ps, 1)

            def tail_transpose(G):
                pe.wait_ge(s_att, TPG * (G + 1))
                for tt in range(TPG):
                    last = nc.tensor.transpose(X[:, 0, tt * P:(tt + 1) * P], att[:, tt, :], ident[:, :])
                last.then_inc(s_attT_ps, 1)

            def tail_project(G):
                pe.wait_ge(s_attT, G + 1)
                for tt in range(TPG):
                    last = mm(X[:, 1, tt * P:(tt + 1) * P], attT[:, tt * P:(tt + 1) * P], w_o[:, G // GROUPS, :],
                              start=True, stop=True)
                last.then_inc(s_wo_ps, 1)

            def group(G, guarded):
                a, g = divmod(G, GROUPS)
                if a == 0:
                    for i in range(2):
                        pe.wait_ge(s_mt[i], 16 * 2 * (g + 1))
                for s in range(GSTEPS):
                    scores(G, s, guarded)
                    if s % 2 and s > 1:
                        weighted_values(G, s - 2)
                    if g:
                        if s == 7:
                            if a == 0:
                                pe.wait_ge(s_idx, 4 * TPG * min(g + 1, GROUPS))
                            tail_outputs(G - 1)
                        if s == 15:
                            tail_transpose(G - 1)
                        if s == 19:
                            tail_project(G - 1)
                        if s == 23:
                            pe.wait_ge(s_res, G)
                    if a == 0 and g + 1 < GROUPS:
                        if s == FIRST_PIECE and g:
                            pe.wait_ge(s_res, G)
                        if piece_at(s) and piece_at(s)[1] < COPIES:
                            index_chunk((g + 1) * TPG + piece_at(s)[0], piece_at(s)[1])
                        if s == CHECK_STEP + 2:
                            check_counts(g + 1)
                        if s == CAREFUL_STEP:
                            care_for(g + 1)
                weighted_values(G, GSTEPS - 1)

            def attention(a):
                pe.wait_ge(s_ka, 32 * (a + 1))
                for G in range(GROUPS * a, GROUPS * (a + 1)):
                    if a == 0:
                        fine = pe.value_load(fli[0:1, G:G + 1], min_val=0, max_val=1)
                        with pe.If(fine == 0):
                            group(G, True)
                        with pe.Else():
                            group(G, False)
                    else:
                        group(G, False)
                G = GROUPS * (a + 1) - 1
                tail_outputs(G)
                tail_transpose(G)
                tail_project(G)

            pe.wait_ge(s_id, 3)
            pe.wait_ge(s_w, 16 * WEIGHT_LOADS)
            pe.wait_ge(s_init, 1)
            prologue(0)
            for t in range(TPG):
                for c in range(4):
                    index_chunk(t, c)
            pe.wait_ge(s_idx, 4 * TPG)
            check_counts(0)
            care_for(0)
            attention(0)
            prologue(1)
            fine = pe.value_load(fli[0:1, GROUPS:GROUPS + 1], min_val=0, max_val=1)
            with pe.If(fine == 0):
                careful(1, list(range(GROUPS)), care[GROUPS])
            attention(1)
            pe.wait_ge(s_res, 2 * GROUPS)
            pe.wait_ge(s_moe_w, 32 * E)
            for g in range(GROUPS):
                cols = slice(g * QG, (g + 1) * QG)
                transpose_tiles(2 * GROUPS + g)
                if g:
                    pe.wait_ge(s_fin, g)
                for tt in range(TPG):
                    last = mm(X[:, 1, tt * E:(tt + 1) * E], xT[:, g * QG + tt * P:g * QG + (tt + 1) * P], gw[:, :],
                              start=True, stop=True)
                last.then_inc(s_g_ps, 1)

                def hidden(e):
                    for c in range(4):
                        i = 4 * (g * E + e) + c
                        if i >= 4:
                            pe.wait_ge(s_h, i - 3)
                        mm(Sp[:, c, :], w1[:, e, c * P:(c + 1) * P], xT[:, cols], start=True, stop=True
                           ).then_inc(s_h_ps, 1)

                def output(e):
                    i = g * E + e
                    pe.wait_ge(s_h, 4 * (i + 1))
                    if i >= 2:
                        pe.wait_ge(s_y, i - 1)
                    for tt in range(TPG):
                        for c in range(4):
                            last = mm(Po[:, i % 2, tt * P:(tt + 1) * P], hT[:, i % 2, c, tt * P:(tt + 1) * P],
                                      w2[:, e, c, :], start=(c == 0), stop=(c == 3), skip_group_check=True)
                    last.then_inc(s_y_ps, 1)

                hidden(0)
                for e in range(E):
                    if e + 1 < E:
                        hidden(e + 1)
                    output(e)

        @block.vector
        def _(dve):
            v = nc.vector
            def chain(done):
                count = [0]

                def link(ins):
                    count[0] += 1
                    ins.then_inc(done, 1)
                    dve.wait_ge(done, count[0])
                return link

            link = chain(s_chain)

            def statistics(src, n):
                for t in range(TILES):
                    if n == 0 and t % TPG == 0:
                        dve.wait_ge(s_x[t // TPG], 16)
                    last = v.bn_stats(st[:, t, :], src[:, t, :])
                link(last)
                for t in range(TILES):
                    last = v.bn_aggr(mv[:, t, :], st[:, t, :])
                link(last)
                v.tensor_scalar(ve[:, :], mv[:, :, 1], EPS, None, ALU.add).then_inc(s_var, 1)
                dve.wait_ge(s_var, n + 1)
                dve.wait_ge(s_pow, n + 1)
                link(v.tensor_tensor(rt[:, :], rs[:, :], rs[:, :], ALU.mult))
                link(v.tensor_tensor(rt[:, :], rt[:, :], ve[:, :], ALU.mult))
                link(v.tensor_scalar(rt[:, :], rt[:, :], -0.5, 1.5, ALU.mult, ALU.add))
                link(v.tensor_tensor(rs[:, :], rs[:, :], rt[:, :], ALU.mult))

            def normalise(dst, src, t):
                return v.tensor_scalar(dst, src[:, t, :], mv[:, t, 0:1], rs[:, t:t + 1], ALU.subtract, ALU.mult)

            def tiles_for_transpose(src, G):
                if G:
                    dve.wait_ge(s_xt_ps, G)
                for tt in range(TPG):
                    last = normalise(att[:, tt, :], src, (G % GROUPS) * TPG + tt)
                last.then_inc(s_xg, 1)

            def split(full, rest, high, middle, low, link=link):
                link(v.tensor_copy(high, full))
                link(v.tensor_tensor(rest, full, high, ALU.subtract))
                link(v.tensor_copy(middle, rest))
                return v.tensor_tensor(low, rest, middle, ALU.subtract)

            def prologue(a, src):
                if a:
                    dve.wait_ge(s_attT_ps, GROUPS)
                    dve.wait_ge(s_qd, 16 * SLOTS)
                    dve.wait_ge(s_kd, 16 * SLOTS)
                    dve.wait_ge(s_mt[0], 16 * TILES // 2)
                    dve.wait_ge(s_mt[1], 16 * TILES // 2)
                tiles_for_transpose(src, GROUPS * a)
                for g in range(GROUPS):
                    G = GROUPS * a + g
                    cols = slice(g * QG, (g + 1) * QG)
                    if g + 1 < GROUPS:
                        tiles_for_transpose(src, G + 1)
                    dve.wait_ge(s_q_ps, G + 1)
                    if G:
                        dve.wait_ge(s_sqq, G)
                    if a == 0:
                        v.tensor_scalar(qf, Sp[:, 0, :], colb[:, 0:1], SCALE, ALU.add, ALU.mult).then_inc(s_qf, 1)
                    else:
                        v.tensor_scalar(qf, Sp[:, 0, :], SCALE, None, ALU.mult).then_inc(s_qf, 1)
                    dve.wait_ge(s_k_ps, G + 1)
                    if a == 0:
                        v.tensor_scalar(kf, Sp[:, 1, :], colb[:, 1:2], None, ALU.add).then_inc(s_kf, 1)
                    else:
                        v.tensor_copy(kf, Sp[:, 1, :]).then_inc(s_kf, 1)
                    dve.wait_ge(s_qf, G + 1)
                    split(qf, qr, Qs[:, 0, cols], Qs[:, 1, cols], Lo[:, 0, cols]).then_inc(s_qs, 1)
                    dve.wait_ge(s_kf, G + 1)
                    split(kf, kr, Ks[:, 0, cols], Ks[:, 1, cols], Lo[:, 1, cols]).then_inc(s_ks, 1)
                    dve.wait_ge(s_v_ps, G + 1)
                    dve.wait_ge(s_ones, 1)
                    vdst = VA[:, g * TPG:(g + 1) * TPG, :, 0:DH]
                    vsrc = Sp[:, 2, :].rearrange("p (t h d) -> p t h d", t=TPG, h=H)
                    if a == 0:
                        for tt in range(TPG):
                            last = v.tensor_tensor(vdst[:, tt], vsrc[:, tt],
                                                   bv[:, :].rearrange("p (h d) -> p h d", h=H), ALU.add)
                    else:
                        last = v.tensor_copy(vdst, vsrc)
                    last.then_inc(s_va, 1)
                    dve.wait_ge(s_kn_ps, G + 1)
                    v.tensor_reduce(kn[:, g:g + 1], X[0:H, 1, :], AX_X, ALU.max).then_inc(s_kn, 1)
                dve.wait_ge(s_ks, GROUPS * (a + 1))
                for part in range(2):
                    last = v.tensor_tensor(Kbd[:, part], Ks[:, part, ASSOC:S].unsqueeze(1).to_broadcast([P, H, WORK]),
                                           hmask[:, :].unsqueeze(2).to_broadcast([P, H, WORK]), ALU.mult)
                last.then_inc(s_kbd, 1)
                dve.wait_ge(s_kn, GROUPS * (a + 1))
                link(v.tensor_reduce(kd[:, 0:1], kn[:, :], AX_X, ALU.max))
                v.tensor_scalar(kd[:, 2:2 + H], ident[0:H, 0:H], kd[:, 0:1], None, ALU.mult).then_inc(s_kdg, 1)
                for t in range(TILES):
                    n = TILES * a + t
                    dve.wait_ge(s_win_ps, n + 1)
                    v.tensor_reduce(mx[:, t, :],
                                    Sp[:, 2 * (t % 2):2 * (t % 2) + 2, :].rearrange("p b (h n) -> p (b h) n", n=WORK),
                                    AX_X, ALU.max).then_inc(s_win, 1)
                dve.wait_ge(s_win, TILES * (a + 1))
                v.tensor_scalar(ngm[:, :, :], mx[:, :, :], -1.0, -SHIFT[a], ALU.mult, ALU.add).then_inc(s_ngm, 1)
                dve.wait_ge(s_nq_ps, GROUPS * (a + 1))
                link(v.tensor_copy(nq[:, :, :], Po[:, 0, 0:TILES * H].rearrange("p (t h) -> p t h", h=H)))
                dve.wait_ge(s_kb_ps, a + 1)
                link(v.tensor_tensor(nq[:, :, :], nq[:, :, :],
                                     Po[:, 1, 0:H].unsqueeze(1).to_broadcast([P, TILES, H]), ALU.mult))
                if a == 0:
                    link(v.tensor_scalar(ok[:, :, :], nq[:, :, :], 4.0, LIMIT[0] ** 2, ALU.mult, ALU.is_le))
                else:
                    link(v.tensor_scalar(mx[:, :, :], mx[:, :, :], LIMIT[1], None, ALU.add))
                    link(v.tensor_scalar(ok[:, :, :], mx[:, :, :], 0.0, None, ALU.max))
                    link(v.tensor_tensor(mx[:, :, :], ok[:, :, :], mx[:, :, :], ALU.mult))
                    link(v.tensor_tensor(ok[:, :, :], nq[:, :, :], mx[:, :, :], ALU.is_le))
                v.tensor_reduce(fl[:, 0:1], ok[:, :, :].rearrange("p t h -> p (t h)"), AX_X, ALU.min
                                ).then_inc(s_ok, 1)
                for g in range(GROUPS):
                    G = GROUPS * a + g
                    dve.wait_ge(s_m_ps, G + 1)
                    if G:
                        dve.wait_ge(s_md, 16 * G)
                    link(v.tensor_copy(msc[:, 0, :], X[0:H, 1, :]))
                    split(msc[:, 0, :], msc[:, 1, :], Ms[:, 0, :], Ms[:, 1, :], Ms[:, 2, :]).then_inc(s_ms, 1)
                dve.wait_ge(s_ok_ps, a + 1)
                link(v.tensor_reduce(fl[0:1, 1:2], X[0:1, 1, 0:P], AX_X, ALU.min))
                v.tensor_copy(fli[0:1, GROUPS:GROUPS + 1], fl[0:1, 1:2]).then_inc(s_flag, 1)
                dve.wait_ge(s_flag, a + 1)

            def copy_index_scores(k):
                n = min(QG, ASSOC - k * QG)
                return v.scalar_tensor_tensor(out=sw[:, k * QG:k * QG + n], in0=X[:, k % 2, 0:n], scalar=0.0,
                                              in1=tie[:, k * QG:k * QG + n], op0=ALU.max, op1=ALU.add)

            def write_mask(t, threshold):
                return v.tensor_scalar(Mq[:, t % 2, 0:ASSOC], sw[:, :], threshold, -MASK, ALU.is_le, ALU.mult)

            def select(t, k):
                if k < COPIES:
                    i = COPIES * t + k
                    dve.wait_ge(s_idx_ps, i + 1)
                    if k == 0 and t:
                        dve.wait_ge(s_mq, t)
                    copy_index_scores(k).then_inc(s_idx, 1)
                    if k == COPIES - 1:
                        dve.wait_ge(s_idx, i + 1)
                elif k < COPIES + STRIPES // 8:
                    for i in range(8 * (k - COPIES), 8 * (k - COPIES) + 8):
                        last = v.max(cand[:, 8 * i:8 * i + 8], sw[:, i:ASSOC:STRIPES])
                    if k == COPIES + STRIPES // 8 - 1:
                        link(last)
                elif k < PIECES - 2:
                    link(v.max(top8[:, :], cand[:, :]))
                    link(v.match_replace(cand[:, :], top8[:, :], cand[:, :], TAKEN))
                elif k == PIECES - 2:
                    link(v.max(top8[:, :], cand[:, :]))
                    link(v.match_replace(sw[:, :], top8[:, :], sw[:, :], KEPT))
                else:
                    if t >= 2:
                        dve.wait_ge(s_mt[t % 2], 16 * (t // 2))
                    write_mask(t, top8[:, 7:8]).then_inc(s_mq, 1)

            def check_counts(g):
                dve.wait_ge(s_cnt, TPG * (g + 1))
                link(v.tensor_scalar(cm[:, :], cnt[:, g * TPG:(g + 1) * TPG], -MASK * (ASSOC - TOPK), None,
                                     ALU.is_equal))
                v.tensor_reduce(fl[:, 2:3], cm[:, :], AX_X, ALU.min).then_inc(s_cok, 1)

            def flag_group(g):
                dve.wait_ge(s_cok_ps, g + 1)
                link(v.tensor_reduce(fl[0:1, 3:4], X[0:1, 1, 0:P], AX_X, ALU.min))
                v.tensor_tensor(fli[0:1, g:g + 1], fl[0:1, 3:4], fl[0:1, 1:2], ALU.min).then_inc(s_cflag, 1)

            def care_for(g):
                dve.wait_ge(s_cflag, g + 1)
                fine = dve.value_load(fli[0:1, g:g + 1], min_val=0, max_val=1)
                with dve.If(fine == 0):
                    careful(0, [g], care[g])

            def exact_max(a, i, t, c):
                with dve.Fori(0, H) as h:
                    v.tensor_scalar(qm, Qs[:, :, t * P:(t + 1) * P], hmask[:, bass.ds(h, 1)], None, ALU.mult
                                    ).then_inc(c.q, 1)
                    for ch in range(4):
                        dve.wait_ge(c.sc, h * 4 + (4 * i * H + ch + 1))
                        if a == 0:
                            v.tensor_tensor(cs, X[:, ch % 2, :], Mq[:, t % 2, ch * QG:(ch + 1) * QG], ALU.add
                                            ).then_inc(c.add, 1)
                            dve.wait_ge(c.add, h * 4 + (4 * i * H + ch + 1))
                            v.tensor_reduce(cm[:, ch:ch + 1], cs, AX_X, ALU.max).then_inc(c.red, 1)
                        else:
                            v.tensor_reduce(cm[:, ch:ch + 1], X[:, ch % 2, :], AX_X, ALU.max).then_inc(c.red, 1)
                        dve.wait_ge(c.red, h * 4 + (4 * i * H + ch + 1))
                    v.tensor_reduce(mx[:, t, bass.ds(h, 1)], cm[:, :], AX_X, ALU.max).then_inc(c.mx, 1)
                    dve.wait_ge(c.mx, h + (i * H + 1))

            def careful(a, groups, c):
                follow = chain(c.chain)
                dve.wait_ge(s_md, 16 * GROUPS * (a + 1))
                for i, g in enumerate(groups):
                    for tt in range(TPG):
                        t = g * TPG + tt
                        if a == 0:
                            for k in range(COPIES):
                                dve.wait_ge(c.idx_ps, COPIES * tt + k + 1)
                                copy_index_scores(k).then_inc(c.idx, 1)
                            dve.wait_ge(c.idx, COPIES * (tt + 1))
                            for _ in range(ROUNDS):
                                follow(v.max(top8[:, :], sw[:, :]))
                                follow(v.match_replace(sw[:, :], top8[:, :], sw[:, :], TAKEN))
                            for buf in range(2):
                                dve.wait_ge(s_mt[buf], 16 * 2 * (g + 1))
                            if tt >= 2:
                                dve.wait_ge(c.mt, 16 * (tt - 1))
                            follow(v.tensor_scalar(Mq[:, tt % 2, 0:ASSOC], sw[:, :], TAKEN, -MASK, ALU.is_gt,
                                                   ALU.mult))
                            v.tensor_copy(cm[:, 0:1], cm[:, 0:1]).then_inc(c.mq, 1)
                            dve.wait_ge(c.mq, tt + 1)
                        exact_max(a, TPG * i + tt, t, c)
                    part = slice(g * TPG, (g + 1) * TPG)
                    v.tensor_scalar(ngm[:, part, :], mx[:, part, :], -1.0, -SHIFT[a], ALU.mult, ALU.add
                                    ).then_inc(c.ngm, 1)
                    dve.wait_ge(c.m_ps, i + 1)
                    if i:
                        dve.wait_ge(c.md, 16 * i)
                    follow(v.tensor_copy(msc[:, 0, :], X[0:H, 1, :]))
                    split(msc[:, 0, :], msc[:, 1, :], Ms[:, 0, :], Ms[:, 1, :], Ms[:, 2, :], follow
                          ).then_inc(c.ms, 1)
                if a == 0:
                    dve.wait_ge(c.mt, 16 * TPG)
                dve.wait_ge(c.md, 16 * len(groups))

            def block_masks(G, s):
                i = (GSTEPS * G + s) // PPP
                if i >= KEYS_AHEAD:
                    dve.wait_ge(s_pm, MASKED_BEFORE["pool"][(i - KEYS_AHEAD + 1) * PPP])
                v.tensor_scalar(keep[:, i % KEYS_AHEAD, :], MT[:, G % 2, s % STEPS // PPP, :], 0.0, None, ALU.is_ge
                                ).then_inc(s_keep, 1)

            def mask_weights(G, s):
                n = GSTEPS * G + s
                kb = s % STEPS // PPP
                w = Pb[:, n % 4, :].rearrange("p (b n) -> p b n", b=2)
                dve.wait_ge(s_exp, n + 1)
                v.scalar_tensor_tensor(out=w, in0=MT[:, G % 2, kb, :].unsqueeze(1).to_broadcast([P, 2, QG]),
                                       scalar=MASK, in1=w, op0=ALU.add, op1=ALU.min).then_inc(s_vm, 1)

            def copy_outputs(G, hh):
                dve.wait_ge(s_pv, (GSTEPS * G + STEPS * (hh + 1)) // 2)
                if G and hh == 0:
                    dve.wait_ge(s_ot_ps, TPG * G)
                v.tensor_copy(OT[:, hh, :, :], Po[:, :, :]).then_inc(s_po, 1)

            def tail_normalise(G):
                for tt in range(TPG):
                    n = TPG * G + tt
                    dve.wait_ge(s_ot_ps, n + 1)
                    o = X[:, tt % 2, :].rearrange("p (h c) -> p h c", h=H)
                    link(v.reciprocal(rec[:, tt % 2, :], o[:, :, DH]))
                    v.tensor_tensor(att[:, tt, :].rearrange("p (h d) -> p h d", h=H), o[:, :, 0:DH],
                                    rec[:, tt % 2, :].unsqueeze(2).to_broadcast([P, H, DH]), ALU.mult
                                    ).then_inc(s_att, 1)

            def tail_copy(G):
                dve.wait_ge(s_attT_ps, G + 1)
                v.tensor_copy(attT[:, :], X[:, 0, :]).then_inc(s_attT, 1)

            def tail_residual(G):
                a, g = divmod(G, GROUPS)
                dve.wait_ge(s_wo_ps, G + 1)
                res = (x if a == 0 else y)[:, g * TPG:(g + 1) * TPG, :]
                o = X[:, 1, :].rearrange("p (t d) -> p t d", d=D)
                if a == 0:
                    link(v.tensor_tensor(acc[:, :, :], o, bo[:, :].unsqueeze(1).to_broadcast([P, TPG, D]), ALU.add))
                    v.tensor_tensor(res, res, acc[:, :, :], ALU.add).then_inc(s_res, 1)
                else:
                    v.tensor_tensor(res, res, o, ALU.add).then_inc(s_res, 1)

            def attention(a):
                for G in range(GROUPS * a, GROUPS * (a + 1)):
                    g = G % GROUPS
                    for i in range(2 if a == 0 else 0):
                        dve.wait_ge(s_mt[i], 16 * 2 * (g + 1))
                    for s in range(GSTEPS):
                        if a == 0 and s % PPP == 0:
                            if s == 0:
                                block_masks(G, 0)
                            if s + PPP < GSTEPS:
                                block_masks(G, s + PPP)
                        if a == 0 and masker(g, s) == "dve":
                            mask_weights(G, s)
                        if g:
                            if s == 7:
                                tail_normalise(G - 1)
                            if s == 15:
                                tail_copy(G - 1)
                            if s == 21:
                                tail_residual(G - 1)
                        if a == 0 and g + 1 < GROUPS:
                            if piece_at(s):
                                select((g + 1) * TPG + piece_at(s)[0], piece_at(s)[1])
                            if s == CHECK_STEP:
                                check_counts(g + 1)
                            if s == CHECK_STEP + 4:
                                flag_group(g + 1)
                            if s == CAREFUL_STEP:
                                care_for(g + 1)
                        if s == STEPS + 1:
                            copy_outputs(G, 0)
                    copy_outputs(G, 1)
                tail_normalise(G)
                tail_copy(G)
                tail_residual(G)

            v.memset(ones[:, :], 1.0)
            v.memset(Po[:, :, :], 0.0).then_inc(s_init, 1)
            dve.wait_ge(s_init, 1)
            statistics(x, 0)
            dve.wait_ge(s_const, 3)
            v.tensor_scalar(tie[:, :], tie[:, :].bitcast(I32), -TIE, None, ALU.mult)
            link(v.tensor_scalar(rank[:, :], rank[:, :].bitcast(I32), 1.0, None, ALU.mult))
            dve.wait_ge(s_w, 16 * WEIGHT_LOADS)
            dve.wait_ge(s_id, 3)
            prologue(0, x)
            dve.wait_ge(s_qd, 16 * SLOTS)
            dve.wait_ge(s_kd, 16 * SLOTS)
            link(v.memset(Mq[:, :, ASSOC:S], 0.0))
            dve.wait_ge(s_md, 16 * GROUPS)
            for t in range(TPG):
                for k in range(PIECES):
                    select(t, k)
            check_counts(0)
            flag_group(0)
            care_for(0)
            attention(0)
            dve.wait_ge(s_res, GROUPS)
            statistics(x, 1)
            for t in range(TILES):
                last = normalise(y[:, t, :], x, t)
            link(last)
            statistics(y, 2)
            prologue(1, y)
            fine = dve.value_load(fli[0:1, GROUPS:GROUPS + 1], min_val=0, max_val=1)
            with dve.If(fine == 0):
                careful(1, list(range(GROUPS)), care[GROUPS])
            attention(1)
            dve.wait_ge(s_res, 2 * GROUPS)
            statistics(y, 3)
            dve.wait_ge(s_attT_ps, 2 * GROUPS)
            tiles_for_transpose(y, 2 * GROUPS)
            for g in range(GROUPS):
                G = 2 * GROUPS + g
                if g + 1 < GROUPS:
                    tiles_for_transpose(y, G + 1)
                dve.wait_ge(s_g_ps, g + 1)
                link(v.tensor_tensor(lg[:, :, :], X[:, 1, 0:TPG * E].rearrange("p (t e) -> p t e", e=E),
                                     gb[:, :].unsqueeze(1).to_broadcast([P, TPG, E]), ALU.add))
                link(v.tensor_reduce(lm[:, :], lg[:, :, :], AX_X, ALU.max))
                link(v.tensor_tensor(l1[:, :, :], lg[:, :, :], lm[:, :].unsqueeze(2).to_broadcast([P, TPG, E]),
                                     ALU.is_equal))
                link(v.tensor_tensor(l1[:, :, :], l1[:, :, :], rank[:, :].unsqueeze(1).to_broadcast([P, TPG, E]),
                                     ALU.mult))
                link(v.tensor_reduce(lm[:, :], l1[:, :, :], AX_X, ALU.max))
                link(v.tensor_tensor(oh[:, :, :], l1[:, :, :], lm[:, :].unsqueeze(2).to_broadcast([P, TPG, E]),
                                     ALU.is_equal))
                res = x[:, g * TPG:(g + 1) * TPG, :]
                link(v.tensor_tensor(res, res, y[:, g * TPG:(g + 1) * TPG, :], ALU.add))
                for e in range(E):
                    i = g * E + e
                    dve.wait_ge(s_y_ps, i + 1)
                    for tt in range(TPG):
                        last = v.scalar_tensor_tensor(out=res[:, tt, :], in0=Po[:, i % 2, tt * P:(tt + 1) * P],
                                                      scalar=oh[:, tt, e:e + 1], in1=res[:, tt, :],
                                                      op0=ALU.mult, op1=ALU.add)
                    last.then_inc(s_y, 1)
                    dve.wait_ge(s_y, i + 1)
                v.tensor_copy(lm[:, 0:1], lm[:, 0:1]).then_inc(s_fin, 1)


WEIGHT_LOADS = 22


def kernel(**inputs):
    import numpy as np
    import concourse.bacc as bacc
    from concourse.bass_utils import run_bass_kernel_spmd

    def flat(name):
        return np.ascontiguousarray(inputs[name])

    def turned(name):
        return np.ascontiguousarray(np.asarray(inputs[name]).T)

    given = {
        "x": flat("L0_attn_x"), "wqT": turned("L0_attn_wq"), "bq": flat("L0_attn_bq"), "wkT": turned("L0_attn_wk"),
        "bk": flat("L0_attn_bk"), "wvT": turned("L0_attn_wv"), "bv": flat("L0_attn_bv"), "woT": turned("L0_attn_wo"),
        "bo": flat("L0_attn_bo"), "wqiT": turned("L0_attn_wqi"), "bqi": flat("L0_attn_bqi"),
        "wkiT": turned("L0_attn_wki"), "bki": flat("L0_attn_bki"), "ln1_w": flat("L0_ffn_ln1_w"),
        "ln1_b": flat("L0_ffn_ln1_b"), "w_qkv": flat("L0_ffn_w_qkv"), "w_proj": flat("L0_ffn_w_proj"),
        "ln2_w": flat("L0_ffn_ln2_w"), "ln2_b": flat("L0_ffn_ln2_b"), "gate_w": flat("L0_ffn_gate_w"),
        "gate_b": flat("L0_ffn_gate_b"), "w1": flat("L0_ffn_w1"), "w2": flat("L0_ffn_w2"),
    }
    nc = bacc.Bacc("TRN2", target_bir_lowering=False, num_devices=1)
    in_ = {n: nc.dram_tensor(f"in_{n}", a.shape, mybir.dt.from_np(a.dtype), kind="ExternalInput").ap()
           for n, a in given.items()}
    out = nc.dram_tensor("out", (1, S, D), F32, kind="ExternalOutput").ap()
    build(nc, in_, out)
    r = run_bass_kernel_spmd(nc, [{f"in_{n}": a for n, a in given.items()}], core_ids=[0])
    return r.results[0]["out"]
```

```python
from contextlib import ExitStack

import concourse.bass as bass
from concourse import mybir

F32 = mybir.dt.float32
BF16 = mybir.dt.bfloat16
I32 = mybir.dt.int32
ALU = mybir.AluOpType
ACT = mybir.ActivationFunctionType
AX_X = mybir.AxisListType.X

P = 128
S = 2048
D = 128
H = 16
DH = D // H
WORK = 64
ASSOC = S - WORK
TOPK = 64
IDX = 64
E = 8
HID = 4 * D
EPS = 1e-5
SCALE = float(DH) ** -0.5

QG = 512
GROUPS = S // QG
TPG = QG // P
TILES = S // P
PASSES = 2
PAIRS = H // 2
PPP = PAIRS // PASSES
STEPS = TILES * PPP
GSTEPS = PASSES * STEPS
SLOTS = 6
KQ = SLOTS * DH
KROWS = KQ + 3
VW = DH + 1
Q_PART = (0, 0, 0, 1, 1, 2)
K_PART = (0, 1, 2, 0, 1, 0)

SLOT_TILES = TILES + E
LOADS = 4
TPL = SLOT_TILES // LOADS
SHIFTS = 3 * TILES * H
SHIFT_STORES = 16 * (P // H)
NONE = TILES // 2

MASK = 2.0 ** 117
TAKEN = -3.0e38
KEPT = 3.0e38
STRIPES = 64
TIE = 2.0 ** -100

SHIFT = (0.0, 48.0)
LIMIT = (72.0, 116.0)

ROUNDS = TOPK // 8
COUNTS = 4
COPIES = -(-ASSOC // QG)
PIECES = COPIES + STRIPES // 8 + ROUNDS + 1
FIRST_PIECE = 22

TAIL_OUTPUTS = (5, 6, 8, 10)
TAIL_TRANSPOSE = 13
TAIL_PROJECT = 16
TAIL_END = 19


def piece_at(s):
    k = s - FIRST_PIECE
    return divmod(k, PIECES) if 0 <= k < TPG * PIECES else None


def count_at(s):
    k = s - FIRST_PIECE - PIECES - 3
    return (k // PIECES, k % PIECES // 2) if 0 <= k < TPG * PIECES and k % PIECES in (0, 2, 4, 6) else None


CHECK_STEP = 117
CAREFUL_STEP = 125


KEYS_AHEAD = 4


POOL_QUERIES = 176


def selects(g, s):
    return g < GROUPS - 1 and FIRST_PIECE <= s < FIRST_PIECE + TPG * PIECES


def masked_by_tensor(g, s):
    return selects(g, s) and piece_at(s)[1] >= COPIES


VECTOR_MASKED = [sum(not masked_by_tensor(n // GSTEPS, n % GSTEPS) for n in range(m))
                 for m in range(GROUPS * GSTEPS + 1)]


def vector_masked(g, s):
    return VECTOR_MASKED[GSTEPS * g + s]


def third_pair_free(n):
    G, s = divmod(n, GSTEPS)
    if G % GROUPS and s <= TAIL_END:
        return False
    if G < GROUPS - 1 and s >= FIRST_PIECE - 1:
        k = s - FIRST_PIECE
        return (0 <= k < TPG * PIECES and COPIES < k % PIECES < PIECES - 1 or
                TPG * PIECES <= k <= CHECK_STEP - FIRST_PIECE or s > CAREFUL_STEP)
    return True


def place_scores():
    last, banks, before = {0: None, 1: None, 2: None}, [], []
    for n in range(2 * GROUPS * GSTEPS):
        allowed = (0, 1, 2) if third_pair_free(n) else (0, 1)
        b = min(allowed, key=lambda i: -1 if last[i] is None else last[i])
        banks.append(b)
        before.append(last[b])
        last[b] = n
    return banks, before


BANKS, LAST_IN_BANKS = place_scores()


def last_in_third(n):
    return max((m for m in range(max(0, n - 64), n) if BANKS[m] == 2), default=None)


def build(nc, in_, out):
    ctx = ExitStack()
    with ctx:
        def sb(name, shape, dt):
            return ctx.enter_context(nc.sbuf_tensor(name, shape, dt))

        def ps(name, shape, dt):
            return ctx.enter_context(nc.psum_tensor(name, shape, dt))

        def sem(name):
            return ctx.enter_context(nc.semaphore(name))

        x = sb("x", [P, TILES, D], F32)
        xT = sb("xT", [P, S], F32)
        Qs = sb("Qs", [P, 2, S], BF16)
        Ks = sb("Ks", [P, 2, S], BF16)
        KA = sb("KA", [P, PAIRS, S], BF16)
        QA = sb("QA", [P, H, QG], BF16)
        VA = sb("VA", [P, TILES, H, VW], F32)
        Pb = sb("Pb", [P, 4, 2 * QG], F32)
        MT = sb("MT", [P, 2, TILES, QG], BF16)
        Mq = sb("Mq", [P, 2, S], BF16)
        sw = sb("sw", [P, ASSOC], F32)
        tie = sb("tie", [P, S], F32)
        kiT = sb("kiT", [IDX, S], F32)
        qiT = sb("qiT", [IDX, S], F32)
        OT = sb("OT", [P, PASSES, 2, QG], F32)
        msc = sw[0:H, 0:2 * QG].rearrange("p (a n) -> p a n", a=2)
        Ms = sw[0:H, 2 * QG:2 * QG + 3 * QG // 2].bitcast(BF16).rearrange("p (a n) -> p a n", a=3)
        otflat = OT[:, :, :, :].rearrange("p a b n -> p (a b n)")
        Mq_parts = otflat[:, 0:SHIFTS // 2].bitcast(BF16)
        MT_parts = otflat[:, SHIFTS // 2:SHIFTS].bitcast(BF16).rearrange("p (b q) -> p b q", q=P)
        att = sb("att", [P, TPG, D], F32)
        attT = sb("attT", [P, QG], F32)
        mx = sb("mx", [P, TILES, H], F32)
        ngm = sb("ngm", [P, TILES, H], F32)
        nq = sb("nq", [P, TILES, H], F32)
        ok = sb("ok", [P, TILES, H], F32)
        mv = sb("mv", [P, TILES, 2], F32)
        st = sb("st", [P, TILES, 6], F32)
        ve = sb("ve", [P, TILES], F32)
        rs = sb("rs", [P, TILES], F32)
        rt = sb("rt", [P, TILES], F32)
        mhalf = sb("mhalf", [P, TILES], F32)
        top8 = sb("top8", [P, 8], F32)
        masked_keys = sb("masked_keys", [P, TILES, COUNTS], F32)
        cand = sb("cand", [P, STRIPES * 8], F32)
        cm = sb("cm", [P, 4], F32)
        ck = sb("ck", [P, TPG], F32)
        keep = sb("keep", [P, KEYS_AHEAD, QG], BF16)
        rec = sb("rec", [P, 2, H], F32)
        kn = sb("kn", [H, GROUPS], F32)
        kd = sb("kd", [H, 2 + H], F32)
        fl = sb("fl", [P, 4], F32)
        fli = sb("fli", [1, GROUPS + 1], I32)
        ident = sb("ident", [P, P], F32)
        masking = sb("masking", [P, P], BF16)
        ones = sb("ones", [H, P], F32)
        hmask = sb("hmask", [P, H], F32)
        w_q = sb("w_q", [P, 2, D], F32)
        w_k = sb("w_k", [P, 2, D], F32)
        w_v = sb("w_v", [P, 2, D], F32)
        w_o = sb("w_o", [P, 2, D], F32)
        w_i = sb("w_i", [P, 2, IDX], F32)
        colb = sb("colb", [P, 8], F32)
        bv = sb("bv", [P, D], F32)
        bo = sb("bo", [P, D], F32)
        gw = sb("gw", [P, E], F32)
        gb = sb("gb", [P, E], F32)
        rank = sb("rank", [P, E], F32)
        Lo = Mq
        y = tie[:, :].rearrange("p (t d) -> p t d", d=D)
        mtflat = MT[:, :, :, :].rearrange("p a b c -> p (a b c)")
        Kbd = mtflat[:, 0:2 * H * WORK].rearrange("p (a h n) -> p a h n", a=2, h=H)
        sqq = Pb[:, 0, 0:QG]
        sqk = Pb[:, 0, QG:2 * QG]
        qf = Pb[:, 1, 0:QG]
        qr = Pb[:, 1, QG:2 * QG]
        kf = Pb[:, 2, 0:QG]
        kr = Pb[:, 2, QG:2 * QG]
        w1 = mtflat[:, 0:2 * E * HID].bitcast(F32).rearrange("p (e h) -> p e h", e=E)
        w2 = mtflat[:, 2 * E * HID:4 * E * HID].bitcast(F32).rearrange("p (e c d) -> p e c d", e=E, c=4)
        hT = Pb[:, 0, :].rearrange("p (a n) -> p a n", a=2)
        kaflat = KA[:, :, :].rearrange("p a b -> p (a b)").bitcast(F32)
        expert_regions = [0]

        def over_keys(n):
            first = expert_regions[0]
            expert_regions[0] += n
            return kaflat[:, first:first + n]

        xs = over_keys(SLOT_TILES * D).rearrange("p (j d) -> p j d", d=D)
        ys = over_keys(SLOT_TILES * D).rearrange("p (j d) -> p j d", d=D)
        w1s = over_keys(2 * HID).rearrange("p (a h) -> p a h", a=2)
        w2s = over_keys(2 * HID).rearrange("p (a h) -> p a h", a=2)
        gathered = QA[:, :, :].rearrange("p a b -> p (a b)").bitcast(F32)[:, 0:S].rearrange("p (t d) -> p t d", d=D)
        xsT = attT[:, 0:2 * P].rearrange("p (a n) -> p a n", a=2)
        mqflat = Mq[:, :, :].rearrange("p a b -> p (a b)").bitcast(F32)
        routing_regions = [0]

        def over_masks(*shape):
            first, n = routing_regions[0], 1
            for m in shape:
                n *= m
            routing_regions[0] += n
            flat = mqflat[:, first:first + n]
            return flat if len(shape) == 1 else flat.rearrange("p (a b) -> p a b", a=shape[0])

        zeros = over_masks(D)
        before = over_masks(P)
        ones_all = over_masks(P)
        full = over_masks(TILES)
        slot = over_masks(SLOT_TILES)
        earlier = over_masks(E, E)
        lg = over_masks(TILES, E)
        l1 = over_masks(TILES, E)
        lm = over_masks(TILES)
        oh = over_masks(TILES, E)
        sums = over_masks(2, (NONE + TILES) * E).rearrange("p a (t e) -> p a t e", e=E)
        in_expert = over_masks(E)
        begun = over_masks(E, TILES)
        tiles_of = over_masks(E)
        products = over_masks(E, E)
        first_of = over_masks(E)
        end_of = over_masks(E)
        past = over_masks(SLOT_TILES, E)
        expert_f = over_masks(SLOT_TILES)
        expert_i = over_masks(SLOT_TILES).bitcast(I32)
        place_f = over_masks(TILES)
        place_i = over_masks(TILES).bitcast(I32)
        qm = attT[:, :].bitcast(BF16)[:, 0:2 * P].rearrange("p (a n) -> p a n", a=2)
        counted = attT[:, :].bitcast(BF16)[:, 0:ASSOC // COUNTS]
        cs = att[:, :, :].rearrange("p t d -> p (t d)")

        Sp = ps("Sp", [P, 4, QG], F32)
        Po = ps("Po", [P, 2, QG], F32)
        X = ps("X", [P, 2, QG], F32)

        def index_bank(t, c):
            return Sp[:, c, :] if t < TPG else X[:, c % 2, :]

        def pair(n):
            return X[:, :, :] if BANKS[n] == 2 else Sp[:, 2 * BANKS[n]:2 * BANKS[n] + 2, :]

        qd = [nc.dram_tensor(f"q_rows{a}", [D, SLOTS, S], BF16).ap() for a in range(2)]
        kd_ = [nc.dram_tensor(f"k_rows{a}", [D, SLOTS, S], BF16).ap() for a in range(2)]
        md = [nc.dram_tensor(f"shift_rows{a}", [H, 3, S], BF16).ap() for a in range(2)]

        xs_rows = nc.dram_tensor("sorted_tokens", [SLOT_TILES * P, D], F32).ap()
        ys_rows = nc.dram_tensor("sorted_results", [SLOT_TILES * P, D], F32).ap()

        s_x = [sem(f"tokens_loaded{g}") for g in range(GROUPS)]
        s_w = sem("weights_loaded")
        s_moe_w = sem("expert_weights_loaded_and_slots_cleared")
        s_const = sem("constants_ready")
        s_id0 = sem("identity_zeroed")
        s_id = sem("identity_ready")
        s_init = sem("vector_init_done")
        s_ones = sem("operands_filled")
        s_var = sem("variance_ready")
        s_pow = sem("rsqrt_guess_ready")
        s_xg = sem("normalised_tiles_ready")
        s_xt_ps = sem("tiles_transposed")
        s_xT = sem("xT_ready")
        s_q_ps = sem("q_projected")
        s_k_ps = sem("k_projected")
        s_v_ps = sem("v_projected")
        s_i_ps = sem("index_projected")
        s_qf = sem("q_float_ready")
        s_kf = sem("k_float_ready")
        s_round = sem("high_and_middle_parts_ready")
        s_rest = sem("rests_ready")
        s_qs = sem("q_parts_ready")
        s_ks = sem("k_parts_ready")
        s_va = sem("values_ready")
        s_iT = sem("index_rows_ready")
        s_sqq = sem("q_squares_ready")
        s_sqk = sem("k_squares_ready")
        s_nq_ps = sem("q_norms_summed")
        s_kn_ps = sem("k_norms_summed")
        s_kn = sem("k_norm_max_taken")
        s_kbd = sem("window_keys_then_k_norm_diagonal_ready")
        s_win_ps = sem("window_scores_ready")
        s_win = sem("window_max_taken")
        s_ms = sem("shift_parts_ready")
        s_mst = sem("shift_parts_transposed")
        s_kb_ps = sem("k_norm_spread")
        s_ok = sem("bound_checked")
        s_ok_ps = sem("bound_transposed")
        s_flag = sem("flag_ready")
        s_qd = sem("q_rows_stored")
        s_kd = sem("k_rows_stored")
        s_md = sem("shift_rows_stored")
        s_ka = sem("k_operand_loaded")
        s_qa = [sem(f"q_operand_loaded{i}") for i in range(PASSES)]
        s_qk = sem("scores_ready")
        s_exp = sem("weights_exp_done")
        s_pv = sem("weights_used")
        s_po = sem("outputs_copied")
        s_ot_ps = sem("outputs_transposed")
        s_att = sem("outputs_normalised")
        s_attT_ps = sem("att_transposed")
        s_attT = sem("attT_ready")
        s_wo_ps = sem("att_projected")
        s_res = sem("residual_added")
        s_idx_ps = sem("index_scores_ready")
        s_idx = sem("index_scores_copied")
        s_mq = sem("mask_ready")
        s_mt = [sem(f"mask_transposed{i}") for i in range(2)]
        s_zeros = sem("routing_constants_begun")
        s_rc = sem("routing_constants_then_residuals_ready")
        s_g_ps = sem("gate_scores_ready")
        s_rank_ps = sem("token_ranks_ready")
        s_place = sem("one_hot_then_places_ready")
        s_scat = sem("tokens_scattered")
        s_w1s = sem("first_layer_copied")
        s_w2s = sem("second_layer_copied")
        s_xsT_ps = sem("slot_tile_transposed")
        s_xsT = sem("slot_tile_scaled")
        s_h_ps = sem("hidden_ready")
        s_h = sem("gelu_done")
        s_y_ps = sem("expert_output_ready")
        s_ys = sem("expert_output_copied")
        s_yst = sem("sorted_results_stored")
        s_gat = [sem(f"results_gathered{i}") for i in range(GROUPS)]
        s_fin = sem("result_ready")
        s_out = sem("result_stored")
        s_chain = sem("vector_chain")
        s_vm = sem("weights_masked_by_vector")
        s_pm = sem("weights_masked_by_pool")
        s_keep = sem("key_block_masks_ready")
        s_cnt = sem("masked_keys_counted")
        s_cok = sem("selection_checked")
        s_cok_ps = sem("check_transposed")
        s_cflag = sem("check_flag_ready")

        class Careful:

            def __init__(self, n):
                if n < GROUPS:
                    self.selection(n)
                self.q = sem(f"c{n}_head_q_ready")
                self.sc = sem(f"c{n}_scores_ready")
                self.red = sem(f"c{n}_chunk_max_taken")
                self.mx = sem(f"c{n}_head_max_taken")
                self.ngm = sem(f"c{n}_shift_ready")
                self.m_ps = sem(f"c{n}_shift_transposed")
                self.ms = sem(f"c{n}_shift_parts_ready")
                self.md = sem(f"c{n}_shift_rows_stored")
                self.chain = sem(f"c{n}_vector_chain")

            def selection(self, n):
                self.idx_ps = sem(f"c{n}_index_scores_ready")
                self.idx = sem(f"c{n}_index_scores_copied")
                self.mq = sem(f"c{n}_mask_ready")
                self.mt = sem(f"c{n}_mask_transposed")
                self.add = sem(f"c{n}_scores_masked")

        care = [Careful(n) for n in range(GROUPS + 1)]

        block = ctx.enter_context(nc.Block())

        @block.sync
        def _(sp):
            for g in range(GROUPS):
                sp.dma_start(x[:, g * TPG:(g + 1) * TPG, :],
                             in_["x"].rearrange("b (t p) d -> p (b t) d", p=P)[:, g * TPG:(g + 1) * TPG, :]
                             ).then_inc(s_x[g], 16)
            loads = [(w_q[:, 0, :], in_["wqT"]), (w_k[:, 0, :], in_["wkT"]), (w_v[:, 0, :], in_["wvT"]),
                     (w_o[:, 0, :], in_["woT"]), (w_i[:, 0, :], in_["wqiT"]), (w_i[:, 1, :], in_["wkiT"]),
                     (w_q[:, 1, :], in_["w_qkv"][:, 0:D]), (w_k[:, 1, :], in_["w_qkv"][:, D:2 * D]),
                     (w_v[:, 1, :], in_["w_qkv"][:, 2 * D:3 * D]), (w_o[:, 1, :], in_["w_proj"]),
                     (gw[:, :], in_["gate_w"]),
                     (bv[:, :], in_["bv"].partition_broadcast(P)), (bo[:, :], in_["bo"].partition_broadcast(P)),
                     (gb[:, :], in_["gate_b"].partition_broadcast(P))]
            for i, name in enumerate(["bq", "bk", "bqi", "bki", "ln1_w", "ln1_b", "ln2_w", "ln2_b"]):
                n = in_[name].shape[0]
                loads.append((colb[0:n, i:i + 1], in_[name].rearrange("(p a) -> p a", a=1)))
            for dst, src in loads:
                sp.dma_start(dst, src).then_inc(s_w, 16)
            assert len(loads) == WEIGHT_LOADS

            def store_parts(a):
                for part, slots, dram, done in ((Ks, K_PART, kd_[a], s_kd), (Qs, Q_PART, qd[a], s_qd)):
                    sp.wait_ge(s_ks if part is Ks else s_qs, GROUPS * (a + 1))
                    for slot in range(SLOTS):
                        src = part[:, slots[slot], :] if slots[slot] < 2 else Lo[:, int(part is Ks), :]
                        sp.dma_start(dram[:, slot, :], src).then_inc(done, 16)

            def load_k(a):
                sp.wait_ge(s_kd, 16 * SLOTS * (a + 1))
                if a:
                    sp.wait_ge(s_qk, GROUPS * GSTEPS)
                else:
                    sp.wait_ge(s_ones, 4)
                rows = kd_[a].rearrange("(j hx d) s n -> hx (d s) j n", hx=2, d=DH)
                for hx in range(2):
                    sp.dma_start(KA[64 * hx:64 * hx + KQ, :, :], rows[hx]).then_inc(s_ka, 16)

            def store_shifts(a):
                sp.wait_ge(s_ms, a + 1)
                sp.dma_start_transpose(MT_parts, Mq_parts).then_inc(s_mst, 16)
                sp.wait_ge(s_mst, 16 * (a + 1))
                for t in range(P // H):
                    sp.dma_start(md[a].rearrange("h s (u t q) -> t h (s u) q", t=P // H, q=P)[t],
                                 MT_parts[t * H:(t + 1) * H]).then_inc(s_md, 16)

            def load_q(G, hh, rows=True, shifts=True):
                a, g = divmod(G, GROUPS)
                cols = slice(g * QG, (g + 1) * QG)
                js = slice(hh * PPP, (hh + 1) * PPP)
                half = QA[:, :, :].rearrange("p (j hx) n -> p hx j n", hx=2)
                if rows:
                    if g == 0 and hh == 0:
                        sp.wait_ge(s_qd, 16 * SLOTS * (a + 1))
                    if 2 * G + hh >= 2:
                        sp.wait_ge(s_qk, STEPS * (2 * G + hh - 1))
                    part_rows = qd[a].rearrange("(j hx d) s n -> hx (d s) j n", hx=2, d=DH)
                    for hx in range(2):
                        sp.dma_start(half[64 * hx:64 * hx + KQ, hx, js, :], part_rows[hx][:, js, cols]
                                     ).then_inc(s_qa[hh], 16)
                if shifts:
                    if g == 0 and hh == 0:
                        sp.wait_ge(s_md, SHIFT_STORES * (a + 1))
                    shift_rows = md[a].rearrange("(j hx) s n -> hx s j n", hx=2)
                    for hx in range(2):
                        sp.dma_start(half[64 * hx + KQ:64 * hx + KROWS, hx, js, :], shift_rows[hx][:, js, cols]
                                     ).then_inc(s_qa[hh], 16)

            def transpose_mask(t):
                sp.wait_ge(s_mq, t + 1)
                g, tt = divmod(t, TPG)
                if g >= 2 and tt == 0:
                    sp.wait_ge(s_qk, GSTEPS * (g - 1))
                    sp.wait_ge(s_vm, vector_masked(g - 2, GSTEPS))
                    sp.wait_ge(s_keep, (g - 1) * GSTEPS // PPP)
                sp.dma_start_transpose(MT[:, g % 2, :, tt * P:(tt + 1) * P], Mq[:, t % 2, :]
                                       ).then_inc(s_mt[t % 2], 16)

            def careful(a, groups, c):
                if a == 0:
                    g = groups[0]
                    for i in range(2):
                        sp.wait_ge(s_mt[i], 16 * 2 * (g + 1))
                    for tt in range(TPG):
                        sp.wait_ge(c.mq, tt + 1)
                        sp.dma_start_transpose(MT[:, g % 2, :, tt * P:(tt + 1) * P], Mq[:, tt % 2, :]
                                               ).then_inc(c.mt, 16)
                        sp.wait_ge(c.mt, 16 * (tt + 1))
                for i, g in enumerate(groups):
                    sp.wait_ge(c.ms, i + 1)
                    sp.dma_start(md[a][:, :, g * QG:(g + 1) * QG], Ms
                                 ).then_inc(c.md, 16)
                    sp.wait_ge(c.md, 16 * (i + 1))

            store_parts(0)
            load_k(0)
            store_shifts(0)
            sp.wait_ge(s_win, TILES)
            for g in range(GROUPS):
                for t in range(TPG):
                    transpose_mask(g * TPG + t)
                sp.wait_ge(s_cflag, g + 1)
                fine = sp.value_load(fli[0:1, g:g + 1], min_val=0, max_val=1)
                with sp.If(fine == 0):
                    if g == 0:
                        sp.wait_ge(s_md, SHIFT_STORES)
                    careful(0, [g], care[g])
                load_q(g, 0)
                load_q(g, 1)
            store_parts(1)
            load_k(1)
            for hh in range(PASSES):
                load_q(GROUPS, hh, shifts=False)
            store_shifts(1)
            sp.wait_ge(s_flag, 2)
            fine = sp.value_load(fli[0:1, GROUPS:GROUPS + 1], min_val=0, max_val=1)
            with sp.If(fine == 0):
                sp.wait_ge(s_md, SHIFT_STORES * 2)
                careful(1, list(range(GROUPS)), care[GROUPS])
            for hh in range(PASSES):
                load_q(GROUPS, hh, rows=False)
            sp.wait_ge(s_win, 2 * TILES)
            for e in range(E):
                sp.dma_start(w1[:, e, :], in_["w1"][e]).then_inc(s_moe_w, 16)
                sp.dma_start(w2[:, e, :, :], in_["w2"][e].rearrange("(c p) d -> p c d", p=P)).then_inc(s_moe_w, 16)
            sp.wait_ge(s_zeros, 3)
            sp.dma_start(xs_rows.rearrange("(j p) d -> p j d", p=P),
                         zeros[:, :].unsqueeze(1).to_broadcast([P, SLOT_TILES, D])).then_inc(s_moe_w, 16)
            for G in range(GROUPS + 1, 2 * GROUPS):
                load_q(G, 0)
                load_q(G, 1)
            sp.wait_ge(s_scat, 16 * TILES)
            for i in range(LOADS):
                js = slice(i * TPL, (i + 1) * TPL)
                sp.dma_start(xs[:, js, :], xs_rows.rearrange("(j p) d -> p j d", p=P)[:, js, :]).then_inc(s_x[i], 16)
            for i in range(LOADS):
                js = slice(i * TPL, (i + 1) * TPL)
                sp.wait_ge(s_ys, (i + 1) * TPL)
                sp.dma_start(ys_rows.rearrange("(j p) d -> p j d", p=P)[:, js, :], ys[:, js, :]).then_inc(s_yst, 16)
            for g in range(GROUPS):
                sp.wait_ge(s_fin, g + 1)
                sp.dma_start(out.rearrange("b (t p) d -> p (b t) d", p=P)[:, g * TPG:(g + 1) * TPG, :],
                             x[:, g * TPG:(g + 1) * TPG, :]).then_inc(s_out, 16)
            sp.wait_ge(s_out, 16 * GROUPS)

        @block.gpsimd
        def _(pool):
            nc.gpsimd.memset(ident[:, :], 0.0).then_inc(s_id0, 1)
            nc.gpsimd.memset(masking[:, :], 0.0).then_inc(s_id0, 1)
            nc.gpsimd.memset(hmask[:, :], 1.0).then_inc(s_id0, 1)
            pool.wait_ge(s_id0, 3)
            for m, value in ((ident, 1.0), (masking, -MASK)):
                nc.gpsimd.affine_select(out=m[:, :], in_=m[:, :], compare_op=ALU.not_equal, fill=value, base=0,
                                        pattern=[[-1, P]], channel_multiplier=1).then_inc(s_id, 1)
            nc.gpsimd.affine_select(out=hmask[:, :], in_=hmask[:, :], compare_op=ALU.is_ge, fill=0.0, base=0,
                                    pattern=[[-DH, H]], channel_multiplier=1).then_inc(s_id0, 1)
            pool.wait_ge(s_id0, 4)
            nc.gpsimd.affine_select(out=hmask[:, :], in_=hmask[:, :], compare_op=ALU.is_ge, fill=0.0, base=DH - 1,
                                    pattern=[[DH, H]], channel_multiplier=-1).then_inc(s_id, 1)
            nc.gpsimd.memset(mhalf[:, :], -0.5).then_inc(s_const, 1)
            nc.gpsimd.iota(tie[:, :].bitcast(I32), pattern=[[1, S]], base=1, channel_multiplier=0).then_inc(s_const, 1)
            nc.gpsimd.iota(rank[:, :].bitcast(I32), pattern=[[-1, E]], base=E, channel_multiplier=0
                           ).then_inc(s_const, 1)
            pool.wait_ge(s_const, 3)
            for n in range(4):
                if n == 3:
                    pool.wait_ge(s_qd, 16 * SLOTS * 2)
                    pool.wait_ge(s_kd, 16 * SLOTS * 2)
                    nc.gpsimd.memset(zeros[:, :], 0.0).then_inc(s_zeros, 1)
                    nc.gpsimd.memset(before[:, :], 1.0).then_inc(s_zeros, 1)
                    nc.gpsimd.memset(earlier[:, :, :], 1.0).then_inc(s_zeros, 1)
                    nc.gpsimd.memset(ones_all[:, :], 1.0).then_inc(s_rc, 1)
                    for i in range(2):
                        nc.gpsimd.memset(sums[:, i, 0:NONE, :], 0.0).then_inc(s_rc, 1)
                    nc.gpsimd.iota(full[:, :].bitcast(I32), pattern=[[P, TILES]], base=0, channel_multiplier=0
                                   ).then_inc(s_rc, 1)
                    nc.gpsimd.iota(slot[:, :].bitcast(I32), pattern=[[1, SLOT_TILES]], base=0, channel_multiplier=0
                                   ).then_inc(s_rc, 1)
                    pool.wait_ge(s_zeros, 3)
                    nc.gpsimd.affine_select(out=before[:, :], in_=before[:, :], compare_op=ALU.is_ge, fill=0.0,
                                            base=-1, pattern=[[1, P]], channel_multiplier=-1).then_inc(s_rc, 1)
                    nc.gpsimd.affine_select(out=earlier[:, :, :], in_=earlier[:, :, :], compare_op=ALU.is_ge,
                                            fill=0.0, base=-1, pattern=[[1, E], [-1, E]], channel_multiplier=0
                                            ).then_inc(s_rc, 1)
                    pool.wait_ge(s_res, 2 * GROUPS)
                    nc.gpsimd.tensor_tensor(x[:, :, :], x[:, :, :], y[:, :, :], ALU.add).then_inc(s_rc, 1)
                pool.wait_ge(s_var, n + 1)
                nc.gpsimd.tensor_tensor(rs[:, :], ve[:, :], mhalf[:, :], ALU.pow).then_inc(s_pow, 1)
                if n == 0:
                    nc.gpsimd.memset(VA[:, :, :, :], 1.0).then_inc(s_ones, 1)
                    pool.wait_ge(s_ones, 1)
                    nc.gpsimd.memset(KA[32:64, :, :], 1.0).then_inc(s_ones, 1)
                    pool.wait_ge(s_ones, 2)
                    nc.gpsimd.memset(KA[96:128, :, :], 1.0).then_inc(s_ones, 1)
                    pool.wait_ge(s_ones, 3)
                    nc.gpsimd.memset(QA[:, :, :], 0.0).then_inc(s_ones, 1)
                    pool.wait_ge(s_xg, GROUPS)
                    nc.gpsimd.tensor_tensor(x[:, :, :], x[:, :, :], bo[:, :].unsqueeze(1).to_broadcast([P, TILES, D]),
                                            ALU.add).then_inc(s_ones, 1)
                    pool.wait_ge(s_ones, 5)
                    for g in range(GROUPS):
                        for s in range(GSTEPS):
                            m = GSTEPS * g + s
                            pool.wait_ge(s_exp, m + 1)
                            if s % PPP == 0:
                                pool.wait_ge(s_keep, m // PPP + 1)
                            w = Pb[:, m % 4, :].rearrange("p (b n) -> p b n", b=2)
                            k = keep[:, m // PPP % KEYS_AHEAD, :].unsqueeze(1)
                            if selects(g, s):
                                nc.gpsimd.tensor_tensor(w[:, 1:2, :], w[:, 1:2, :], k, ALU.mult).then_inc(s_pm, 1)
                            else:
                                w, k = w[:, :, QG - POOL_QUERIES:], k[:, :, QG - POOL_QUERIES:]
                                nc.gpsimd.tensor_tensor(w, w, k.to_broadcast([P, 2, POOL_QUERIES]), ALU.mult
                                                        ).then_inc(s_pm, 1)
            pool.wait_ge(s_place, 2)
            pool.wait_ge(s_moe_w, 32 * E + 16)
            for t in range(TILES):
                nc.gpsimd.indirect_dma_start(xs_rows, bass.IndirectOffsetOnAxis(place_i[:, t:t + 1], 0), y[:, t, :],
                                             None).then_inc(s_scat, 16)
            pool.wait_ge(s_yst, 16 * LOADS)
            for t in range(TILES):
                nc.gpsimd.indirect_dma_start(gathered[:, t, :], None, ys_rows,
                                             bass.IndirectOffsetOnAxis(place_i[:, t:t + 1], 0)
                                             ).then_inc(s_gat[t // TPG], 16)

        @block.scalar
        def _(act):
            def copy_tokens(a, g):
                cols = slice(g * QG, (g + 1) * QG)
                act.wait_ge(s_xt_ps, GROUPS * a + g + 1)
                if a == 0:
                    nc.scalar.activation(xT[:, cols], X[:, 0, :], ACT.Copy).then_inc(s_xT, 1)
                else:
                    nc.scalar.activation(xT[:, cols], X[:, 0, :], ACT.Identity, scale=colb[:, 4:5],
                                         bias=colb[:, 5:6]).then_inc(s_xT, 1)

            def prologue(a):
                copy_tokens(a, 0)
                for g in range(GROUPS):
                    G = GROUPS * a + g
                    cols = slice(g * QG, (g + 1) * QG)
                    act.wait_ge(s_qf, G + 1)
                    nc.scalar.activation(Qs[:, 0, cols], qf, ACT.Copy).then_inc(s_round, 1)
                    nc.scalar.activation(sqq, qf, ACT.Square).then_inc(s_sqq, 1)
                    act.wait_ge(s_kf, G + 1)
                    nc.scalar.activation(Ks[:, 0, cols], kf, ACT.Copy).then_inc(s_round, 1)
                    if G:
                        act.wait_ge(s_kn_ps, G)
                    nc.scalar.activation(sqk, Sp[:, 1, :], ACT.Square).then_inc(s_sqk, 1)
                    if g + 1 < GROUPS:
                        copy_tokens(a, g + 1)
                    if a == 0:
                        act.wait_ge(s_i_ps, g + 1)
                        nc.scalar.activation(qiT[:, cols], Sp[0:IDX, 3, :], ACT.Identity, bias=colb[0:IDX, 2:3]
                                             ).then_inc(s_iT, 1)
                        nc.scalar.activation(kiT[:, cols], Po[0:IDX, 1, :], ACT.Identity, bias=colb[0:IDX, 3:4]
                                             ).then_inc(s_iT, 1)
                    act.wait_ge(s_rest, 2 * G + 1)
                    nc.scalar.activation(Qs[:, 1, cols], qr, ACT.Copy).then_inc(s_round, 1)
                    act.wait_ge(s_rest, 2 * G + 2)
                    nc.scalar.activation(Ks[:, 1, cols], kr, ACT.Copy).then_inc(s_round, 1)

            def count(t, i):
                act.wait_ge(s_mq, t + 1)
                if COUNTS * t + i:
                    act.wait_ge(s_cnt, COUNTS * t + i)
                n = ASSOC // COUNTS
                nc.scalar.activation(counted[:, :], Mq[:, t % 2, i * n:(i + 1) * n], ACT.Identity,
                                     accum_out=masked_keys[:, t, i:i + 1]).then_inc(s_cnt, 1)

            def attention(a):
                for G in range(GROUPS * a, GROUPS * (a + 1)):
                    for s in range(GSTEPS):
                        if a == 0 and G + 1 < GROUPS and count_at(s):
                            tile, i = count_at(s)
                            count((G + 1) * TPG + tile, i)
                        n = GSTEPS * G + s
                        act.wait_ge(s_qk, n + 1)
                        if n >= 4:
                            act.wait_ge(s_pv, (n - 4) // 2 + 1)
                        nc.scalar.activation(Pb[:, n % 4, :], pair(n), ACT.Exp).then_inc(s_exp, 1)

            act.wait_ge(s_w, 16 * WEIGHT_LOADS)
            prologue(0)
            for t in range(TPG):
                for i in range(COUNTS):
                    count(t, i)
            attention(0)
            prologue(1)
            attention(1)
            for g in range(GROUPS):
                act.wait_ge(s_xt_ps, 2 * GROUPS + g + 1)
                nc.scalar.activation(xT[:, g * QG:(g + 1) * QG], Sp[:, g, :], ACT.Identity, scale=colb[:, 6:7],
                                     bias=colb[:, 7:8]).then_inc(s_xT, 1)

            def scale_tile(j):
                act.wait_ge(s_xsT_ps, j + 1)
                if j >= 2:
                    act.wait_ge(s_h_ps, j - 1)
                nc.scalar.activation(xsT[:, j % 2, :], X[:, j % 2, 0:P], ACT.Identity, scale=colb[:, 6:7],
                                     bias=colb[:, 7:8]).then_inc(s_xsT, 1)

            scale_tile(0)
            for j in range(SLOT_TILES):
                if j + 1 < SLOT_TILES:
                    scale_tile(j + 1)
                act.wait_ge(s_h_ps, j + 1)
                if j >= 2:
                    act.wait_ge(s_y_ps, j - 1)
                nc.scalar.activation(hT[:, j % 2, :], Sp[:, j % 2, :], ACT.Gelu_apprx_tanh).then_inc(s_h, 1)

        @block.tensor
        def _(pe):
            mm = nc.tensor.matmul

            def transpose_tiles(G):
                pe.wait_ge(s_xg, G + 1)
                if G:
                    pe.wait_ge(s_xT, G)
                for tt in range(TPG):
                    last = nc.tensor.transpose(X[:, 0, tt * P:(tt + 1) * P], att[:, tt, :], ident[:, :])
                last.then_inc(s_xt_ps, 1)

            def prologue(a):
                if a:
                    pe.wait_ge(s_res, GROUPS)
                transpose_tiles(GROUPS * a)
                for g in range(GROUPS):
                    G = GROUPS * a + g
                    cols = slice(g * QG, (g + 1) * QG)
                    pe.wait_ge(s_xT, G + 1)
                    if G:
                        pe.wait_ge(s_qf, G)
                    mm(Sp[:, 0, :], w_q[:, a, :], xT[:, cols], start=True, stop=True).then_inc(s_q_ps, 1)
                    if G:
                        pe.wait_ge(s_kf, G)
                        pe.wait_ge(s_sqk, G)
                    mm(Sp[:, 1, :], w_k[:, a, :], xT[:, cols], start=True, stop=True).then_inc(s_k_ps, 1)
                    if G:
                        pe.wait_ge(s_va, G)
                    for tt in range(TPG):
                        last = mm(Sp[:, 2, tt * P:(tt + 1) * P], xT[:, g * QG + tt * P:g * QG + (tt + 1) * P],
                                  w_v[:, a, :], start=True, stop=True)
                    last.then_inc(s_v_ps, 1)
                    if g + 1 < GROUPS:
                        transpose_tiles(G + 1)
                    if a == 0:
                        if g:
                            pe.wait_ge(s_iT, 2 * g)
                        mm(Sp[0:IDX, 3, :], w_i[:, 0, :], xT[:, cols], start=True, stop=True)
                        mm(Po[0:IDX, 1, :], w_i[:, 1, :], xT[:, cols], start=True, stop=True).then_inc(s_i_ps, 1)
                    pe.wait_ge(s_sqq, G + 1)
                    for tt in range(TPG):
                        t = g * TPG + tt
                        last = mm(Po[:, 0, t * H:(t + 1) * H], sqq[:, tt * P:(tt + 1) * P], hmask[:, :],
                                  start=True, stop=True, skip_group_check=True)
                    last.then_inc(s_nq_ps, 1)
                    pe.wait_ge(s_sqk, G + 1)
                    if G:
                        pe.wait_ge(s_kn, G)
                    mm(X[0:H, 1, :], hmask[:, :], sqk, start=True, stop=True).then_inc(s_kn_ps, 1)
                pe.wait_ge(s_kbd, 2 * (a + 1))
                if a == 0:
                    pe.wait_ge(s_iT, 2 * GROUPS)
                mm(Po[:, 1, 0:H], ones[:, :], kd[:, 2:2 + H], start=True, stop=True).then_inc(s_kb_ps, 1)
                pe.wait_ge(s_va, GROUPS * (a + 1))
                pe.wait_ge(s_sqk, GROUPS * (a + 1))
                for t in range(TILES):
                    n = TILES * a + t
                    if t >= 2:
                        pe.wait_ge(s_win, n - 1)
                    for i, (qp, kp) in enumerate(((0, 0), (0, 1), (1, 0))):
                        for hf in range(2):
                            last = mm(Sp[:, 2 * (t % 2) + hf, :], Qs[:, qp, t * P:(t + 1) * P],
                                      Kbd[:, kp, hf * 8:(hf + 1) * 8, :], start=(i == 0), stop=(i == 2),
                                      skip_group_check=True)
                    last.then_inc(s_win_ps, 1)
                if a == 0:
                    pe.wait_ge(s_win, TILES)
                    for c in range(COPIES):
                        index_chunk(0, c)
                pe.wait_ge(s_kn, GROUPS * (a + 1))
                pe.wait_ge(s_ok, a + 1)
                nc.tensor.transpose(X[0:1, 1, 0:P], fl[:, 0:1], ident[:, :]).then_inc(s_ok_ps, 1)
                pe.wait_ge(s_flag, a + 1)

            def third_pair_read(n):
                if last_in_third(n) is not None:
                    pe.wait_ge(s_exp, last_in_third(n) + 1)

            def index_chunk(t, c):
                i = COPIES * t + c
                w = min(QG, ASSOC - c * QG)
                last = i - (COPIES if t < TPG else 2)
                if last >= 0:
                    pe.wait_ge(s_idx, last + 1)
                mm(index_bank(t, c)[:, 0:w], qiT[:, t * P:(t + 1) * P], kiT[:, c * QG:c * QG + w], start=True, stop=True
                   ).then_inc(s_idx_ps, 1)

            def check_selection(g):
                pe.wait_ge(s_cok, g + 1)
                nc.tensor.transpose(X[0:1, 1, 0:P], fl[:, 2:3], ident[:, :]).then_inc(s_cok_ps, 1)

            def exact_max(i, t, c):
                with pe.Fori(0, H) as h:
                    pe.wait_ge(c.q, h + (i * H + 1))
                    for ch in range(4):
                        if ch >= 2:
                            pe.wait_ge(c.red, h * 4 + (4 * i * H + ch - 1))
                        for n, (qp, kp) in enumerate(((0, 0), (0, 1), (1, 0))):
                            last = mm(X[:, ch % 2, :], qm[:, qp, :], Ks[:, kp, ch * QG:(ch + 1) * QG],
                                      start=(n == 0), stop=(n == 2), skip_group_check=True)
                        last.then_inc(c.sc, 1)

            def careful(a, groups, c):
                for i, g in enumerate(groups):
                    for tt in range(TPG):
                        t = g * TPG + tt
                        if a == 0:
                            for ch in range(COPIES):
                                w = min(QG, ASSOC - ch * QG)
                                if ch >= 2:
                                    pe.wait_ge(c.idx, COPIES * tt + ch - 1)
                                elif tt:
                                    pe.wait_ge(c.mx, H * tt)
                                mm(X[:, ch % 2, 0:w], qiT[:, t * P:(t + 1) * P], kiT[:, ch * QG:ch * QG + w],
                                   start=True, stop=True).then_inc(c.idx_ps, 1)
                            pe.wait_ge(c.idx, COPIES * (tt + 1))
                        exact_max(TPG * i + tt, t, c)
                    pe.wait_ge(c.ngm, i + 1)
                    if i:
                        pe.wait_ge(c.ms, i)
                    for tt in range(TPG):
                        last = nc.tensor.transpose(X[0:H, 1, tt * P:(tt + 1) * P], ngm[:, g * TPG + tt, :],
                                                   ident[:, :])
                    last.then_inc(c.m_ps, 1)
                pe.wait_ge(c.ms, len(groups))
                if a == 0:
                    pe.wait_ge(c.mt, 16 * TPG)

            def care_for(g):
                pe.wait_ge(s_cflag, g + 1)
                fine = pe.value_load(fli[0:1, g:g + 1], min_val=0, max_val=1)
                with pe.If(fine == 0):
                    careful(0, [g], care[g])

            def scores(G, s, guarded):
                a = G // GROUPS
                n = GSTEPS * G + s
                hh, r = divmod(s, STEPS)
                kb, jj = divmod(r, PPP)
                j = hh * PPP + jj
                heads = () if a else (0, 1) if guarded else (0,) if masked_by_tensor(G, s) else ()
                if r == 0:
                    pe.wait_ge(s_qa[hh], 64 * (G + 1))
                if LAST_IN_BANKS[n] is not None:
                    pe.wait_ge(s_exp, LAST_IN_BANKS[n] + 1)
                if BANKS[n] == 2 and G < GROUPS - 1 and s >= FIRST_PIECE:
                    pe.wait_ge(s_idx, COPIES * (TPG * (G + 1) + (piece_at(s)[0] + 1 if piece_at(s) else TPG)))
                for hx in range(2):
                    last = mm(pair(n)[:, hx, :], KA[:, j, kb * P:(kb + 1) * P], QA[:, 2 * j + hx, :],
                              start=True, stop=hx not in heads, skip_group_check=True)
                for hx in heads:
                    last = mm(pair(n)[:, hx, :], masking[:, :], MT[:, G % 2, kb, :],
                              start=False, stop=True, skip_group_check=True)
                last.then_inc(s_qk, 1)

            def weighted_values(G, s):
                n = GSTEPS * G + s
                hh, r = divmod(s, STEPS)
                kb, jj = divmod(r, PPP)
                q = jj // 2
                pe.wait_ge(s_exp, n + 1)
                if G < GROUPS:
                    pe.wait_ge(s_pm, n + 1)
                    if not masked_by_tensor(G, s) or not masked_by_tensor(G, s - 1):
                        pe.wait_ge(s_vm, vector_masked(G, s + 1))
                if kb == 0 and 2 * G + hh >= 1:
                    pe.wait_ge(s_po, 2 * (2 * G + hh) - 1 + q)
                for i in range(4):
                    h = hh * 8 + q * 4 + i
                    last = mm(Po[32 * i:32 * i + VW, q, :], VA[:, kb, h, :],
                              Pb[:, (n - 1 + i // 2) % 4, (i % 2) * QG:(i % 2 + 1) * QG],
                              start=(kb == 0), stop=(kb == TILES - 1), skip_group_check=True)
                last.then_inc(s_pv, 1)

            def tail_outputs(G, tt):
                pe.wait_ge(s_po, 4 * (G + 1))
                if tt >= 2:
                    pe.wait_ge(s_att, TPG * G + tt - 1)
                for i in range(4):
                    last = nc.tensor.transpose(X[:, tt % 2, i * P:(i + 1) * P],
                                               OT[:, i // 2, i % 2, tt * P:(tt + 1) * P], ident[:, :])
                last.then_inc(s_ot_ps, 1)

            def tail_transpose(G):
                pe.wait_ge(s_att, TPG * (G + 1))
                for tt in range(TPG):
                    last = nc.tensor.transpose(X[:, 0, tt * P:(tt + 1) * P], att[:, tt, :], ident[:, :])
                last.then_inc(s_attT_ps, 1)

            def tail_project(G):
                pe.wait_ge(s_attT, G + 1)
                for tt in range(TPG):
                    last = mm(X[:, 1, tt * P:(tt + 1) * P], attT[:, tt * P:(tt + 1) * P], w_o[:, G // GROUPS, :],
                              start=True, stop=True)
                last.then_inc(s_wo_ps, 1)

            def group(G, guarded):
                a, g = divmod(G, GROUPS)
                if a == 0:
                    for i in range(2):
                        pe.wait_ge(s_mt[i], 16 * 2 * (g + 1))
                def products(s):
                    if s >= 4:
                        weighted_values(G, s - 3)
                    elif g:
                        weighted_values(G - 1, GSTEPS + s - 3)

                for s in range(GSTEPS):
                    n = GSTEPS * G + s
                    ahead = LAST_IN_BANKS[n] is None or n - LAST_IN_BANKS[n] >= 3
                    if s % 2 == 0 and not ahead:
                        products(s)
                    scores(G, s, guarded)
                    if s % 2 == 0 and ahead:
                        products(s)
                    if g:
                        if s == TAIL_OUTPUTS[0] and a == 0:
                            pe.wait_ge(s_idx, 4 * TPG * min(g + 1, GROUPS))
                        if s in TAIL_OUTPUTS:
                            tail_outputs(G - 1, TAIL_OUTPUTS.index(s))
                        if s == TAIL_TRANSPOSE:
                            tail_transpose(G - 1)
                        if s == TAIL_PROJECT:
                            tail_project(G - 1)
                        if s == TAIL_END:
                            pe.wait_ge(s_res, G)
                    if a == 0 and g + 1 < GROUPS:
                        if s == FIRST_PIECE and g:
                            pe.wait_ge(s_res, G)
                        if piece_at(s) and piece_at(s)[1] == 0:
                            third_pair_read(GSTEPS * G + s + 1)
                        if piece_at(s) and piece_at(s)[1] < COPIES:
                            index_chunk((g + 1) * TPG + piece_at(s)[0], piece_at(s)[1])
                        if s == CHECK_STEP + 2:
                            third_pair_read(GSTEPS * G + s + 1)
                            check_selection(g + 1)
                        if s == CAREFUL_STEP:
                            care_for(g + 1)

            def attention(a):
                pe.wait_ge(s_ka, 32 * (a + 1))
                for G in range(GROUPS * a, GROUPS * (a + 1)):
                    if a == 0:
                        fine = pe.value_load(fli[0:1, G:G + 1], min_val=0, max_val=1)
                        with pe.If(fine == 0):
                            group(G, True)
                        with pe.Else():
                            group(G, False)
                    else:
                        group(G, False)
                G = GROUPS * (a + 1) - 1
                weighted_values(G, GSTEPS - 3)
                weighted_values(G, GSTEPS - 1)
                for tt in range(TPG):
                    tail_outputs(G, tt)
                tail_transpose(G)
                tail_project(G)

            pe.wait_ge(s_id, 3)
            pe.wait_ge(s_w, 16 * WEIGHT_LOADS)
            pe.wait_ge(s_init, 1)
            prologue(0)
            for t in range(1, TPG):
                for c in range(COPIES):
                    index_chunk(t, c)
            pe.wait_ge(s_idx, 4 * TPG)
            check_selection(0)
            care_for(0)
            attention(0)
            prologue(1)
            fine = pe.value_load(fli[0:1, GROUPS:GROUPS + 1], min_val=0, max_val=1)
            with pe.If(fine == 0):
                careful(1, list(range(GROUPS)), care[GROUPS])
            attention(1)
            pe.wait_ge(s_res, 2 * GROUPS)
            pe.wait_ge(s_exp, 2 * GROUPS * GSTEPS)
            for g in range(GROUPS):
                pe.wait_ge(s_xg, 2 * GROUPS + g + 1)
                for tt in range(TPG):
                    last = nc.tensor.transpose(Sp[:, g, tt * P:(tt + 1) * P], y[:, g * TPG + tt, :], ident[:, :])
                last.then_inc(s_xt_ps, 1)
            for g in range(GROUPS):
                pe.wait_ge(s_xT, 2 * GROUPS + g + 1)
                for t in range(g * TPG, (g + 1) * TPG):
                    last = mm(X[:, 1, t * E:(t + 1) * E], xT[:, t * P:(t + 1) * P], gw[:, :], start=True, stop=True)
            last.then_inc(s_g_ps, 1)
            pe.wait_ge(s_place, 1)
            pe.wait_ge(s_rc, 7)
            mm(Sp[:, 1, 0:E], ones_all[:, :], sums[:, 0, NONE + TILES - 1, :], start=True, stop=True)
            mm(Sp[:, 0, 0:TILES * E], before[:, :], oh[:, :, :].rearrange("p t e -> p (t e)"), start=True, stop=False,
               skip_group_check=True)
            mm(Sp[:, 0, 0:TILES * E], ones_all[:, :],
               sums[:, 0, NONE - 1:NONE + TILES - 1, :].rearrange("p t e -> p (t e)"), start=False, stop=True,
               skip_group_check=True).then_inc(s_rank_ps, 1)

            def transpose_slots(j):
                if j % TPL == 0:
                    pe.wait_ge(s_x[j // TPL], 32)
                if j >= 2:
                    pe.wait_ge(s_xsT, j - 1)
                nc.tensor.transpose(X[:, j % 2, 0:P], xs[:, j, :], ident[:, :]).then_inc(s_xsT_ps, 1)

            def hidden(j):
                pe.wait_ge(s_xsT, j + 1)
                pe.wait_ge(s_w1s, j + 1)
                if j >= 2:
                    pe.wait_ge(s_h, j - 1)
                for c in range(4):
                    last = mm(Sp[:, j % 2, c * P:(c + 1) * P], w1s[:, j % 2, c * P:(c + 1) * P], xsT[:, j % 2, :],
                              start=True, stop=True)
                last.then_inc(s_h_ps, 1)

            def output(j):
                pe.wait_ge(s_h, j + 1)
                pe.wait_ge(s_w2s, j + 1)
                if j >= 2:
                    pe.wait_ge(s_ys, j - 1)
                for c in range(4):
                    last = mm(Po[:, j % 2, 0:D], hT[:, j % 2, c * P:(c + 1) * P], w2s[:, j % 2, c * D:(c + 1) * D],
                              start=(c == 0), stop=(c == 3), skip_group_check=True)
                last.then_inc(s_y_ps, 1)

            transpose_slots(0)
            transpose_slots(1)
            hidden(0)
            for j in range(SLOT_TILES):
                if j + 2 < SLOT_TILES:
                    transpose_slots(j + 2)
                if j + 1 < SLOT_TILES:
                    hidden(j + 1)
                output(j)

        @block.vector
        def _(dve):
            v = nc.vector
            def chain(done):
                count = [0]

                def link(ins):
                    count[0] += 1
                    ins.then_inc(done, 1)
                    dve.wait_ge(done, count[0])
                return link

            link = chain(s_chain)

            def statistics(src, n, first=0):
                for t in range(first, TILES):
                    if n == 0 and t % TPG == 0:
                        dve.wait_ge(s_x[t // TPG], 16)
                    last = v.bn_stats(st[:, t, :], src[:, t, :])
                link(last)
                for t in range(TILES):
                    last = v.bn_aggr(mv[:, t, :], st[:, t, :])
                link(last)
                v.tensor_scalar(ve[:, :], mv[:, :, 1], EPS, None, ALU.add).then_inc(s_var, 1)
                dve.wait_ge(s_var, n + 1)
                dve.wait_ge(s_pow, n + 1)
                link(v.tensor_tensor(rt[:, :], rs[:, :], rs[:, :], ALU.mult))
                link(v.tensor_tensor(rt[:, :], rt[:, :], ve[:, :], ALU.mult))
                link(v.tensor_scalar(rt[:, :], rt[:, :], -0.5, 1.5, ALU.mult, ALU.add))
                link(v.tensor_tensor(rs[:, :], rs[:, :], rt[:, :], ALU.mult))

            def normalise(dst, src, t):
                return v.tensor_scalar(dst, src[:, t, :], mv[:, t, 0:1], rs[:, t:t + 1], ALU.subtract, ALU.mult)

            def tiles_for_transpose(src, G):
                if G:
                    dve.wait_ge(s_xt_ps, G)
                for tt in range(TPG):
                    last = normalise(att[:, tt, :], src, (G % GROUPS) * TPG + tt)
                last.then_inc(s_xg, 1)

            def split(full, rest, high, middle, low, link=link):
                link(v.tensor_copy(high, full))
                link(v.tensor_tensor(rest, full, high, ALU.subtract))
                link(v.tensor_copy(middle, rest))
                return v.tensor_tensor(low, rest, middle, ALU.subtract)

            def prologue(a, src):
                if a:
                    dve.wait_ge(s_attT_ps, GROUPS)
                    dve.wait_ge(s_qd, 16 * SLOTS)
                    dve.wait_ge(s_kd, 16 * SLOTS)
                    dve.wait_ge(s_mt[0], 16 * TILES // 2)
                    dve.wait_ge(s_mt[1], 16 * TILES // 2)
                tiles_for_transpose(src, GROUPS * a)
                for g in range(GROUPS):
                    G = GROUPS * a + g
                    cols = slice(g * QG, (g + 1) * QG)
                    if g + 1 < GROUPS:
                        tiles_for_transpose(src, G + 1)
                    dve.wait_ge(s_q_ps, G + 1)
                    if G:
                        dve.wait_ge(s_sqq, G)
                    if a == 0:
                        v.tensor_scalar(qf, Sp[:, 0, :], colb[:, 0:1], SCALE, ALU.add, ALU.mult).then_inc(s_qf, 1)
                    else:
                        v.tensor_scalar(qf, Sp[:, 0, :], SCALE, None, ALU.mult).then_inc(s_qf, 1)
                    dve.wait_ge(s_k_ps, G + 1)
                    if a == 0:
                        v.tensor_scalar(kf, Sp[:, 1, :], colb[:, 1:2], None, ALU.add).then_inc(s_kf, 1)
                    else:
                        v.tensor_copy(kf, Sp[:, 1, :]).then_inc(s_kf, 1)
                    dve.wait_ge(s_round, 4 * G + 1)
                    v.tensor_tensor(qr, qf, Qs[:, 0, cols], ALU.subtract).then_inc(s_rest, 1)
                    dve.wait_ge(s_round, 4 * G + 2)
                    v.tensor_tensor(kr, kf, Ks[:, 0, cols], ALU.subtract).then_inc(s_rest, 1)
                    dve.wait_ge(s_v_ps, G + 1)
                    dve.wait_ge(s_ones, 1)
                    vdst = VA[:, g * TPG:(g + 1) * TPG, :, 0:DH]
                    vsrc = Sp[:, 2, :].rearrange("p (t h d) -> p t h d", t=TPG, h=H)
                    if a == 0:
                        for tt in range(TPG):
                            last = v.tensor_tensor(vdst[:, tt], vsrc[:, tt],
                                                   bv[:, :].rearrange("p (h d) -> p h d", h=H), ALU.add)
                    else:
                        last = v.tensor_copy(vdst, vsrc)
                    last.then_inc(s_va, 1)
                    dve.wait_ge(s_kn_ps, G + 1)
                    v.tensor_reduce(kn[:, g:g + 1], X[0:H, 1, :], AX_X, ALU.max).then_inc(s_kn, 1)
                    dve.wait_ge(s_round, 4 * G + 3)
                    v.tensor_tensor(Lo[:, 0, cols], qr, Qs[:, 1, cols], ALU.subtract).then_inc(s_qs, 1)
                    dve.wait_ge(s_round, 4 * G + 4)
                    v.tensor_tensor(Lo[:, 1, cols], kr, Ks[:, 1, cols], ALU.subtract).then_inc(s_ks, 1)
                dve.wait_ge(s_ks, GROUPS * (a + 1))
                for part in range(2):
                    last = v.tensor_tensor(Kbd[:, part], Ks[:, part, ASSOC:S].unsqueeze(1).to_broadcast([P, H, WORK]),
                                           hmask[:, :].unsqueeze(2).to_broadcast([P, H, WORK]), ALU.mult)
                last.then_inc(s_kbd, 1)
                dve.wait_ge(s_kn, GROUPS * (a + 1))
                link(v.tensor_reduce(kd[:, 0:1], kn[:, :], AX_X, ALU.max))
                v.tensor_scalar(kd[:, 2:2 + H], ident[0:H, 0:H], kd[:, 0:1], None, ALU.mult).then_inc(s_kbd, 1)
                for t in range(TILES):
                    n = TILES * a + t
                    dve.wait_ge(s_win_ps, n + 1)
                    v.tensor_reduce(mx[:, t, :],
                                    Sp[:, 2 * (t % 2):2 * (t % 2) + 2, :].rearrange("p b (h n) -> p (b h) n", n=WORK),
                                    AX_X, ALU.max).then_inc(s_win, 1)
                dve.wait_ge(s_win, TILES * (a + 1))
                link(v.tensor_scalar(ngm[:, :, :], mx[:, :, :], -1.0, -SHIFT[a], ALU.mult, ALU.add))
                parts = Mq_parts.rearrange("p (s n) -> p s n", s=3)
                split(ngm[:, :, :].rearrange("p t h -> p (t h)"), ok[:, :, :].rearrange("p t h -> p (t h)"),
                      parts[:, 0, :], parts[:, 1, :], parts[:, 2, :]).then_inc(s_ms, 1)
                dve.wait_ge(s_ms, a + 1)
                dve.wait_ge(s_nq_ps, GROUPS * (a + 1))
                link(v.tensor_copy(nq[:, :, :], Po[:, 0, 0:TILES * H].rearrange("p (t h) -> p t h", h=H)))
                dve.wait_ge(s_kb_ps, a + 1)
                link(v.tensor_tensor(nq[:, :, :], nq[:, :, :],
                                     Po[:, 1, 0:H].unsqueeze(1).to_broadcast([P, TILES, H]), ALU.mult))
                if a == 0:
                    link(v.tensor_scalar(ok[:, :, :], nq[:, :, :], 4.0, LIMIT[0] ** 2, ALU.mult, ALU.is_le))
                else:
                    link(v.tensor_scalar(mx[:, :, :], mx[:, :, :], LIMIT[1], None, ALU.add))
                    link(v.tensor_scalar(ok[:, :, :], mx[:, :, :], 0.0, None, ALU.max))
                    link(v.tensor_tensor(mx[:, :, :], ok[:, :, :], mx[:, :, :], ALU.mult))
                    link(v.tensor_tensor(ok[:, :, :], nq[:, :, :], mx[:, :, :], ALU.is_le))
                v.tensor_reduce(fl[:, 0:1], ok[:, :, :].rearrange("p t h -> p (t h)"), AX_X, ALU.min
                                ).then_inc(s_ok, 1)
                dve.wait_ge(s_ok_ps, a + 1)
                link(v.tensor_reduce(fl[0:1, 1:2], X[0:1, 1, 0:P], AX_X, ALU.min))
                v.tensor_copy(fli[0:1, GROUPS:GROUPS + 1], fl[0:1, 1:2]).then_inc(s_flag, 1)
                dve.wait_ge(s_flag, a + 1)

            def copy_index_scores(k, bank):
                n = min(QG, ASSOC - k * QG)
                return v.scalar_tensor_tensor(out=sw[:, k * QG:k * QG + n], in0=bank[:, 0:n], scalar=0.0,
                                              in1=tie[:, k * QG:k * QG + n], op0=ALU.max, op1=ALU.add)

            def write_mask(t, threshold):
                return v.tensor_scalar(Mq[:, t % 2, 0:ASSOC], sw[:, :], threshold, None, ALU.is_le)

            def select(t, k):
                if k < COPIES:
                    i = COPIES * t + k
                    dve.wait_ge(s_idx_ps, i + 1)
                    if k == 0 and t:
                        dve.wait_ge(s_mq, t)
                    copy_index_scores(k, index_bank(t, k)).then_inc(s_idx, 1)
                    if k == COPIES - 1:
                        dve.wait_ge(s_idx, i + 1)
                elif k < COPIES + STRIPES // 8:
                    for i in range(8 * (k - COPIES), 8 * (k - COPIES) + 8):
                        last = v.max(cand[:, 8 * i:8 * i + 8], sw[:, i:ASSOC:STRIPES])
                    if k == COPIES + STRIPES // 8 - 1:
                        link(last)
                elif k < PIECES - 2:
                    link(v.max(top8[:, :], cand[:, :]))
                    link(v.match_replace(cand[:, :], top8[:, :], cand[:, :], TAKEN))
                elif k == PIECES - 2:
                    link(v.max(top8[:, :], cand[:, :]))
                    link(v.match_replace(sw[:, :], top8[:, :], sw[:, :], KEPT))
                else:
                    if t >= 2:
                        dve.wait_ge(s_mt[t % 2], 16 * (t // 2))
                        dve.wait_ge(s_cnt, COUNTS * (t - 1))
                    write_mask(t, top8[:, 7:8]).then_inc(s_mq, 1)

            def check_selection(g):
                dve.wait_ge(s_cnt, COUNTS * TPG * (g + 1))
                link(v.tensor_reduce(ck[:, :], masked_keys[:, g * TPG:(g + 1) * TPG, :], AX_X, ALU.add))
                link(v.tensor_scalar(ck[:, :], ck[:, :], float(ASSOC - TOPK), None, ALU.is_equal))
                v.tensor_reduce(fl[:, 2:3], ck[:, :], AX_X, ALU.min).then_inc(s_cok, 1)

            def flag_group(g):
                dve.wait_ge(s_cok_ps, g + 1)
                link(v.tensor_reduce(fl[0:1, 3:4], X[0:1, 1, 0:P], AX_X, ALU.min))
                v.tensor_tensor(fli[0:1, g:g + 1], fl[0:1, 3:4], fl[0:1, 1:2], ALU.min).then_inc(s_cflag, 1)

            def care_for(g):
                dve.wait_ge(s_cflag, g + 1)
                fine = dve.value_load(fli[0:1, g:g + 1], min_val=0, max_val=1)
                with dve.If(fine == 0):
                    careful(0, [g], care[g])

            def exact_max(a, i, t, c):
                with dve.Fori(0, H) as h:
                    v.tensor_scalar(qm, Qs[:, :, t * P:(t + 1) * P], hmask[:, bass.ds(h, 1)], None, ALU.mult
                                    ).then_inc(c.q, 1)
                    for ch in range(4):
                        dve.wait_ge(c.sc, h * 4 + (4 * i * H + ch + 1))
                        if a == 0:
                            v.scalar_tensor_tensor(out=cs, in0=Mq[:, t % 2, ch * QG:(ch + 1) * QG], scalar=-MASK,
                                                   in1=X[:, ch % 2, :], op0=ALU.mult, op1=ALU.add).then_inc(c.add, 1)
                            dve.wait_ge(c.add, h * 4 + (4 * i * H + ch + 1))
                            v.tensor_reduce(cm[:, ch:ch + 1], cs, AX_X, ALU.max).then_inc(c.red, 1)
                        else:
                            v.tensor_reduce(cm[:, ch:ch + 1], X[:, ch % 2, :], AX_X, ALU.max).then_inc(c.red, 1)
                        dve.wait_ge(c.red, h * 4 + (4 * i * H + ch + 1))
                    v.tensor_reduce(mx[:, t, bass.ds(h, 1)], cm[:, :], AX_X, ALU.max).then_inc(c.mx, 1)
                    dve.wait_ge(c.mx, h + (i * H + 1))

            def careful(a, groups, c):
                follow = chain(c.chain)
                dve.wait_ge(s_md, SHIFT_STORES * (a + 1))
                for i, g in enumerate(groups):
                    for tt in range(TPG):
                        t = g * TPG + tt
                        if a == 0:
                            for k in range(COPIES):
                                dve.wait_ge(c.idx_ps, COPIES * tt + k + 1)
                                copy_index_scores(k, X[:, k % 2, :]).then_inc(c.idx, 1)
                            dve.wait_ge(c.idx, COPIES * (tt + 1))
                            for _ in range(ROUNDS):
                                follow(v.max(top8[:, :], sw[:, :]))
                                follow(v.match_replace(sw[:, :], top8[:, :], sw[:, :], TAKEN))
                            for buf in range(2):
                                dve.wait_ge(s_mt[buf], 16 * 2 * (g + 1))
                            if tt >= 2:
                                dve.wait_ge(c.mt, 16 * (tt - 1))
                            follow(v.tensor_scalar(Mq[:, tt % 2, 0:ASSOC], sw[:, :], TAKEN, None, ALU.is_gt))
                            v.tensor_copy(top8[:, 0:1], top8[:, 0:1]).then_inc(c.mq, 1)
                            dve.wait_ge(c.mq, tt + 1)
                        exact_max(a, TPG * i + tt, t, c)
                    part = slice(g * TPG, (g + 1) * TPG)
                    v.tensor_scalar(ngm[:, part, :], mx[:, part, :], -1.0, -SHIFT[a], ALU.mult, ALU.add
                                    ).then_inc(c.ngm, 1)
                    dve.wait_ge(c.m_ps, i + 1)
                    if i:
                        dve.wait_ge(c.md, 16 * i)
                    follow(v.tensor_copy(msc[:, 0, :], X[0:H, 1, :]))
                    split(msc[:, 0, :], msc[:, 1, :], Ms[:, 0, :], Ms[:, 1, :], Ms[:, 2, :], follow
                          ).then_inc(c.ms, 1)
                if a == 0:
                    dve.wait_ge(c.mt, 16 * TPG)
                dve.wait_ge(c.md, 16 * len(groups))

            def block_masks(G, s):
                i = (GSTEPS * G + s) // PPP
                if i >= KEYS_AHEAD:
                    dve.wait_ge(s_pm, (i - KEYS_AHEAD + 1) * PPP)
                v.tensor_scalar(keep[:, i % KEYS_AHEAD, :], MT[:, G % 2, s % STEPS // PPP, :], 0.0, None, ALU.is_equal
                                ).then_inc(s_keep, 1)

            def mask_weights(G, s):
                n = GSTEPS * G + s
                kb = s % STEPS // PPP
                heads, own = (1, QG) if selects(G, s) else (2, QG - POOL_QUERIES)
                w = Pb[:, n % 4, :].rearrange("p (b n) -> p b n", b=2)[:, 0:heads, 0:own]
                dve.wait_ge(s_exp, n + 1)
                v.scalar_tensor_tensor(out=w, in0=MT[:, G % 2, kb, 0:own].unsqueeze(1).to_broadcast([P, heads, own]),
                                       scalar=0.0, in1=w, op0=ALU.is_equal, op1=ALU.mult).then_inc(s_vm, 1)

            def copy_outputs(G, hh, q):
                dve.wait_ge(s_pv, (GSTEPS * G + STEPS * (hh + 1)) // 2 - 1 + q)
                if G and hh == 0:
                    dve.wait_ge(s_ot_ps, TPG * G)
                v.tensor_copy(OT[:, hh, q, :], Po[:, q, :]).then_inc(s_po, 1)

            def tail_normalise(G, tt):
                dve.wait_ge(s_ot_ps, TPG * G + tt + 1)
                o = X[:, tt % 2, :].rearrange("p (h c) -> p h c", h=H)
                link(v.reciprocal(rec[:, tt % 2, :], o[:, :, DH]))
                v.tensor_tensor(att[:, tt, :].rearrange("p (h d) -> p h d", h=H), o[:, :, 0:DH],
                                rec[:, tt % 2, :].unsqueeze(2).to_broadcast([P, H, DH]), ALU.mult
                                ).then_inc(s_att, 1)

            def tail_copy(G):
                dve.wait_ge(s_attT_ps, G + 1)
                v.tensor_copy(attT[:, :], X[:, 0, :]).then_inc(s_attT, 1)

            def tail_residual(G):
                a, g = divmod(G, GROUPS)
                dve.wait_ge(s_wo_ps, G + 1)
                res = (x if a == 0 else y)[:, g * TPG:(g + 1) * TPG, :]
                o = X[:, 1, :].rearrange("p (t d) -> p t d", d=D)
                v.tensor_tensor(res, res, o, ALU.add).then_inc(s_res, 1)

            def attention(a):
                for G in range(GROUPS * a, GROUPS * (a + 1)):
                    g = G % GROUPS
                    for i in range(2 if a == 0 else 0):
                        dve.wait_ge(s_mt[i], 16 * 2 * (g + 1))
                    for s in range(GSTEPS):
                        if a == 0 and s % PPP == 0:
                            if s == 0:
                                block_masks(G, 0)
                            if s + PPP < GSTEPS:
                                block_masks(G, s + PPP)
                        if a == 0 and selects(g, s) and piece_at(s)[1] < COPIES:
                            select((g + 1) * TPG + piece_at(s)[0], piece_at(s)[1])
                        if a == 0 and not masked_by_tensor(g, s):
                            mask_weights(G, s)
                        if g:
                            if s - 1 in TAIL_OUTPUTS:
                                tail_normalise(G - 1, TAIL_OUTPUTS.index(s - 1))
                            if s == TAIL_TRANSPOSE + 1:
                                tail_copy(G - 1)
                            if s == TAIL_PROJECT + 1:
                                tail_residual(G - 1)
                            if 0 <= s - TAIL_PROJECT - 2 < TPG:
                                dve.wait_ge(s_res, G)
                                t = (g - 1) * TPG + s - TAIL_PROJECT - 2
                                v.bn_stats(st[:, t, :], (y if a else x)[:, t, :])
                        if a == 0 and g + 1 < GROUPS:
                            if piece_at(s) and piece_at(s)[1] >= COPIES:
                                select((g + 1) * TPG + piece_at(s)[0], piece_at(s)[1])
                            if s == CHECK_STEP:
                                check_selection(g + 1)
                            if s == CHECK_STEP + 4:
                                flag_group(g + 1)
                            if s == CAREFUL_STEP:
                                care_for(g + 1)
                        if s in (0, 2) and g:
                            copy_outputs(G - 1, 1, s // 2)
                        if s in (STEPS, STEPS + 2):
                            copy_outputs(G, 0, (s - STEPS) // 2)
                for q in range(2):
                    copy_outputs(G, 1, q)
                for tt in range(TPG):
                    tail_normalise(G, tt)
                tail_copy(G)
                tail_residual(G)

            v.memset(ones[:, :], 1.0)
            v.memset(Po[:, :, :], 0.0).then_inc(s_init, 1)
            dve.wait_ge(s_init, 1)
            statistics(x, 0)
            dve.wait_ge(s_const, 3)
            v.tensor_scalar(tie[:, :], tie[:, :].bitcast(I32), -TIE, None, ALU.mult)
            link(v.tensor_scalar(rank[:, :], rank[:, :].bitcast(I32), 1.0, None, ALU.mult))
            dve.wait_ge(s_w, 16 * WEIGHT_LOADS)
            dve.wait_ge(s_id, 3)
            prologue(0, x)
            dve.wait_ge(s_qd, 16 * SLOTS)
            dve.wait_ge(s_kd, 16 * SLOTS)
            link(v.memset(Mq[:, :, ASSOC:S], 0.0))
            for t in range(TPG):
                for k in range(PIECES):
                    select(t, k)
            check_selection(0)
            flag_group(0)
            care_for(0)
            dve.wait_ge(s_ones, 5)
            attention(0)
            dve.wait_ge(s_res, GROUPS)
            statistics(x, 1, TILES - TPG)
            for t in range(TILES):
                last = normalise(y[:, t, :], x, t)
            link(last)
            statistics(y, 2)
            prologue(1, y)
            fine = dve.value_load(fli[0:1, GROUPS:GROUPS + 1], min_val=0, max_val=1)
            with dve.If(fine == 0):
                careful(1, list(range(GROUPS)), care[GROUPS])
            attention(1)
            dve.wait_ge(s_res, 2 * GROUPS)
            statistics(y, 3, TILES - TPG)
            dve.wait_ge(s_rc, 8)
            for g in range(GROUPS):
                for t in range(g * TPG, (g + 1) * TPG):
                    last = normalise(y[:, t, :], y, t)
                last.then_inc(s_xg, 1)
            dve.wait_ge(s_rc, 7)
            v.tensor_scalar(full[:, :], full[:, :].bitcast(I32), 1.0, None, ALU.mult)
            link(v.tensor_scalar(slot[:, :], slot[:, :].bitcast(I32), 1.0, None, ALU.mult))
            dve.wait_ge(s_g_ps, 1)
            link(v.tensor_tensor(lg[:, :, :], X[:, 1, 0:TILES * E].rearrange("p (t e) -> p t e", e=E),
                                 gb[:, :].unsqueeze(1).to_broadcast([P, TILES, E]), ALU.add))
            link(v.tensor_reduce(lm[:, :], lg[:, :, :], AX_X, ALU.max))
            link(v.tensor_tensor(l1[:, :, :], lg[:, :, :], lm[:, :].unsqueeze(2).to_broadcast([P, TILES, E]),
                                 ALU.is_equal))
            link(v.tensor_tensor(l1[:, :, :], l1[:, :, :], rank[:, :].unsqueeze(1).to_broadcast([P, TILES, E]),
                                 ALU.mult))
            link(v.tensor_reduce(lm[:, :], l1[:, :, :], AX_X, ALU.max))
            v.tensor_tensor(oh[:, :, :], l1[:, :, :], lm[:, :].unsqueeze(2).to_broadcast([P, TILES, E]), ALU.is_equal)
            link(v.tensor_tensor(sums[:, 0, NONE:, :], l1[:, :, :], lm[:, :].unsqueeze(2).to_broadcast([P, TILES, E]),
                                 ALU.is_equal))
            at = 0
            for step in (1, 2, 4, 8):
                last = v.tensor_tensor(sums[:, 1 - at, NONE:, :], sums[:, at, NONE:, :],
                                       sums[:, at, NONE - step:NONE + TILES - step, :], ALU.add)
                at = 1 - at
                if step < 8:
                    link(last)
            last.then_inc(s_place, 1)
            dve.wait_ge(s_rank_ps, 1)
            dve.wait_ge(s_place, 1)
            link(v.tensor_copy(in_expert[:, :], Sp[:, 1, 0:E]))
            link(v.tensor_tensor(begun[:, :, :], in_expert[:, :].unsqueeze(2).to_broadcast([P, E, TILES]),
                                 full[:, :].unsqueeze(1).to_broadcast([P, E, TILES]), ALU.is_gt))
            link(v.tensor_reduce(tiles_of[:, :], begun[:, :, :], AX_X, ALU.add))
            link(v.tensor_tensor(products[:, :, :], earlier[:, :, :],
                                 tiles_of[:, :].unsqueeze(1).to_broadcast([P, E, E]), ALU.mult))
            link(v.tensor_reduce(first_of[:, :], products[:, :, :], AX_X, ALU.add))
            link(v.scalar_tensor_tensor(out=l1[:, :, :], in0=first_of[:, :].unsqueeze(1).to_broadcast([P, TILES, E]),
                                        scalar=float(P), in1=Sp[:, 0, 0:TILES * E].rearrange("p (t e) -> p t e", e=E),
                                        op0=ALU.mult, op1=ALU.add))
            link(v.tensor_tensor(l1[:, :, :], l1[:, :, :], oh[:, :, :], ALU.mult))
            link(v.tensor_reduce(place_f[:, :], l1[:, :, :], AX_X, ALU.add))
            v.tensor_copy(place_i[:, :], place_f[:, :]).then_inc(s_place, 1)
            link(v.tensor_tensor(end_of[:, :], first_of[:, :], tiles_of[:, :], ALU.add))
            link(v.tensor_tensor(past[:, :, :], end_of[:, :].unsqueeze(1).to_broadcast([P, SLOT_TILES, E]),
                                 slot[:, :].unsqueeze(2).to_broadcast([P, SLOT_TILES, E]), ALU.is_le))
            link(v.tensor_reduce(expert_f[:, :], past[:, :, :], AX_X, ALU.add))
            link(v.tensor_scalar(expert_i[:, :], expert_f[:, :], float(E - 1), None, ALU.min))

            def first_layer(j):
                e = dve.value_load(expert_i[0:1, j:j + 1], min_val=0, max_val=E - 1)
                if j >= 2:
                    dve.wait_ge(s_h_ps, j - 1)
                v.tensor_copy(w1s[:, j % 2, :], w1[:, bass.ds(e, 1), :].rearrange("p a h -> p (a h)")
                              ).then_inc(s_w1s, 1)
                return e

            def second_layer(j, e):
                if j >= 2:
                    dve.wait_ge(s_y_ps, j - 1)
                v.tensor_copy(w2s[:, j % 2, :], w2[:, bass.ds(e, 1), :, :].rearrange("p a c d -> p (a c d)")
                              ).then_inc(s_w2s, 1)

            dve.wait_ge(s_moe_w, 32 * E + 16)
            dve.wait_ge(s_qk, 2 * GROUPS * GSTEPS)
            for j in range(2):
                second_layer(j, first_layer(j))
            for j in range(SLOT_TILES):
                if j + 2 < SLOT_TILES:
                    e = first_layer(j + 2)
                dve.wait_ge(s_y_ps, j + 1)
                v.tensor_copy(ys[:, j, :], Po[:, j % 2, 0:D]).then_inc(s_ys, 1)
                if j + 2 < SLOT_TILES:
                    second_layer(j + 2, e)
            for g in range(GROUPS):
                dve.wait_ge(s_gat[g], 16 * TPG)
                part = x[:, g * TPG:(g + 1) * TPG, :]
                v.tensor_tensor(part, part, gathered[:, g * TPG:(g + 1) * TPG, :], ALU.add).then_inc(s_fin, 1)


WEIGHT_LOADS = 22


def kernel(**inputs):
    import numpy as np
    import concourse.bacc as bacc
    from concourse.bass_utils import run_bass_kernel_spmd

    def flat(name):
        return np.ascontiguousarray(inputs[name])

    def turned(name):
        return np.ascontiguousarray(np.asarray(inputs[name]).T)

    given = {
        "x": flat("L0_attn_x"), "wqT": turned("L0_attn_wq"), "bq": flat("L0_attn_bq"), "wkT": turned("L0_attn_wk"),
        "bk": flat("L0_attn_bk"), "wvT": turned("L0_attn_wv"), "bv": flat("L0_attn_bv"), "woT": turned("L0_attn_wo"),
        "bo": flat("L0_attn_bo"), "wqiT": turned("L0_attn_wqi"), "bqi": flat("L0_attn_bqi"),
        "wkiT": turned("L0_attn_wki"), "bki": flat("L0_attn_bki"), "ln1_w": flat("L0_ffn_ln1_w"),
        "ln1_b": flat("L0_ffn_ln1_b"), "w_qkv": flat("L0_ffn_w_qkv"), "w_proj": flat("L0_ffn_w_proj"),
        "ln2_w": flat("L0_ffn_ln2_w"), "ln2_b": flat("L0_ffn_ln2_b"), "gate_w": flat("L0_ffn_gate_w"),
        "gate_b": flat("L0_ffn_gate_b"), "w1": flat("L0_ffn_w1"), "w2": flat("L0_ffn_w2"),
    }
    nc = bacc.Bacc("TRN2", target_bir_lowering=False, num_devices=1)
    in_ = {n: nc.dram_tensor(f"in_{n}", a.shape, mybir.dt.from_np(a.dtype), kind="ExternalInput").ap()
           for n, a in given.items()}
    out = nc.dram_tensor("out", (1, S, D), F32, kind="ExternalOutput").ap()
    build(nc, in_, out)
    r = run_bass_kernel_spmd(nc, [{f"in_{n}": a for n, a in given.items()}], core_ids=[0])
    return r.results[0]["out"]
```
